# Optimizing a Trainium2 kernel written in Bass

```python
import numpy as np
import jax
import jax.numpy as jnp

def _softmax(x, axis=-1):
    return jax.nn.softmax(x, axis=axis)

def _gelu(x):
    return jax.nn.gelu(x, approximate=True)

def _silu(x):
    return jax.nn.silu(x)

def _sigmoid(x):
    return jax.nn.sigmoid(x)

def _layernorm(x, axis=-1, eps=1e-05):
    m = jnp.mean(x, axis=axis, keepdims=True)
    v = jnp.var(x, axis=axis, keepdims=True)
    return (x - m) / jnp.sqrt(v + eps)

def _scatter_add(tgt, idx, src, axis=0):
    return tgt.at[idx].add(src)

def _segment_sum(src, seg, n):
    return jax.ops.segment_sum(src, seg, n)
kernel_name = 'mk_recurrent_d1_jaxref_r8_6560c7'

def setup_inputs(seed: int=0):
    np.random.seed(seed)
    _w = jnp.asarray

    def _L0_attn_setup():
        import jax, jax.numpy as jnp
        import numpy as np
        B, S, D, H, L, F = (4, 256, 128, 16, 8, 512)
        DH = D // H

        def _ln(x, g, b):
            m = jnp.mean(x, axis=-1, keepdims=True)
            v = jnp.mean((x - m) ** 2, axis=-1, keepdims=True)
            return (x - m) * jax.lax.rsqrt(v + 1e-05) * g + b

        def _phi(t):
            return jax.nn.elu(t) + 1.0
        key = jax.random.key(seed)
        ks = jax.random.split(key, 12)
        s = 0.02
        n = jax.random.normal
        return {'x': n(ks[0], (B, S, D), jnp.float32), 'Wq': n(ks[1], (L, D, D), jnp.float32) * s, 'bq': jnp.zeros((L, D), jnp.float32), 'Wk': n(ks[2], (L, D, D), jnp.float32) * s, 'bk': jnp.zeros((L, D), jnp.float32), 'Wv': n(ks[3], (L, D, D), jnp.float32) * s, 'bv': jnp.zeros((L, D), jnp.float32), 'Wo': n(ks[4], (L, D, D), jnp.float32) * s, 'bo': jnp.zeros((L, D), jnp.float32), 'g1': jnp.ones((L, D), jnp.float32), 'be1': jnp.zeros((L, D), jnp.float32), 'g2': jnp.ones((L, D), jnp.float32), 'be2': jnp.zeros((L, D), jnp.float32), 'W1': n(ks[5], (L, D, F), jnp.float32) * s, 'c1': jnp.zeros((L, F), jnp.float32), 'W2': n(ks[6], (L, F, D), jnp.float32) * s, 'c2': jnp.zeros((L, D), jnp.float32), 'gf': jnp.ones((D,), jnp.float32), 'bef': jnp.zeros((D,), jnp.float32)}
    _L0_attn_in = _L0_attn_setup()

    def _L0_ffn_setup():
        import jax, jax.numpy as jnp
        import numpy as np
        B, S, D, H, E = (64, 128, 128, 64, 8)
        EPS = 1e-05
        key = jax.random.key(seed)
        ks = jax.random.split(key, 8)
        x = jax.random.normal(ks[0], (B, S, D), jnp.float32)
        return {'x': x, 'ln_g': jnp.ones((D,), jnp.float32), 'ln_b': jnp.zeros((D,), jnp.float32), 'bn_g': jnp.ones((D,), jnp.float32), 'bn_b': jnp.zeros((D,), jnp.float32), 'bn_mean': jax.random.normal(ks[1], (D,), jnp.float32) * 0.01, 'bn_var': jnp.ones((D,), jnp.float32), 'Wr': jax.random.normal(ks[2], (D, E), jnp.float32) * 0.02, 'br': jnp.zeros((E,), jnp.float32), 'W_down': jax.random.normal(ks[3], (E, D, H), jnp.float32) * 0.02, 'b_down': jnp.zeros((E, H), jnp.float32), 'W_up': jax.random.normal(ks[4], (E, H, D), jnp.float32) * 0.02, 'b_up': jnp.zeros((E, D), jnp.float32)}
    _L0_ffn_in = _L0_ffn_setup()
    _d = {'L0_attn_x': _L0_attn_in['x'], 'L0_attn_Wq': _L0_attn_in['Wq'], 'L0_attn_bq': _L0_attn_in['bq'], 'L0_attn_Wk': _L0_attn_in['Wk'], 'L0_attn_bk': _L0_attn_in['bk'], 'L0_attn_Wv': _L0_attn_in['Wv'], 'L0_attn_bv': _L0_attn_in['bv'], 'L0_attn_Wo': _L0_attn_in['Wo'], 'L0_attn_bo': _L0_attn_in['bo'], 'L0_attn_g1': _L0_attn_in['g1'], 'L0_attn_be1': _L0_attn_in['be1'], 'L0_attn_g2': _L0_attn_in['g2'], 'L0_attn_be2': _L0_attn_in['be2'], 'L0_attn_W1': _L0_attn_in['W1'], 'L0_attn_c1': _L0_attn_in['c1'], 'L0_attn_W2': _L0_attn_in['W2'], 'L0_attn_c2': _L0_attn_in['c2'], 'L0_attn_gf': _L0_attn_in['gf'], 'L0_attn_bef': _L0_attn_in['bef'], 'L0_ffn_ln_g': _L0_ffn_in['ln_g'], 'L0_ffn_ln_b': _L0_ffn_in['ln_b'], 'L0_ffn_bn_g': _L0_ffn_in['bn_g'], 'L0_ffn_bn_b': _L0_ffn_in['bn_b'], 'L0_ffn_bn_mean': _L0_ffn_in['bn_mean'], 'L0_ffn_bn_var': _L0_ffn_in['bn_var'], 'L0_ffn_Wr': _L0_ffn_in['Wr'], 'L0_ffn_br': _L0_ffn_in['br'], 'L0_ffn_W_down': _L0_ffn_in['W_down'], 'L0_ffn_b_down': _L0_ffn_in['b_down'], 'L0_ffn_W_up': _L0_ffn_in['W_up'], 'L0_ffn_b_up': _L0_ffn_in['b_up']}
    _x0 = _d['L0_attn_x']
    _d['L0_attn_x'] = jax.random.normal(jax.random.fold_in(jax.random.key(seed), 1), (8, 512, 128), dtype=_x0.dtype)
    del _x0
    return _d

def reference(L0_attn_x, L0_attn_Wq, L0_attn_bq, L0_attn_Wk, L0_attn_bk, L0_attn_Wv, L0_attn_bv, L0_attn_Wo, L0_attn_bo, L0_attn_g1, L0_attn_be1, L0_attn_g2, L0_attn_be2, L0_attn_W1, L0_attn_c1, L0_attn_W2, L0_attn_c2, L0_attn_gf, L0_attn_bef, L0_ffn_ln_g, L0_ffn_ln_b, L0_ffn_bn_g, L0_ffn_bn_b, L0_ffn_bn_mean, L0_ffn_bn_var, L0_ffn_Wr, L0_ffn_br, L0_ffn_W_down, L0_ffn_b_down, L0_ffn_W_up, L0_ffn_b_up):

    def _L0_attn_ref(x, Wq, bq, Wk, bk, Wv, bv, Wo, bo, g1, be1, g2, be2, W1, c1, W2, c2, gf, bef):
        import jax, jax.numpy as jnp
        import numpy as np
        B, S, D, H, L, F = (4, 256, 128, 16, 8, 512)
        DH = D // H

        def _ln(x, g, b):
            m = jnp.mean(x, axis=-1, keepdims=True)
            v = jnp.mean((x - m) ** 2, axis=-1, keepdims=True)
            return (x - m) * jax.lax.rsqrt(v + 1e-05) * g + b

        def _phi(t):
            return jax.nn.elu(t) + 1.0
        b, s, d = x.shape

        def layer(h, p):
            wq, bq_, wk, bk_, wv, bv_, wo, bo_, g1_, be1_, g2_, be2_, w1, c1_, w2, c2_ = p
            q = _phi((h @ wq + bq_).reshape(b, s, H, DH))
            k = _phi((h @ wk + bk_).reshape(b, s, H, DH))
            v = (h @ wv + bv_).reshape(b, s, H, DH)
            kv = jnp.einsum('bshd,bshm->bhdm', k, v)
            z = 1.0 / (jnp.einsum('bshd,bhd->bsh', q, k.sum(axis=1)) + 1e-06)
            att = jnp.einsum('bshd,bhdm,bsh->bshm', q, kv, z).reshape(b, s, d)
            h = h + att @ wo + bo_
            h = _ln(h, g1_, be1_)
            y = jax.nn.gelu(h @ w1 + c1_, approximate=False) @ w2 + c2_
            return (_ln(h + y, g2_, be2_), None)
        params = (Wq, bq, Wk, bk, Wv, bv, Wo, bo, g1, be1, g2, be2, W1, c1, W2, c2)
        h, _ = jax.lax.scan(layer, x, params)
        return _ln(h, gf, bef)

    def _L0_ffn_ref(x, ln_g, ln_b, bn_g, bn_b, bn_mean, bn_var, Wr, br, W_down, b_down, W_up, b_up):
        import jax, jax.numpy as jnp
        import numpy as np
        B, S, D, H, E = (64, 128, 128, 64, 8)
        EPS = 1e-05
        mu = jnp.mean(x, axis=-1, keepdims=True)
        var = jnp.var(x, axis=-1, keepdims=True)
        z = (x - mu) * jax.lax.rsqrt(var + EPS) * ln_g + ln_b
        z_sent = jnp.mean(z, axis=1)
        z_bn = (z_sent - bn_mean) * jax.lax.rsqrt(bn_var + EPS) * bn_g + bn_b
        probs = jax.nn.softmax(z_bn @ Wr + br, axis=-1)
        idx = jnp.argmax(probs, axis=-1)
        gate = jnp.take_along_axis(probs, idx[:, None], axis=1)[:, 0]
        h = jax.nn.relu(jnp.einsum('bsd,bdh->bsh', z, W_down[idx]) + b_down[idx][:, None, :])
        y = jnp.einsum('bsh,bhd->bsd', h, W_up[idx]) + b_up[idx][:, None, :]
        return y * gate[:, None, None]
    x = L0_attn_x
    xn = _layernorm(x, axis=-1)
    s = _L0_attn_ref(xn, L0_attn_Wq, L0_attn_bq, L0_attn_Wk, L0_attn_bk, L0_attn_Wv, L0_attn_bv, L0_attn_Wo, L0_attn_bo, L0_attn_g1, L0_attn_be1, L0_attn_g2, L0_attn_be2, L0_attn_W1, L0_attn_c1, L0_attn_W2, L0_attn_c2, L0_attn_gf, L0_attn_bef)
    g = _silu(_L0_ffn_ref(xn, L0_ffn_ln_g, L0_ffn_ln_b, L0_ffn_bn_g, L0_ffn_bn_b, L0_ffn_bn_mean, L0_ffn_bn_var, L0_ffn_Wr, L0_ffn_br, L0_ffn_W_down, L0_ffn_b_down, L0_ffn_W_up, L0_ffn_b_up))
    x = x + s * g
    return x

_drawn_inputs = setup_inputs


def setup_inputs(seed=0):
    import zlib

    import numpy as np

    out = dict(_drawn_inputs(seed))
    spreads = {'L0_attn_bq': (0.0, 2.0),
     'L0_attn_bk': (0.0, 2.0),
     'L0_attn_bv': (0.0, 0.8),
     'L0_attn_bo': (0.0, 0.8),
     'L0_attn_g1': (1.0, 0.6),
     'L0_attn_be1': (0.0, 0.8),
     'L0_attn_g2': (1.0, 0.6),
     'L0_attn_be2': (0.0, 0.8),
     'L0_attn_c1': (0.0, 0.8),
     'L0_attn_c2': (0.0, 0.8),
     'L0_attn_gf': (1.0, 0.6),
     'L0_attn_bef': (0.0, 0.8),
     'L0_ffn_ln_g': (1.0, 0.6),
     'L0_ffn_ln_b': (0.0, 0.8),
     'L0_ffn_bn_g': (1.0, 0.6),
     'L0_ffn_bn_b': (0.0, 0.649),
     'L0_ffn_bn_var': (1.0, 0.6),
     'L0_ffn_br': (0.0, 0.8),
     'L0_ffn_b_down': (0.0, 0.8),
     'L0_ffn_b_up': (0.0, 0.8)}
    factors = {'L0_attn_Wq': 200.0,
     'L0_attn_Wk': 200.0,
     'L0_attn_Wv': 8.0,
     'L0_attn_Wo': 8.0,
     'L0_attn_W1': 8.0,
     'L0_attn_W2': 8.0,
     'L0_ffn_bn_mean': 8.0,
     'L0_ffn_Wr': 5.837,
     'L0_ffn_W_down': 8.0,
     'L0_ffn_W_up': 8.0}
    for name, (base, spread) in spreads.items():
        noise = np.random.default_rng([zlib.crc32(name.encode()), seed]).standard_normal(out[name].shape)
        drawn = base * np.exp(spread * noise) if base else spread * noise
        out[name] = jnp.asarray(drawn.astype(out[name].dtype))
    for name, factor in factors.items():
        out[name] = (out[name] * factor).astype(out[name].dtype)
    return out
```

```python
import concourse.bass as bass
from concourse import mybir
from contextlib import ExitStack

P = 128
EPS = 1e-5
DEN_EPS = 1e-6


def build(nc, x, Wq, bq, Wk, bk, Wv, bv, Wo, bo, g1, be1, g2, be2, W1, c1, W2, c2, gf, bef,
          ln_g, ln_b, bn_g, bn_b, bn_mean, bn_var, Wr, br, W_down, b_down, W_up, b_up, out):
    F32 = mybir.dt.float32
    F32R = mybir.dt.float32r
    I32 = mybir.dt.int32
    ALU = mybir.AluOpType
    ACT = mybir.ActivationFunctionType
    AX = mybir.AxisListType

    SEQS, S, D = x.shape
    L = Wq.shape[0]
    F = W1.shape[2]
    FC = F // P
    DH = D // 16
    UNITS = L * SEQS
    TT = S // P
    E, _, HID = W_down.shape
    assert D == P and S == 512 and E == SEQS

    x_dram = x.rearrange("b (p s) d -> p b s d", s=TT)
    out_dram = out.rearrange("b (p s) d -> p b s d", s=TT)

    with ExitStack() as ctx:
        def sb(name, shape, dt=F32):
            return ctx.enter_context(nc.sbuf_tensor(name, shape, dt))

        def ps(name, shape):
            return ctx.enter_context(nc.psum_tensor(name, shape, F32))

        def sem(name):
            return ctx.enter_context(nc.semaphore(name))

        ident = sb("ident", [P, P])
        centre = sb("centre", [P, P])
        head_mask = sb("head_mask", [P, P])
        mean_mat = sb("mean_mat", [P, P])
        ones = sb("ones", [P, P])
        eps_col = sb("eps_col", [P, 1])
        den_eps_col = sb("den_eps_col", [P, 1])
        neg1_col = sb("neg1_col", [P, 1])
        expert_m8 = sb("expert_m8", [SEQS, E])

        x_tm = sb("x_tm", [P, SEQS, TT, D])
        gate_tm = sb("gate_tm", [P, SEQS, TT, D])
        vec_rows = sb("vec_rows", [P, D])
        NVEC = 7 * L + FC * L + 6
        R_C1 = 7 * L
        R_FFN = R_C1 + FC * L
        cols = sb("cols", [P, NVEC])
        NLV = 7 + FC
        layer_vecs = sb("layer_vecs", [P, L + 1, NLV])
        V_BQ, V_BO, V_G1, V_BE1, V_G2P, V_BE2P, V_C2, V_C1 = range(8)
        gf_bc = sb("gf_bc", [P, D])
        bef_bc = sb("bef_bc", [P, D])
        z_hi = sb("z_hi", [P, SEQS, S], F32R)
        z_lo = sb("z_lo", [P, SEQS, S], F32R)

        raw_att = sb("raw_att", [P, 4, D])
        raw_w1 = sb("raw_w1", [P, F])
        raw_w2 = sb("raw_w2", [P, FC, D])
        raw_bkv = sb("raw_bkv", [1, 2 * D])
        lv_a = sb("lv_a", [P, NLV])
        lv_f = sb("lv_f", [P, NLV])
        fold_att = sb("fold_att", [P, 3 * D])
        fold_cg2 = sb("fold_cg2", [P, D])
        fold_w1 = sb("fold_w1", [P, F])
        fold_cg1 = sb("fold_cg1", [P, D])
        wqkv_hi = sb("wqkv_hi", [P, 3 * D], F32R)
        wqkv_lo = sb("wqkv_lo", [P, 3 * D], F32R)
        cg2_hi = sb("cg2_hi", [P, D], F32R)
        cg2_lo = sb("cg2_lo", [P, D], F32R)
        wo_sum = sb("wo_sum", [P, 1])
        wo_c = sb("wo_c", [P, D])
        w1_hi = sb("w1_hi", [P, F], F32R)
        w1_lo = sb("w1_lo", [P, F], F32R)
        cg1_hi = sb("cg1_hi", [P, D], F32R)
        cg1_lo = sb("cg1_lo", [P, D], F32R)
        w2_sum = sb("w2_sum", [P, FC])
        w2_c = sb("w2_c", [P, FC, D])
        be2_bc = sb("be2_bc", [P, P])
        bkv1_bc = sb("bkv1_bc", [P, 2 * D])
        bo_be2 = sb("bo_be2", [P, 1])
        c2_be1 = sb("c2_be1", [P, 1])
        bq_f = sb("bq_f", [P, 2])
        cb1 = sb("cb1", [P, 1])
        c1_f = sb("c1_f", [P, FC])
        colb = sb("colb", [P, FC + 2])
        cb2 = sb("cb2", [P, 1])

        kv1 = sb("kv1", [P, TT, 2 * D])
        k_min = sb("k_min", [P, TT, D])
        k_exp = sb("k_exp", [P, TT, D])
        k_phi = sb("k_phi", [P, TT, D])
        q_exp = sb("q_exp", [P, S])
        q_min = sb("q_min", [P, S])
        q_phi = sb("q_phi", [P, S])
        ksum_blk = sb("ksum_blk", [P, P])
        kvT_blk = sb("kvT_blk", [P, P])
        kvo = sb("kvo", [P, P])
        den = sb("den", [P, S])
        rden = sb("rden", [P, S])
        q_n = sb("q_n", [P, S])
        sq1 = sb("sq1", [P, S])
        sq2 = sb("sq2", [P, S])
        lnv1 = sb("lnv1", [P, S])
        lnv2 = sb("lnv2", [P, S])
        rstd1 = sb("rstd1", [P, S])
        rstd2 = sb("rstd2", [P, S])
        z1 = sb("z1", [P, S])
        z1_hi = sb("z1_hi", [P, 2, S], F32R)
        z1_lo = sb("z1_lo", [P, 2, S], F32R)
        z2 = sb("z2", [P, S])
        hid = sb("hid", [P, FC, S])

        kv_ps = [ps(f"kv_ps{i}", [P, TT // 2, 2 * D]) for i in range(2)]
        q_ps = ps("q_ps", [P, S])
        small_ps = ps("small_ps", [P, 512])
        KVT, KVO, BIAS = small_ps[:, 0:P], small_ps[:, P:2 * P], small_ps[:, 0:2 * P]
        KSUM, COLB = small_ps[:, 2 * P:2 * P + 1], small_ps[:, 2 * P + 8:2 * P + 16]
        att_ps = ps("att_ps", [P, S])
        up_ps = [ps(f"up_ps{i}", [P, S]) for i in range(2)]
        down_ps = ps("down_ps", [P, S])

        names = """pool_waited sp_waited x_in vec_in row_in fold_in const_ready
            stats rstd_x xn tr_ps cols_ready lv_ready zsum zin_ps zin_hi
            zff_ps zff bn_chain logit_ps logit pmax_r softmax_e routed expert_in gate_ps gate_bc_r
            eh_ps eh ey_ps ey gated
            raw_loaded raw_att_free raw_ffn_free lva lvf fold_att_s fold_att_v fold_ffn_s fold_ffn_v
            attw_ready ffnw_ready bias_in attb_ps ffnb_ps attb_ready cb1_ready c1_ready cb2_ready
            kvproj qproj kv_biased kmin kexp kexpm1 qexpm1 kphi qexp qmin qphi kvt_ps ksumblk kvtblk kvo_ps kvo_sb
            den_ps den_sb rden_s qn att_done sq1_s var1 lnv1_s rstd1_s z1_s z1hi_s z1lo_s
            up gelu down sq2_s var2 lnv2_s rstd2_s z2_s z2hi_s state
            htm_ps htm fstat fstd frstd fin out_sent""".split()
        s = {n: sem(n) for n in names}
        x_in = [sem(f"x_in{i}") for i in range(4)]

        def load_layer(sp, l):
            sp.dma_start(raw_att[:, 0, :], Wq[l]).then_inc(s["raw_loaded"], 16)
            sp.dma_start(raw_att[:, 1, :], Wk[l]).then_inc(s["raw_loaded"], 16)
            sp.dma_start(raw_att[:, 2, :], Wv[l]).then_inc(s["raw_loaded"], 16)
            sp.dma_start(raw_att[:, 3, :], Wo[l]).then_inc(s["raw_loaded"], 16)
            sp.dma_start(raw_bkv[0:1, 0:D], bk[l:l + 1, :] if isinstance(l, int) else bk[bass.ds(l, 1), :]).then_inc(s["raw_loaded"], 16)
            sp.dma_start(raw_bkv[0:1, D:2 * D], bv[l:l + 1, :] if isinstance(l, int) else bv[bass.ds(l, 1), :]).then_inc(s["raw_loaded"], 16)
            sp.dma_start(raw_w1[:, :], W1[l]).then_inc(s["raw_loaded"], 16)
            sp.dma_start(raw_w2[:, :, :], W2[l].rearrange("(j p) n -> p j n", p=P)).then_inc(s["raw_loaded"], 16)
        LOADS = 8 * 16

        def pool_fold_att(pool, l, wait_free):
            pool.wait_ge(s["raw_loaded"], l * LOADS + LOADS)
            pool.wait_ge(s["lva"], l * 2 + 1)
            pool.sem_inc(s["pool_waited"], 1)
            nc.gpsimd.tensor_scalar(fold_att[:, :], raw_att[:, 0:3, :], lv_a[:, V_G2P:V_G2P + 1], None,
                                    ALU.mult).then_inc(s["fold_att_s"], 1)
            nc.gpsimd.tensor_scalar(fold_cg2[:, :], centre[:, :], lv_a[:, V_G2P:V_G2P + 1], None,
                                    ALU.mult).then_inc(s["fold_att_s"], 1)
            nc.gpsimd.tensor_scalar(be2_bc[:, :], ones[:, :], lv_a[:, V_BE2P:V_BE2P + 1], None,
                                    ALU.mult).then_inc(s["fold_att_s"], 1)
            pool.wait_ge(s["fold_att_s"], l * 5 + 2)
            if wait_free:
                pool.wait_ge(s["qproj"], l * SEQS)
            pool.sem_inc(s["pool_waited"], 1)
            nc.gpsimd.tensor_copy(wqkv_hi[:, :], fold_att[:, :]).then_inc(s["fold_att_s"], 1)
            pool.wait_ge(s["fold_att_s"], l * 5 + 4)
            nc.gpsimd.tensor_tensor(wqkv_lo[:, :], fold_att[:, :], wqkv_hi[:, :].bitcast(F32),
                                    ALU.subtract).then_inc(s["attw_ready"], 1)
            if wait_free:
                pool.wait_ge(s["att_done"], l * SEQS)
            pool.sem_inc(s["pool_waited"], 1)
            nc.gpsimd.tensor_copy(cg2_hi[:, :], fold_cg2[:, :]).then_inc(s["fold_att_s"], 1)
            pool.wait_ge(s["fold_att_s"], l * 5 + 5)
            nc.gpsimd.tensor_tensor(cg2_lo[:, :], fold_cg2[:, :], cg2_hi[:, :].bitcast(F32),
                                    ALU.subtract).then_inc(s["attw_ready"], 1)

        def pool_fold_ffn(pool, l, wait_free):
            pool.wait_ge(s["lvf"], l * 2 + 1)
            pool.sem_inc(s["pool_waited"], 1)
            nc.gpsimd.tensor_scalar(fold_w1[:, :], raw_w1[:, :], lv_f[:, V_G1:V_G1 + 1], None,
                                    ALU.mult).then_inc(s["fold_ffn_s"], 1)
            nc.gpsimd.tensor_scalar(fold_cg1[:, :], centre[:, :], lv_f[:, V_G1:V_G1 + 1], None,
                                    ALU.mult).then_inc(s["fold_ffn_s"], 1)
            pool.wait_ge(s["fold_ffn_s"], l * 4 + 2)
            if wait_free:
                pool.wait_ge(s["up"], l * SEQS * FC)
            pool.sem_inc(s["pool_waited"], 1)
            nc.gpsimd.tensor_copy(w1_hi[:, :], fold_w1[:, :]).then_inc(s["fold_ffn_s"], 1)
            pool.wait_ge(s["fold_ffn_s"], l * 4 + 3)
            nc.gpsimd.tensor_tensor(w1_lo[:, :], fold_w1[:, :], w1_hi[:, :].bitcast(F32),
                                    ALU.subtract).then_inc(s["ffnw_ready"], 1)
            if wait_free:
                pool.wait_ge(s["down"], l * SEQS)
            pool.sem_inc(s["pool_waited"], 1)
            nc.gpsimd.tensor_copy(cg1_hi[:, :], fold_cg1[:, :]).then_inc(s["fold_ffn_s"], 1)
            pool.wait_ge(s["fold_ffn_s"], l * 4 + 4)
            nc.gpsimd.tensor_tensor(cg1_lo[:, :], fold_cg1[:, :], cg1_hi[:, :].bitcast(F32),
                                    ALU.subtract).then_inc(s["ffnw_ready"], 1)

        def dve_fold_att_first(dve, l, wait_free):
            dve.wait_ge(s["raw_loaded"], l * LOADS + LOADS)
            if wait_free:
                dve.wait_ge(s["attb_ps"], l * 3)
                dve.wait_ge(s["attw_ready"], l * 2)
                dve.wait_ge(s["attb_ready"], l * 5)
            nc.vector.tensor_scalar(lv_a[:, :], layer_vecs[:, l, :], 1.0, None, ALU.mult).then_inc(s["lva"], 1)
            nc.vector.reduce_sum(wo_sum[:, :], raw_att[:, 3, :], AX.X).then_inc(s["fold_att_v"], 1)
            dve.wait_ge(s["lva"], l * 2 + 1)
            nc.vector.tensor_tensor(bo_be2[:, :], lv_a[:, V_BO:V_BO + 1], lv_a[:, V_BE2P:V_BE2P + 1],
                                    ALU.add).then_inc(s["lva"], 1)
            dve.wait_ge(s["fold_att_v"], l * 3 + 1)
            nc.vector.tensor_scalar(wo_sum[:, :], wo_sum[:, :], 1.0 / D, None,
                                    ALU.mult).then_inc(s["fold_att_v"], 1)

        def dve_fold_wo(dve, l, wait_free):
            dve.wait_ge(s["fold_att_v"], l * 3 + 2)
            if wait_free:
                dve.wait_ge(s["kvo_ps"], l * SEQS)
            nc.vector.tensor_scalar(wo_c[:, :], raw_att[:, 3, :], wo_sum[:, :], None,
                                    ALU.subtract).then_inc(s["fold_att_v"], 1)

        def dve_fold_att_biases(dve, l, wait_free):
            dve.wait_ge(s["attb_ps"], l * 3 + 3)
            dve.wait_ge(s["ffnb_ps"], l + 1)
            if wait_free:
                dve.wait_ge(s["cb1_ready"], l)
                dve.wait_ge(s["cb2_ready"], l)
                dve.wait_ge(s["c1_ready"], l)
                dve.wait_ge(s["qphi"], l * SEQS)
            nc.vector.tensor_scalar(bkv1_bc[:, 0:D], BIAS[:, 0:D], 1.0, None, ALU.add).then_inc(s["attb_ready"], 1)
            nc.vector.tensor_copy(bkv1_bc[:, D:2 * D], BIAS[:, D:2 * D]).then_inc(s["attb_ready"], 1)
            nc.vector.tensor_copy(colb[:, :], COLB[:, 1:3 + FC]).then_inc(s["attb_ready"], 1)
            nc.vector.tensor_scalar(bq_f[:, 0:1], COLB[:, 0:1], lv_a[:, V_BQ:V_BQ + 1], None,
                                    ALU.add).then_inc(s["attb_ready"], 1)
            nc.vector.tensor_scalar(bq_f[:, 1:2], COLB[:, 0:1], lv_a[:, V_BQ:V_BQ + 1], 1.0,
                                    ALU.add, ALU.add).then_inc(s["attb_ready"], 1)

        def dve_fold_ffn_first(dve, l, wait_free):
            if wait_free:
                dve.wait_ge(s["ffnb_ps"], l)
                dve.wait_ge(s["ffnw_ready"], l * 2)
                dve.wait_ge(s["c1_ready"], l)
            nc.vector.tensor_scalar(lv_f[:, :], layer_vecs[:, l, :], 1.0, None, ALU.mult).then_inc(s["lvf"], 1)
            nc.vector.reduce_sum(w2_sum[:, :], raw_w2[:, :, :], AX.X).then_inc(s["fold_ffn_v"], 1)
            dve.wait_ge(s["lvf"], l * 2 + 1)
            nc.vector.tensor_tensor(c2_be1[:, :], lv_f[:, V_C2:V_C2 + 1], lv_f[:, V_BE1:V_BE1 + 1],
                                    ALU.add).then_inc(s["lvf"], 1)
            dve.wait_ge(s["fold_ffn_v"], l * 3 + 1)
            nc.vector.tensor_scalar(w2_sum[:, :], w2_sum[:, :], 1.0 / D, None,
                                    ALU.mult).then_inc(s["fold_ffn_v"], 1)

        def dve_fold_w2(dve, l, wait_free):
            dve.wait_ge(s["fold_ffn_v"], l * 3 + 2)
            if wait_free:
                dve.wait_ge(s["down"], l * SEQS)
            nc.vector.tensor_tensor(w2_c[:, :, :], raw_w2[:, :, :],
                                    w2_sum[:, :].unsqueeze(2).to_broadcast([P, FC, D]),
                                    ALU.subtract).then_inc(s["fold_ffn_v"], 1)

        def dve_fold_c1(dve, l, wait_free):
            dve.wait_ge(s["attb_ready"], l * 5 + 5)
            if wait_free:
                dve.wait_ge(s["gelu"], l * SEQS * FC)
            nc.vector.tensor_tensor(c1_f[:, :], colb[:, 1:1 + FC], lv_f[:, V_C1:V_C1 + FC],
                                    ALU.add).then_inc(s["c1_ready"], 1)

        def dve_fold_cb2(dve, l, wait_free):
            if wait_free:
                dve.wait_ge(s["sq2_s"], l * SEQS)
                dve.wait_ge(s["z2_s"], l * SEQS)
            nc.vector.tensor_copy(cb2[:, :], colb[:, 1 + FC:2 + FC]).then_inc(s["cb2_ready"], 1)

        def pe_fold_att(pe, l, wait_free):
            pe.wait_ge(s["raw_loaded"], l * LOADS + LOADS)
            pe.wait_ge(s["lva"], l * 2 + 2)
            pe.wait_ge(s["fold_att_s"], l * 5 + 3)
            if wait_free:
                pe.wait_ge(s["kvo_sb"], l * SEQS)
            nc.tensor.matmul(COLB[:, 0:1], raw_att[:, 0, :], lv_a[:, V_BE2P:V_BE2P + 1],
                             start=True, stop=True).then_inc(s["attb_ps"], 1)
            nc.tensor.matmul(COLB[:, 1:2], centre[:, :], bo_be2[:, :],
                             start=True, stop=True).then_inc(s["attb_ps"], 1)
            nc.tensor.matmul(BIAS, be2_bc[:, :], raw_att[:, 1:3, :], start=True, stop=False)
            nc.tensor.matmul(BIAS, ones[0:1, :], raw_bkv[0:1, :], start=False, stop=True).then_inc(s["attb_ps"], 1)

        def pe_fold_ffn(pe, l, wait_free):
            pe.wait_ge(s["raw_loaded"], l * LOADS + LOADS)
            pe.wait_ge(s["lvf"], l * 2 + 2)
            if wait_free:
                pe.wait_ge(s["attb_ready"], l * 5)
            for j in range(FC):
                nc.tensor.matmul(COLB[:, 2 + j:3 + j], raw_w1[:, j * P:(j + 1) * P], lv_f[:, V_BE1:V_BE1 + 1],
                                 start=True, stop=True)
            nc.tensor.matmul(COLB[:, 2 + FC:3 + FC], centre[:, :], c2_be1[:, :],
                             start=True, stop=True).then_inc(s["ffnb_ps"], 1)

        e_in = [sem(f"e_in{i}") for i in range(2)]
        wr_sb = sb("wr_sb", [P, E])
        br_bc = sb("br_bc", [SEQS, E])
        expert_i = sb("expert_i", [SEQS, 1], I32)
        ew_down = sb("ew_down", [P, 2, HID])
        eb_down = sb("eb_down", [HID, 2])
        ew_up = sb("ew_up", [HID, 2, D])
        eb_up = sb("eb_up", [P, 2, D])
        st = sb("st", [P, SEQS * TT, 6])
        mv = sb("mv", [P, SEQS * TT, 2])
        std_x = sb("std_x", [P, SEQS * TT])
        r_x = sb("r_x", [P, SEQS * TT])
        r_f = sb("r_f", [P, SEQS * TT])
        t_x = sb("t_x", [P, SEQS * TT])
        xn_tm = kv1[:, 0:4, :].rearrange("p (b s) d -> p b (s d)", b=2)
        zf_tm = hid[:, 0:2, :]
        zf_fm = gate_tm[:, :, :, :].rearrange("p b s d -> p b (s d)")
        zf_sum = sb("zf_sum", [P, SEQS])
        bn_v = sb("bn_v", [P, 2])
        z_bn = sb("z_bn", [P, SEQS])
        lg = sb("lg", [SEQS, E])
        lg_e = sb("lg_e", [SEQS, E])
        r_cols = sb("r_cols", [SEQS, 6])
        gate_d = sb("gate_d", [SEQS, SEQS])
        gate_bc = sb("gate_bc", [P, SEQS])
        e_hid = sb("e_hid", [HID, 2, S])
        e_y = sb("e_y", [P, 2, S])

        with nc.Block() as block:
            @block.sync
            def _(sp):
                for i in range(4):
                    sp.dma_start(x_tm[:, 2 * i:2 * i + 2, :, :], x_dram[:, 2 * i:2 * i + 2]).then_inc(x_in[i], 16)
                for i, v in enumerate((bq, bo, g1, be1, g2, be2, c2)):
                    sp.dma_start(vec_rows[i * L:(i + 1) * L, :], v).then_inc(s["vec_in"], 16)
                sp.dma_start(vec_rows[R_C1:R_C1 + FC * L, :],
                             c1.rearrange("l (j p) -> (l j) p", p=P)).then_inc(s["vec_in"], 16)
                for i, v in enumerate((ln_g, ln_b, bn_g, bn_b, bn_mean, bn_var)):
                    sp.dma_start(vec_rows[R_FFN + i:R_FFN + i + 1, :],
                                 v.rearrange("(a n) -> a n", a=1)).then_inc(s["vec_in"], 16)
                sp.dma_start(wr_sb[:, :], Wr).then_inc(s["row_in"], 16)
                sp.dma_start(br_bc[:, :], br.rearrange("(a n) -> a n", a=1).to_broadcast([SEQS, E])).then_inc(s["row_in"], 16)
                sp.dma_start(gf_bc[:, :], gf.rearrange("(a n) -> a n", a=1).to_broadcast([P, D])).then_inc(s["row_in"], 16)
                sp.dma_start(bef_bc[:, :], bef.rearrange("(a n) -> a n", a=1).to_broadcast([P, D])).then_inc(s["row_in"], 16)
                load_layer(sp, 0)
                sp.wait_ge(s["routed"], 1)
                for b in range(SEQS):
                    e = sp.value_load(expert_i[b:b + 1, 0:1], min_val=0, max_val=E - 1)
                    if b >= 2:
                        sp.wait_ge(s["ey"], b - 1)
                    sp.dma_start(ew_down[:, b % 2, :], W_down[bass.ds(e, 1)].rearrange("a d h -> d (a h)")).then_inc(e_in[b % 2], 16)
                    sp.dma_start(eb_down[:, b % 2:b % 2 + 1], b_down[bass.ds(e, 1)].rearrange("a h -> h a")).then_inc(e_in[b % 2], 16)
                    sp.dma_start(ew_up[:, b % 2, :], W_up[bass.ds(e, 1)].rearrange("a h d -> h (a d)")).then_inc(e_in[b % 2], 16)
                    sp.dma_start(eb_up[:, b % 2, :], b_up[bass.ds(e, 1)].to_broadcast([P, D])).then_inc(e_in[b % 2], 16)

            @block.gpsimd
            def _(pool):
                c = s["const_ready"]
                nc.gpsimd.memset(ident[:, :], 0.0).then_inc(c, 1)
                nc.gpsimd.memset(ones[:, :], 1.0).then_inc(c, 1)
                nc.gpsimd.memset(mean_mat[:, :], 1.0 / D).then_inc(c, 1)
                nc.gpsimd.memset(eps_col[:, :], EPS).then_inc(c, 1)
                nc.gpsimd.memset(neg1_col[:, :], -1.0).then_inc(c, 1)
                nc.gpsimd.memset(den_eps_col[:, :], DEN_EPS).then_inc(c, 1)
                nc.gpsimd.iota(expert_m8[:, :], pattern=[[1, E]], base=-E, channel_multiplier=0,
                               allow_small_or_imprecise_dtypes=True).then_inc(c, 1)
                pool.wait_ge(c, 7)
                nc.gpsimd.affine_select(out=ident[:, :], in_=ident[:, :], pattern=[[-1, P]], compare_op=ALU.not_equal,
                                        fill=1.0, base=0, channel_multiplier=1).then_inc(c, 1)
                nc.gpsimd.affine_select(out=head_mask[:, :], in_=ones[:, :], pattern=[[-DH, D // DH], [0, DH]],
                                        compare_op=ALU.is_ge, fill=0.0, base=0, channel_multiplier=1).then_inc(c, 1)
                pool.wait_ge(c, 9)
                nc.gpsimd.affine_select(out=head_mask[:, :], in_=head_mask[:, :], pattern=[[DH, D // DH], [0, DH]],
                                        compare_op=ALU.is_ge, fill=0.0, base=DH - 1, channel_multiplier=-1).then_inc(c, 1)
                nc.gpsimd.tensor_tensor(centre[:, :], ident[:, :], mean_mat[:, :], ALU.subtract).then_inc(c, 1)
                pool.wait_ge(c, 11)
                pool_fold_att(pool, 0, False)
                pool_fold_ffn(pool, 0, False)

            @block.scalar
            def _(act):
                act.wait_ge(s["const_ready"], 11)
                act.wait_ge(s["stats"], SEQS * TT)
                nc.scalar.activation(std_x[:, :], mv[:, :, 1], ACT.Sqrt, bias=eps_col[:, :]).then_inc(s["rstd_x"], 1)
                act.wait_ge(s["stats"], SEQS * TT + 2)
                nc.scalar.activation(t_x[:, :], t_x[:, :], ACT.Sqrt, bias=eps_col[:, :]).then_inc(s["rstd_x"], 1)
                act.wait_ge(s["cols_ready"], 1)
                nc.scalar.activation(bn_v[:, 0:1], cols[:, R_FFN + 5:R_FFN + 6], ACT.Sqrt, bias=eps_col[:, :]).then_inc(s["rstd_x"], 1)
                for b in range(SEQS):
                    act.wait_ge(s["zin_ps"], b + 1)
                    nc.scalar.activation(z_hi[:, b, :], kv_ps[b % 2][:, :, :], ACT.Identity).then_inc(s["zin_hi"], 1)
                    act.wait_ge(s["zff_ps"], b + 1)
                    nc.scalar.activation(zf_fm[:, b, :], up_ps[b % 2][:, :], ACT.Identity,
                                         scale=cols[:, R_FFN:R_FFN + 1], bias=cols[:, R_FFN + 1:R_FFN + 2],
                                         accum_out=zf_sum[:, b:b + 1]).then_inc(s["zff"], 1)
                act.wait_ge(s["logit"], 3)
                nc.scalar.activation(lg_e[:, :], lg[:, :], ACT.Exp, bias=r_cols[:, 0:1],
                                     accum_out=r_cols[:, 1:2]).then_inc(s["softmax_e"], 1)
                act.wait_ge(s["gate_bc_r"], 1)
                for b in range(SEQS):
                    act.wait_ge(s["eh_ps"], b + 1)
                    act.wait_ge(e_in[b % 2], 64 * (b // 2 + 1))
                    nc.scalar.activation(e_hid[:, b % 2, :], q_ps[0:HID, :] if b % 2 else att_ps[0:HID, :], ACT.Relu,
                                         bias=eb_down[:, b % 2:b % 2 + 1]).then_inc(s["eh"], 1)
                    act.wait_ge(s["ey"], b + 1)
                    nc.scalar.activation(gate_tm[:, b, :, :], e_y[:, b % 2, :], ACT.Silu,
                                         scale=gate_bc[:, b:b + 1]).then_inc(s["gated"], 1)

            @block.tensor
            def _(pe):
                pe.wait_ge(s["const_ready"], 11)
                pe.wait_ge(s["vec_in"], 14 * 16)
                nc.tensor.transpose(small_ps[:, 0:NVEC], vec_rows[0:NVEC, :], ident[0:NVEC, 0:NVEC]).then_inc(s["tr_ps"], 1)
                for b in range(SEQS):
                    pe.wait_ge(s["xn"], 8 * b + 8)
                    if b >= 2:
                        pe.wait_ge(s["state"], b - 1)
                    for t in range(TT):
                        last = nc.tensor.transpose(kv_ps[b % 2][:, t // 2, (t % 2) * P:(t % 2 + 1) * P],
                                                   xn_tm[:, b % 2, t * D:(t + 1) * D], ident[:, :])
                    last.then_inc(s["zin_ps"], 1)
                    if b >= 2:
                        pe.wait_ge(s["zff"], b - 1)
                    for t in range(TT):
                        last = nc.tensor.transpose(up_ps[b % 2][:, t * P:(t + 1) * P],
                                                   zf_tm[:, b % 2, t * D:(t + 1) * D], ident[:, :])
                    last.then_inc(s["zff_ps"], 1)
                pe.wait_ge(s["bn_chain"], 4)
                pe.wait_ge(s["row_in"], 64)
                nc.tensor.matmul(down_ps[0:SEQS, 0:E], z_bn[:, :], wr_sb[:, :], start=True, stop=True).then_inc(s["logit_ps"], 1)
                pe.wait_ge(s["cols_ready"], 1)
                pe_fold_att(pe, 0, False)
                pe_fold_ffn(pe, 0, False)
                pe.wait_ge(s["pmax_r"], 3)
                nc.tensor.matmul(down_ps[:, 0:SEQS], ones[0:SEQS, :], gate_d[:, :], start=True, stop=True).then_inc(s["gate_ps"], 1)
                pe.wait_ge(s["gate_bc_r"], 1)
                for b in range(SEQS):
                    hp = q_ps if b % 2 else att_ps
                    pe.wait_ge(e_in[b % 2], 64 * (b // 2 + 1))
                    nc.tensor.matmul(hp[0:HID, :], ew_down[:, b % 2, :], zf_fm[:, b, :], start=True, stop=True).then_inc(s["eh_ps"], 1)
                    pe.wait_ge(s["eh"], b + 1)
                    if b >= 2:
                        pe.wait_ge(s["ey"], b - 1)
                    for t in range(TT):
                        last = nc.tensor.matmul(up_ps[b % 2][:, t * P:(t + 1) * P], e_hid[:, b % 2, t * P:(t + 1) * P],
                                                ew_up[:, b % 2, :], start=True, stop=True)
                    last.then_inc(s["ey_ps"], 1)

            @block.vector
            def _(dve):
                for b in range(SEQS):
                    if b % 2 == 0:
                        dve.wait_ge(x_in[b // 2], 16)
                    for t in range(TT):
                        nc.vector.bn_stats(st[:, b * TT + t, :], x_tm[:, b, t, :]).then_inc(s["fstat"], 1)
                for i in range(SEQS * TT):
                    dve.wait_ge(s["fstat"], i + 1)
                    nc.vector.bn_aggr(mv[:, i, :], st[:, i, :]).then_inc(s["stats"], 1)
                dve.wait_ge(s["rstd_x"], 1)
                nc.vector.reciprocal(r_x[:, :], std_x[:, :]).then_inc(s["stats"], 1)
                dve.wait_ge(s["stats"], SEQS * TT + 1)
                nc.vector.tensor_tensor(t_x[:, :], r_x[:, :], r_x[:, :], ALU.mult).then_inc(s["fstd"], 1)
                dve.wait_ge(s["fstd"], 1)
                nc.vector.tensor_tensor(t_x[:, :], t_x[:, :], mv[:, :, 1], ALU.mult).then_inc(s["stats"], 1)
                dve.wait_ge(s["rstd_x"], 2)
                nc.vector.reciprocal(t_x[:, :], t_x[:, :]).then_inc(s["fstd"], 1)
                dve.wait_ge(s["fstd"], 2)
                nc.vector.tensor_tensor(r_f[:, :], t_x[:, :], r_x[:, :], ALU.mult).then_inc(s["fstd"], 1)
                dve.wait_ge(s["fstd"], 3)
                dve.wait_ge(s["tr_ps"], 1)
                nc.vector.tensor_copy(cols[:, :], small_ps[:, 0:NVEC]).then_inc(s["cols_ready"], 1)
                dve.wait_ge(s["cols_ready"], 1)
                nc.vector.tensor_copy(layer_vecs[:, 0:L, V_BQ:V_BE1 + 1],
                                      cols[:, 0:4 * L].rearrange("p (v l) -> p l v", l=L)).then_inc(s["lv_ready"], 1)
                nc.vector.tensor_copy(layer_vecs[:, 1:L + 1, V_G2P:V_BE2P + 1],
                                      cols[:, 4 * L:6 * L].rearrange("p (v l) -> p l v", l=L)).then_inc(s["lv_ready"], 1)
                nc.vector.tensor_copy(layer_vecs[:, 0:L, V_C2:V_C2 + 1],
                                      cols[:, 6 * L:7 * L].rearrange("p (v l) -> p l v", l=L)).then_inc(s["lv_ready"], 1)
                nc.vector.tensor_copy(layer_vecs[:, 0:L, V_C1:V_C1 + FC],
                                      cols[:, R_C1:R_C1 + FC * L].rearrange("p (l j) -> p l j", l=L)).then_inc(s["lv_ready"], 1)
                nc.vector.memset(layer_vecs[:, 0, V_G2P:V_G2P + 1], 1.0).then_inc(s["lv_ready"], 1)
                nc.vector.memset(layer_vecs[:, 0, V_BE2P:V_BE2P + 1], 0.0).then_inc(s["lv_ready"], 1)
                dve.wait_ge(s["lv_ready"], 6)
                dve_fold_att_first(dve, 0, False)
                dve_fold_wo(dve, 0, False)
                dve_fold_ffn_first(dve, 0, False)
                dve_fold_w2(dve, 0, False)
                for b in range(SEQS):
                    if b >= 2:
                        dve.wait_ge(s["zff_ps"], b - 1)
                    for t in range(TT):
                        i = b * TT + t
                        nc.vector.tensor_scalar(xn_tm[:, b % 2, t * D:(t + 1) * D], x_tm[:, b, t, :], mv[:, i, 0:1],
                                                r_x[:, i:i + 1], ALU.subtract, ALU.mult).then_inc(s["xn"], 1)
                        nc.vector.tensor_scalar(zf_tm[:, b % 2, t * D:(t + 1) * D], x_tm[:, b, t, :], mv[:, i, 0:1],
                                                r_f[:, i:i + 1], ALU.subtract, ALU.mult).then_inc(s["xn"], 1)
                    if b >= 1:
                        c = b - 1
                        dve.wait_ge(s["zin_hi"], c + 1)
                        nc.vector.tensor_tensor(z_lo[:, c, :], kv_ps[c % 2][:, :, :], z_hi[:, c, :].bitcast(F32),
                                                ALU.subtract).then_inc(s["state"], 1)
                c = SEQS - 1
                dve.wait_ge(s["zin_hi"], c + 1)
                nc.vector.tensor_tensor(z_lo[:, c, :], kv_ps[c % 2][:, :, :], z_hi[:, c, :].bitcast(F32),
                                        ALU.subtract).then_inc(s["state"], 1)
                ch = s["bn_chain"]
                dve.wait_ge(s["rstd_x"], 3)
                nc.vector.reciprocal(bn_v[:, 1:2], bn_v[:, 0:1]).then_inc(ch, 1)
                dve.wait_ge(ch, 1)
                dve.wait_ge(s["zff"], SEQS)
                nc.vector.tensor_scalar(z_bn[:, :], zf_sum[:, :], 1.0 / S, None, ALU.mult).then_inc(ch, 1)
                dve.wait_ge(ch, 2)
                nc.vector.tensor_scalar(z_bn[:, :], z_bn[:, :], cols[:, R_FFN + 4:R_FFN + 5], bn_v[:, 1:2],
                                        ALU.subtract, ALU.mult).then_inc(ch, 1)
                dve.wait_ge(ch, 3)
                nc.vector.tensor_scalar(z_bn[:, :], z_bn[:, :], cols[:, R_FFN + 2:R_FFN + 3],
                                        cols[:, R_FFN + 3:R_FFN + 4], ALU.mult, ALU.add).then_inc(ch, 1)
                lgs = s["logit"]
                dve.wait_ge(s["logit_ps"], 1)
                nc.vector.tensor_tensor(lg[:, :], down_ps[0:SEQS, 0:E], br_bc[:, :], ALU.add).then_inc(lgs, 1)
                dve.wait_ge(lgs, 1)
                nc.vector.reduce_max(r_cols[:, 2:3], lg[:, :], AX.X).then_inc(lgs, 1)
                dve.wait_ge(lgs, 2)
                nc.vector.tensor_scalar(r_cols[:, 0:1], r_cols[:, 2:3], -1.0, None, ALU.mult).then_inc(lgs, 1)
                dve.wait_ge(s["softmax_e"], 1)
                nc.vector.reciprocal(r_cols[:, 3:4], r_cols[:, 1:2]).then_inc(lgs, 1)
                dve.wait_ge(lgs, 4)
                nc.vector.tensor_scalar(lg_e[:, :], lg_e[:, :], r_cols[:, 3:4], None, ALU.mult).then_inc(lgs, 1)
                dve.wait_ge(lgs, 5)
                pm = s["pmax_r"]
                nc.vector.reduce_max(r_cols[:, 4:5], lg_e[:, :], AX.X).then_inc(pm, 1)
                dve.wait_ge(pm, 1)
                nc.vector.tensor_scalar(gate_d[:, :], ident[0:SEQS, 0:SEQS], r_cols[:, 4:5], None, ALU.mult).then_inc(pm, 2)
                nc.vector.tensor_scalar(lg[:, :], lg_e[:, :], r_cols[:, 4:5], None, ALU.is_equal).then_inc(lgs, 1)
                dve.wait_ge(lgs, 6)
                nc.vector.tensor_tensor(lg[:, :], lg[:, :], expert_m8[:, :], ALU.mult).then_inc(lgs, 1)
                dve.wait_ge(lgs, 7)
                nc.vector.tensor_reduce(r_cols[:, 5:6], lg[:, :], AX.X, ALU.min).then_inc(lgs, 1)
                dve.wait_ge(lgs, 8)
                nc.vector.tensor_scalar(expert_i[:, :], r_cols[:, 5:6], float(E), None, ALU.add).then_inc(s["routed"], 1)
                dve_fold_att_biases(dve, 0, False)
                dve.wait_ge(s["attb_ready"], 5)
                nc.vector.tensor_copy(cb1[:, :], colb[:, 0:1]).then_inc(s["cb1_ready"], 1)
                dve_fold_c1(dve, 0, False)
                dve_fold_cb2(dve, 0, False)
                dve.wait_ge(s["gate_ps"], 1)
                nc.vector.tensor_copy(gate_bc[:, :], down_ps[:, 0:SEQS]).then_inc(s["gate_bc_r"], 1)
                for b in range(SEQS):
                    dve.wait_ge(s["ey_ps"], b + 1)
                    dve.wait_ge(e_in[b % 2], 64 * (b // 2 + 1))
                    if b >= 2:
                        dve.wait_ge(s["gated"], b - 1)
                    nc.vector.tensor_tensor(e_y[:, b % 2, :].rearrange("p (t d) -> p t d", d=D),
                                            up_ps[b % 2][:, :].rearrange("p (t d) -> p t d", d=D),
                                            eb_up[:, b % 2, :].unsqueeze(1).to_broadcast([P, TT, D]),
                                            ALU.add).then_inc(s["ey"], 1)

        def three_pass(dst, w_hi, w_lo, a_hi, a_lo, start, stop):
            nc.tensor.matmul(dst, w_hi, a_hi, start=start, stop=False)
            nc.tensor.matmul(dst, w_hi, a_lo, start=False, stop=False)
            return nc.tensor.matmul(dst, w_lo, a_hi, start=False, stop=stop)

        def is_unit(u):
            return not isinstance(u, int) or 0 <= u < UNITS

        def after_first(u):
            return not isinstance(u, int) or u > 0

        def pe_kv(pe, u, b):
            pe.wait_ge(s["state"], u + 1)
            if after_first(u):
                pe.wait_ge(s["kv_biased"], u * 2)
            for t in range(TT):
                a_hi, a_lo = z_hi[:, b, t * P:(t + 1) * P], z_lo[:, b, t * P:(t + 1) * P]
                dst = kv_ps[t // 2][:, t % 2, :]
                nc.tensor.matmul(dst, a_hi, wqkv_hi[:, D:3 * D], start=True, stop=False)
                nc.tensor.matmul(dst, a_hi, wqkv_lo[:, D:3 * D], start=False, stop=False)
                last = nc.tensor.matmul(dst, a_lo, wqkv_hi[:, D:3 * D], start=False, stop=True)
                if t % 2:
                    last.then_inc(s["kvproj"], 1)

        def pe_q(pe, u, b):
            if after_first(u):
                pe.wait_ge(s["qphi"], u)
            three_pass(q_ps[:, :], wqkv_hi[:, 0:D], wqkv_lo[:, 0:D], z_hi[:, b, :], z_lo[:, b, :],
                       True, True).then_inc(s["qproj"], 1)

        def pe_kvt(pe, u):
            pe.wait_ge(s["kphi"], u + 1)
            if after_first(u):
                pe.wait_ge(s["lnv1_s"], u)
            for t in range(TT):
                nc.tensor.matmul(KVT, kv1[:, t, D:2 * D], k_phi[:, t, :], start=(t == 0), stop=(t == TT - 1))
            for t in range(TT):
                last = nc.tensor.matmul(KSUM, k_phi[:, t, :], ones[:, 0:1], start=(t == 0), stop=(t == TT - 1))
            last.then_inc(s["kvt_ps"], 1)

        def pe_kvo_den(pe, u):
            pe.wait_ge(s["ksumblk"], u + 1)
            nc.tensor.matmul(KVO, kvT_blk[:, :], wo_c[:, :], start=True, stop=True).then_inc(s["kvo_ps"], 1)
            pe.wait_ge(s["qphi"], u + 1)
            if is_unit(u - 2):
                pe.wait_ge(s["gelu"], (u - 1) * FC)
            nc.tensor.matmul(up_ps[1][:, :], ksum_blk[:, :], q_phi[:, :], start=True, stop=True).then_inc(s["den_ps"], 1)

        def pe_att_residual(pe, u, b):
            if after_first(u):
                pe.wait_ge(s["z1_s"], u)
            three_pass(att_ps[:, :], cg2_hi[:, :], cg2_lo[:, :], z_hi[:, b, :], z_lo[:, b, :], True, False)

        def pe_att_out(pe, u):
            pe.wait_ge(s["kvo_sb"], u + 1)
            pe.wait_ge(s["qn"], u + 1)
            nc.tensor.matmul(att_ps[:, :], kvo[:, :], q_n[:, :], start=False, stop=True).then_inc(s["att_done"], 1)

        def pe_var1(pe, u):
            pe.wait_ge(s["sq1_s"], u + 1)
            nc.tensor.matmul(small_ps[:, :], mean_mat[:, :], sq1[:, :], start=True, stop=True).then_inc(s["var1"], 1)

        def pe_up(pe, u, b):
            pe.wait_ge(s["z1lo_s"], u + 1)
            if is_unit(u + 1):
                pe.wait_ge(s["den_sb"], u + 2)
            if after_first(u):
                pe.wait_ge(s["lnv2_s"], u)
            for j in range(FC):
                if j >= 2:
                    pe.wait_ge(s["gelu"], u * FC + j - 1)
                three_pass(up_ps[j % 2][:, :], w1_hi[:, j * P:(j + 1) * P], w1_lo[:, j * P:(j + 1) * P],
                           z1_hi[:, b % 2, :], z1_lo[:, b % 2, :], True, True).then_inc(s["up"], 1)

        def pe_down(pe, u, b):
            if after_first(u):
                pe.wait_ge(s["z2_s"], u)
            three_pass(down_ps[:, :], cg1_hi[:, :], cg1_lo[:, :], z1_hi[:, b % 2, :], z1_lo[:, b % 2, :], True, False)
            for j in range(FC):
                pe.wait_ge(s["gelu"], u * FC + j + 1)
                last = nc.tensor.matmul(down_ps[:, :], w2_c[:, j, :], hid[:, j, :], start=False, stop=(j == FC - 1))
            last.then_inc(s["down"], 1)

        def pe_var2(pe, u):
            pe.wait_ge(s["sq2_s"], u + 1)
            nc.tensor.matmul(up_ps[0][:, :], mean_mat[:, :], sq2[:, :], start=True, stop=True).then_inc(s["var2"], 1)

        def pe_period(pe, l, b):
            p = l * SEQS + b
            att, ffn, proj = is_unit(p), is_unit(p - 2), is_unit(p + 1)
            if ffn:
                if b == 2:
                    pe.wait_ge(s["ffnw_ready"], l * 2 + 1)
                pe_up(pe, p - 2, b)
                if b == 2:
                    pe.wait_ge(s["ffnw_ready"], l * 2 + 2)
                    pe.wait_ge(s["fold_ffn_v"], l * 3 + 3)
                pe_down(pe, p - 2, b)
            if att:
                pe_kvt(pe, p)
                if b == 0:
                    pe.wait_ge(s["attw_ready"], l * 2 + 2)
                    pe.wait_ge(s["fold_att_v"], l * 3 + 3)
                pe_att_residual(pe, p, b)
                pe_kvo_den(pe, p)
            if ffn:
                pe_var2(pe, p - 2)
            if proj:
                if b == SEQS - 1:
                    if p_nonneg(p):
                        pe.wait_ge(s["kvo_sb"], p + 1)
                        pe_fold_att(pe, l + 1, True)
                        pe_fold_ffn(pe, l + 1, True)
                    pe.wait_ge(s["attw_ready"], l * 2 + 3)
                pe_kv(pe, p + 1, (b + 1) % SEQS)
            if att:
                pe_att_out(pe, p)
            if proj:
                pe_q(pe, p + 1, (b + 1) % SEQS)
            if att:
                if b == SEQS - 1 and proj:
                    pe.wait_ge(s["attb_ready"], l * 5 + 10)
                pe_var1(pe, p)

        def act_period(act, l, b):
            p = l * SEQS + b
            att, ffn, ln1 = is_unit(p), is_unit(p - 2), is_unit(p - 1)
            u = p - 2
            if ffn:
                if b == 2:
                    act.wait_ge(s["c1_ready"], l + 1)
                if after_first(u):
                    act.wait_ge(s["down"], u)
                for j in range(FC):
                    act.wait_ge(s["up"], u * FC + j + 1)
                    nc.scalar.activation(hid[:, j, :], up_ps[j % 2][:, :], ACT.Gelu,
                                         bias=c1_f[:, j:j + 1]).then_inc(s["gelu"], 1)
            nc.scalar.preload_act_table_set("natural_log_exp_and_others")
            if att:
                act.wait_ge(s["kmin"], p + 1)
                if after_first(p):
                    act.wait_ge(s["kphi"], p)
                nc.scalar.activation(k_exp[:, :, :], k_min[:, :, :], ACT.Exp, bias=neg1_col[:, :]).then_inc(s["kexp"], 1)
                act.wait_ge(s["qmin"], p + 1)
                if after_first(p):
                    act.wait_ge(s["qphi"], p)
                nc.scalar.activation(q_exp[:, :], q_min[:, :], ACT.Exp).then_inc(s["qexp"], 1)
            if ln1:
                act.wait_ge(s["var1"], p)
                nc.scalar.activation(lnv1[:, :], small_ps[:, :], ACT.Ln, bias=eps_col[:, :]).then_inc(s["lnv1_s"], 1)
                act.wait_ge(s["lnv1_s"], p)
                if after_first(p - 1):
                    act.wait_ge(s["z1_s"], p - 1)
                nc.scalar.activation(rstd1[:, :], lnv1[:, :], ACT.Exp, scale=-0.5).then_inc(s["rstd1_s"], 1)
            if ffn:
                act.wait_ge(s["down"], u + 1)
                if b == 2:
                    act.wait_ge(s["cb2_ready"], l + 1)
                if after_first(u):
                    act.wait_ge(s["var2"], u)
                nc.scalar.activation(sq2[:, :], down_ps[:, :], ACT.Square, bias=cb2[:, :]).then_inc(s["sq2_s"], 1)
            if ln1:
                act.wait_ge(s["z1_s"], p)
                if is_unit(p - 3):
                    act.wait_ge(s["down"], p - 2)
                nc.scalar.activation(z1_hi[:, (b - 1) % 2, :], z1[:, :], ACT.Identity).then_inc(s["z1hi_s"], 1)
            if att:
                act.wait_ge(s["den_ps"], p + 1)
                nc.scalar.activation(den[:, :], up_ps[1][:, :], ACT.Ln, bias=den_eps_col[:, :]).then_inc(s["den_sb"], 1)
                act.wait_ge(s["den_sb"], p + 1)
                if after_first(p):
                    act.wait_ge(s["qn"], p)
                nc.scalar.activation(rden[:, :], den[:, :], ACT.Exp, scale=-1.0).then_inc(s["rden_s"], 1)
            if ffn:
                act.wait_ge(s["var2"], u + 1)
                nc.scalar.activation(lnv2[:, :], up_ps[0][:, :], ACT.Ln, bias=eps_col[:, :]).then_inc(s["lnv2_s"], 1)
                act.wait_ge(s["lnv2_s"], u + 1)
                if after_first(u):
                    act.wait_ge(s["z2_s"], u)
                nc.scalar.activation(rstd2[:, :], lnv2[:, :], ACT.Exp, scale=-0.5).then_inc(s["rstd2_s"], 1)
            if att:
                act.wait_ge(s["att_done"], p + 1)
                if b == 0:
                    act.wait_ge(s["cb1_ready"], l + 1)
                if after_first(p):
                    act.wait_ge(s["var1"], p)
                nc.scalar.activation(sq1[:, :], att_ps[:, :], ACT.Square, bias=cb1[:, :]).then_inc(s["sq1_s"], 1)
            if ffn:
                act.wait_ge(s["z2_s"], u + 1)
                nc.scalar.activation(z_hi[:, (b - 2) % SEQS, :], z2[:, :], ACT.Identity).then_inc(s["z2hi_s"], 1)

        def dve_kv_bias(dve, u):
            if after_first(u):
                dve.wait_ge(s["kvt_ps"], u)
            for i in range(2):
                dve.wait_ge(s["kvproj"], u * 2 + i + 1)
                nc.vector.tensor_tensor(kv1[:, 2 * i:2 * i + 2, :], kv_ps[i][:, :, :],
                                        bkv1_bc[:, :].unsqueeze(1).to_broadcast([P, 2, 2 * D]),
                                        ALU.add).then_inc(s["kv_biased"], 1)
            if after_first(u):
                dve.wait_ge(s["kexp"], u)
            dve.wait_ge(s["kv_biased"], u * 2 + 2)
            nc.vector.tensor_scalar(k_min[:, :, :], kv1[:, :, 0:D], 1.0, None, ALU.min).then_inc(s["kmin"], 1)

        def dve_q_min(dve, u):
            dve.wait_ge(s["qproj"], u + 1)
            if after_first(u):
                dve.wait_ge(s["qexp"], u)
            nc.vector.tensor_scalar(q_min[:, :], q_ps[:, :], bq_f[:, 0:1], 0.0, ALU.add, ALU.min).then_inc(s["qmin"], 1)

        def dve_phi(dve, u):
            dve.wait_ge(s["kexp"], u + 1)
            nc.vector.tensor_scalar(k_exp[:, :, :], k_exp[:, :, :], -1.0, 1.0, ALU.add, ALU.add).then_inc(s["kexpm1"], 1)
            dve.wait_ge(s["kexpm1"], u + 1)
            nc.vector.tensor_tensor(k_phi[:, :, :], k_exp[:, :, :], kv1[:, :, 0:D], ALU.max).then_inc(s["kphi"], 1)
            dve.wait_ge(s["qexp"], u + 1)
            nc.vector.tensor_scalar(q_exp[:, :], q_exp[:, :], -1.0, 1.0, ALU.add, ALU.add).then_inc(s["qexpm1"], 1)
            dve.wait_ge(s["qexpm1"], u + 1)
            if after_first(u):
                dve.wait_ge(s["qn"], u)
            nc.vector.scalar_tensor_tensor(q_phi[:, :], q_ps[:, :], bq_f[:, 1:2], q_exp[:, :],
                                           ALU.add, ALU.max).then_inc(s["qphi"], 1)

        def dve_blocks(dve, u):
            dve.wait_ge(s["kvt_ps"], u + 1)
            if after_first(u):
                dve.wait_ge(s["den_ps"], u)
            nc.vector.tensor_tensor(kvT_blk[:, :], KVT, head_mask[:, :], ALU.mult).then_inc(s["kvtblk"], 1)
            nc.vector.tensor_scalar(ksum_blk[:, :], head_mask[:, :], KSUM, None, ALU.mult).then_inc(s["ksumblk"], 1)

        def dve_kvo(dve, u):
            dve.wait_ge(s["kvo_ps"], u + 1)
            if after_first(u):
                dve.wait_ge(s["att_done"], u)
            nc.vector.tensor_copy(kvo[:, :], KVO).then_inc(s["kvo_sb"], 1)

        def dve_period(dve, l, b):
            p = l * SEQS + b
            att, ffn, ln1, proj = is_unit(p), is_unit(p - 2), is_unit(p - 1), is_unit(p + 1)
            u = p - 2
            fold = isinstance(l, int) is False or l + 1 < L
            folded = isinstance(l, int) is False or l > 0
            if att:
                dve_phi(dve, p)
            if ln1:
                dve.wait_ge(s["rstd1_s"], p)
                if after_first(p - 1):
                    dve.wait_ge(s["z1lo_s"], p - 1)
                nc.vector.scalar_tensor_tensor(z1[:, :], att_ps[:, :], cb1[:, :], rstd1[:, :],
                                               ALU.add, ALU.mult).then_inc(s["z1_s"], 1)
            if att and b == 0 and folded:
                dve.wait_ge(s["z1_s"], p)
                nc.vector.tensor_copy(cb1[:, :], colb[:, 0:1]).then_inc(s["cb1_ready"], 1)
            if att:
                dve_blocks(dve, p)
            if ln1:
                dve.wait_ge(s["z1hi_s"], p)
                if is_unit(p - 3):
                    dve.wait_ge(s["down"], p - 2)
                nc.vector.tensor_tensor(z1_lo[:, (b - 1) % 2, :], z1[:, :], z1_hi[:, (b - 1) % 2, :].bitcast(F32),
                                        ALU.subtract).then_inc(s["z1lo_s"], 1)
            if att:
                dve_kvo(dve, p)
                if b == SEQS - 1 and fold and p_nonneg(p):
                    dve_fold_wo(dve, l + 1, True)
                dve.wait_ge(s["rden_s"], p + 1)
                nc.vector.tensor_tensor(q_n[:, :], q_phi[:, :], rden[:, :], ALU.mult).then_inc(s["qn"], 1)
            if b == 1 and folded and ffn and is_layer(l):
                dve_fold_c1(dve, l, True)
            if proj:
                if b == SEQS - 1 and p_nonneg(p):
                    dve_fold_att_biases(dve, l + 1, True)
                if b == SEQS - 1:
                    dve.wait_ge(s["attb_ready"], l * 5 + 10)
                dve_kv_bias(dve, p + 1)
            if ffn:
                dve.wait_ge(s["rstd2_s"], u + 1)
                if after_first(u):
                    dve.wait_ge(s["state"], u + SEQS)
                nc.vector.scalar_tensor_tensor(z2[:, :], down_ps[:, :], cb2[:, :], rstd2[:, :],
                                               ALU.add, ALU.mult).then_inc(s["z2_s"], 1)
            if proj:
                dve_q_min(dve, p + 1)
            if ffn:
                dve.wait_ge(s["z2hi_s"], u + 1)
                nc.vector.tensor_tensor(z_lo[:, (b - 2) % SEQS, :], z2[:, :], z_hi[:, (b - 2) % SEQS, :].bitcast(F32),
                                        ALU.subtract).then_inc(s["state"], 1)
            if b == 1 and folded and ffn and is_layer(l):
                dve_fold_w2(dve, l, True)
                dve_fold_cb2(dve, l, True)
            if b == SEQS - 2 and fold:
                dve_fold_att_first(dve, l + 1, True)
                dve_fold_ffn_first(dve, l + 1, True)

        def p_nonneg(p):
            return not isinstance(p, int) or p >= 0

        def is_layer(l):
            return not isinstance(l, int) or l < L

        with nc.Block() as block:
            def all_periods(eng, period):
                period(eng, -1, SEQS - 1)
                for b in range(SEQS):
                    period(eng, 0, b)
                with eng.Fori(1, L - 1) as l:
                    for b in range(SEQS):
                        period(eng, l, b)
                for b in range(SEQS + 2):
                    period(eng, L - 1 + b // SEQS, b % SEQS)

            @block.sync
            def _(sp):
                with sp.Fori(1, L) as l:
                    l2, l3 = l * 2, l * 3
                    sp.wait_ge(s["attw_ready"], l2)
                    sp.wait_ge(s["ffnw_ready"], l2)
                    sp.sem_inc(s["sp_waited"], 1)
                    sp.wait_ge(s["fold_att_v"], l3)
                    sp.wait_ge(s["fold_ffn_v"], l3)
                    sp.wait_ge(s["attb_ps"], l3)
                    sp.sem_inc(s["sp_waited"], 1)
                    sp.wait_ge(s["ffnb_ps"], l)
                    sp.sem_inc(s["sp_waited"], 1)
                    load_layer(sp, l)

            @block.gpsimd
            def _(pool):
                with pool.Fori(1, L) as l:
                    pool_fold_att(pool, l, True)
                    pool_fold_ffn(pool, l, True)

            @block.tensor
            def _(pe):
                all_periods(pe, pe_period)

            @block.scalar
            def _(act):
                all_periods(act, act_period)

            @block.vector
            def _(dve):
                all_periods(dve, dve_period)

        h_tm = hid[:, :, :].rearrange("p b (t d) -> p b t d", d=D)
        y_tm = sb("y_tm", [P, 2, TT, D])
        f_st = sb("f_st", [P, SEQS * TT, 6])
        f_mv = sb("f_mv", [P, SEQS * TT, 2])
        f_std = sb("f_std", [P, SEQS * TT])
        f_r = sb("f_r", [P, SEQS * TT])
        g_hi, g_lo = cg2_hi, cg2_lo
        o_sent = [sem(f"o_sent{i}") for i in range(2)]
        with nc.Block() as block:
            @block.gpsimd
            def _(pool):
                f = s["fin"]
                nc.gpsimd.tensor_scalar(fold_cg2[:, :], ident[:, :], layer_vecs[:, L, V_G2P:V_G2P + 1], None,
                                        ALU.mult).then_inc(f, 1)
                nc.gpsimd.tensor_scalar(be2_bc[:, :], ones[:, :], layer_vecs[:, L, V_BE2P:V_BE2P + 1], None,
                                        ALU.mult).then_inc(f, 1)
                pool.wait_ge(f, 2)
                nc.gpsimd.tensor_copy(g_hi[:, :], fold_cg2[:, :]).then_inc(f, 1)
                pool.wait_ge(f, 3)
                nc.gpsimd.tensor_tensor(g_lo[:, :], fold_cg2[:, :], g_hi[:, :].bitcast(F32), ALU.subtract).then_inc(f, 1)

            @block.tensor
            def _(pe):
                pe.wait_ge(s["fin"], 4)
                nc.tensor.matmul(small_ps[:, 0:P], be2_bc[:, :], ident[:, :], start=True, stop=True).then_inc(s["bias_in"], 1)
                banks = [up_ps[0], up_ps[1]]
                for b in range(SEQS):
                    if b >= 2:
                        pe.wait_ge(s["htm"], b - 1)
                    for t in range(TT):
                        a_hi, a_lo = z_hi[:, b, t * P:(t + 1) * P], z_lo[:, b, t * P:(t + 1) * P]
                        dst = banks[b % 2][:, t * P:(t + 1) * P]
                        nc.tensor.matmul(dst, a_hi, g_hi[:, :], start=True, stop=False)
                        nc.tensor.matmul(dst, a_hi, g_lo[:, :], start=False, stop=False)
                        last = nc.tensor.matmul(dst, a_lo, g_hi[:, :], start=False, stop=True)
                    last.then_inc(s["htm_ps"], 1)

            @block.scalar
            def _(act):
                for b in range(SEQS):
                    act.wait_ge(s["fstd"], 3 + TT * (b + 1))
                    nc.scalar.activation(f_std[:, b * TT:(b + 1) * TT], f_mv[:, b * TT:(b + 1) * TT, 1], ACT.Sqrt,
                                         bias=eps_col[:, :]).then_inc(s["frstd"], 1)

            @block.vector
            def _(dve):
                dve.wait_ge(s["bias_in"], 1)
                nc.vector.tensor_copy(bkv1_bc[:, 0:P], small_ps[:, 0:P]).then_inc(s["zsum"], 1)
                dve.wait_ge(s["zsum"], 1)
                sc = s["eh"]
                sent = 0
                for b in range(SEQS + 1):
                    if b < SEQS:
                        dve.wait_ge(s["htm_ps"], b + 1)
                        nc.vector.tensor_tensor(h_tm[:, b % 4], up_ps[b % 2][:, :].rearrange("p (t d) -> p t d", d=D),
                                                bkv1_bc[:, 0:P].unsqueeze(1).to_broadcast([P, TT, D]),
                                                ALU.add).then_inc(s["htm"], 1)
                        dve.wait_ge(s["htm"], b + 1)
                        for t in range(TT):
                            nc.vector.bn_stats(f_st[:, b * TT + t, :], h_tm[:, b % 4, t, :]).then_inc(s["fstat"], 1)
                        for t in range(TT):
                            dve.wait_ge(s["fstat"], SEQS * TT + b * TT + t + 1)
                            nc.vector.bn_aggr(f_mv[:, b * TT + t, :], f_st[:, b * TT + t, :]).then_inc(s["fstd"], 1)
                    if b >= 1:
                        c = b - 1
                        dve.wait_ge(s["frstd"], c + 1)
                        dve.wait_ge(s["fstd"], 3 + TT * (c + 1))
                        nc.vector.reciprocal(f_r[:, c * TT:(c + 1) * TT], f_std[:, c * TT:(c + 1) * TT]).then_inc(s["bias_in"], 1)
                        dve.wait_ge(s["bias_in"], c + 2)
                        if c >= 2:
                            dve.wait_ge(o_sent[c % 2], 16 * (c // 2))
                        y = y_tm[:, c % 2]
                        for t in range(TT):
                            i = c * TT + t
                            nc.vector.tensor_scalar(y[:, t, :], h_tm[:, c % 4, t, :], f_mv[:, i, 0:1], f_r[:, i:i + 1],
                                                    ALU.subtract, ALU.mult).then_inc(s["z1hi_s"], 1)
                        dve.wait_ge(s["z1hi_s"], UNITS + TT * (c + 1))
                        nc.vector.tensor_tensor(y, y, gf_bc[:, :].unsqueeze(1).to_broadcast([P, TT, D]), ALU.mult).then_inc(s["z2hi_s"], 1)
                        dve.wait_ge(s["z2hi_s"], UNITS + 3 * c + 1)
                        nc.vector.tensor_tensor(y, y, bef_bc[:, :].unsqueeze(1).to_broadcast([P, TT, D]), ALU.add).then_inc(s["z2hi_s"], 1)
                        dve.wait_ge(s["z2hi_s"], UNITS + 3 * c + 2)
                        nc.vector.tensor_tensor(y, y, gate_tm[:, c], ALU.mult).then_inc(s["z2hi_s"], 1)
                        dve.wait_ge(s["z2hi_s"], UNITS + 3 * c + 3)
                        nc.vector.tensor_tensor(y, y, x_tm[:, c], ALU.add).then_inc(s["out_sent"], 1)

            @block.sync
            def _(sp):
                for b in range(SEQS):
                    sp.wait_ge(s["out_sent"], b + 1)
                    sp.dma_start(out_dram[:, b], y_tm[:, b % 2]).then_inc(o_sent[b % 2], 16)
                sp.wait_ge(o_sent[0], 16 * SEQS // 2)
                sp.wait_ge(o_sent[1], 16 * SEQS // 2)


NAMES = ("x", "Wq", "bq", "Wk", "bk", "Wv", "bv", "Wo", "bo", "g1", "be1", "g2", "be2", "W1", "c1", "W2", "c2",
         "gf", "bef")
FFN_NAMES = ("ln_g", "ln_b", "bn_g", "bn_b", "bn_mean", "bn_var", "Wr", "br", "W_down", "b_down", "W_up", "b_up")


def kernel(**inputs):
    import numpy as np
    import concourse.bacc as bacc
    from concourse.bass_utils import run_bass_kernel_spmd

    nc = bacc.Bacc("TRN2", target_bir_lowering=False, num_devices=1)
    arrays, args = {}, []
    for name in [f"L0_attn_{n}" for n in NAMES] + [f"L0_ffn_{n}" for n in FFN_NAMES]:
        a = np.ascontiguousarray(inputs[name])
        arrays[f"in_{name}"] = a
        args.append(nc.dram_tensor(f"in_{name}", a.shape, mybir.dt.from_np(a.dtype), kind="ExternalInput").ap())
    shape = inputs["L0_attn_x"].shape
    out = nc.dram_tensor("out_y", shape, mybir.dt.float32, kind="ExternalOutput").ap()
    build(nc, *args, out)
    r = run_bass_kernel_spmd(nc, [arrays], core_ids=[0])
    return r.results[0]["out_y"]
```

```python
import concourse.bass as bass
from concourse import mybir
from contextlib import ExitStack

P = 128
EPS = 1e-5
DEN_EPS = 1e-6


def build(nc, x, Wq, bq, Wk, bk, Wv, bv, Wo, bo, g1, be1, g2, be2, W1, c1, W2, c2, gf, bef,
          ln_g, ln_b, bn_g, bn_b, bn_mean, bn_var, Wr, br, W_down, b_down, W_up, b_up, out):
    F32 = mybir.dt.float32
    F32R = mybir.dt.float32r
    I32 = mybir.dt.int32
    ALU = mybir.AluOpType
    ACT = mybir.ActivationFunctionType
    AX = mybir.AxisListType

    SEQS, S, D = x.shape
    L = Wq.shape[0]
    F = W1.shape[2]
    FC = F // P
    DH = D // 16
    UNITS = L * SEQS
    TT = S // P
    E, _, HID = W_down.shape
    assert D == P and S == 512 and E == SEQS

    x_dram = x.rearrange("b (p s) d -> p b s d", s=TT)
    out_dram = out.rearrange("b (p s) d -> p b s d", s=TT)

    with ExitStack() as ctx:
        def sb(name, shape, dt=F32):
            return ctx.enter_context(nc.sbuf_tensor(name, shape, dt))

        def ps(name, shape):
            return ctx.enter_context(nc.psum_tensor(name, shape, F32))

        def sem(name):
            return ctx.enter_context(nc.semaphore(name))

        ident = sb("ident", [P, P])
        centre = sb("centre", [P, P])
        head_mask = sb("head_mask", [P, P])
        mean_f32 = sb("mean_f32", [P, P])
        mean_mat = sb("mean_mat", [P, P], F32R)
        ones = sb("ones", [P, P])
        eps_col = sb("eps_col", [P, 1])
        den_eps_col = sb("den_eps_col", [P, 1])
        neg1_col = sb("neg1_col", [P, 1])
        expert_m8 = sb("expert_m8", [SEQS, E])

        x_tm = sb("x_tm", [P, SEQS, TT, D])
        gate_tm = sb("gate_tm", [P, SEQS, TT, D])
        vec_rows = sb("vec_rows", [P, D])
        NVEC = 7 * L + FC * L + 6
        R_C1 = 7 * L
        R_FFN = R_C1 + FC * L
        cols = sb("cols", [P, NVEC])
        NLV = 7 + FC
        layer_vecs = sb("layer_vecs", [P, L + 1, NLV])
        V_BQ, V_BO, V_G1, V_BE1, V_G2P, V_BE2P, V_C2, V_C1 = range(8)
        gf_bc = sb("gf_bc", [P, D])
        bef_bc = sb("bef_bc", [P, D])
        z_hi = sb("z_hi", [P, SEQS, S], F32R)
        z_lo = sb("z_lo", [P, SEQS, S], F32R)

        raw_att = sb("raw_att", [P, 4, D])
        raw_w1 = sb("raw_w1", [P, F])
        raw_w2 = sb("raw_w2", [P, FC, D])
        raw_bkv = sb("raw_bkv", [1, 2 * D])
        lv_a = sb("lv_a", [P, NLV])
        lv_f = sb("lv_f", [P, NLV])
        fold_att = sb("fold_att", [P, 3 * D])
        fold_cg2 = sb("fold_cg2", [P, D])
        fold_w1 = sb("fold_w1", [P, F])
        fold_cg1 = sb("fold_cg1", [P, D])
        wqkv_hi = sb("wqkv_hi", [P, 3 * D], F32R)
        wqkv_lo = sb("wqkv_lo", [P, 3 * D], F32R)
        cg2_hi = sb("cg2_hi", [P, D], F32R)
        cg2_lo = sb("cg2_lo", [P, D], F32R)
        wo_sum = sb("wo_sum", [P, 1])
        wo_c = sb("wo_c", [P, D])
        w1_hi = sb("w1_hi", [P, F], F32R)
        w1_lo = sb("w1_lo", [P, F], F32R)
        cg1_hi = sb("cg1_hi", [P, D], F32R)
        cg1_lo = sb("cg1_lo", [P, D], F32R)
        w2_sum = sb("w2_sum", [P, FC])
        w2_c = sb("w2_c", [P, FC, D])
        w2_hi = sb("w2_hi", [P, FC, D], F32R)
        w2_lo = sb("w2_lo", [P, FC, D], F32R)
        be2_bc = sb("be2_bc", [P, P])
        bkv1_bc = sb("bkv1_bc", [P, 2 * D])
        bo_be2 = sb("bo_be2", [P, 1])
        c2_be1 = sb("c2_be1", [P, 1])
        bq_f = sb("bq_f", [P, 2])
        cb1 = sb("cb1", [P, 1])
        c1_f = sb("c1_f", [P, FC])
        colb = sb("colb", [P, FC + 2])
        cb2 = sb("cb2", [P, 1])

        kv1 = sb("kv1", [P, TT, 2 * D + 1])
        k_min = sb("k_min", [P, TT, D])
        k_exp = sb("k_exp", [P, TT, D])
        k_phi = sb("k_phi", [P, TT, D])
        q_exp = sb("q_exp", [P, S])
        q_min = sb("q_min", [P, S])
        q_phi = sb("q_phi", [P, S])
        ksum_blk = sb("ksum_blk", [P, P])
        kv_blk = sb("kv_blk", [P, P])
        kvT_blk = sb("kvT_blk", [P, P])
        kvo = sb("kvo", [P, P])
        den = sb("den", [P, S])
        rden = sb("rden", [P, S])
        q_n = sb("q_n", [P, S])
        sq1 = sb("sq1", [P, S])
        sq1_hi = sb("sq1_hi", [P, S], F32R)
        sq1_lo = sb("sq1_lo", [P, S], F32R)
        hc2 = sb("hc2", [P, S])
        sq2 = sb("sq2", [P, S])
        sq2_hi = sb("sq2_hi", [P, S], F32R)
        sq2_lo = sb("sq2_lo", [P, S], F32R)
        lnv1 = sb("lnv1", [P, S])
        lnv2 = sb("lnv2", [P, S])
        rstd1 = sb("rstd1", [P, S])
        rstd2 = sb("rstd2", [P, S])
        z1 = sb("z1", [P, S])
        z1_hi = sb("z1_hi", [P, 2, S], F32R)
        z1_lo = sb("z1_lo", [P, 2, S], F32R)
        z2 = sb("z2", [P, S])
        hid = sb("hid", [P, FC, S])
        hid_hi = sb("hid_hi", [P, FC, S], F32R)
        hid_lo = sb("hid_lo", [P, FC, S], F32R)

        kv_ps = [ps(f"kv_ps{i}", [P, TT // 2, 2 * D]) for i in range(2)]
        q_ps = ps("q_ps", [P, S])
        small_ps = ps("small_ps", [P, 512])
        KV_KSUM, KVT, KVO = small_ps[:, 0:P + 1], small_ps[:, 2 * P:3 * P], small_ps[:, 3 * P:4 * P]
        BIAS, COLB = small_ps[:, 0:2 * P], small_ps[:, 2 * P:2 * P + 8]
        att_ps = ps("att_ps", [P, S])
        up_ps = [ps(f"up_ps{i}", [P, S]) for i in range(2)]
        down_ps = ps("down_ps", [P, S])

        names = """pool_waited sp_waited x_in vec_in row_in fold_in const_ready
            kv_ps kvblk kvt_sb att_fold ffn_fold wqkv_split cg2_split wo_ready w1_split ffnw_split
            hc2_s sq1hi_s sq1lo_s sq2hi_s sq2lo_s hid_hi_s hid_lo_s
            stats rstd_x xn tr_ps cols_ready lv_ready zsum zin_ps zin_hi
            zff_ps zff bn_chain logit_ps logit pmax_r softmax_e routed expert_in gate_ps gate_bc_r
            eh_ps eh ey_ps ey gated
            raw_loaded bias_in attb_ps ffnb_ps attb_ready cb1_ready c1_ready cb2_ready
            kvproj qproj kv_biased kmin kexp kexpm1 qexpm1 kphi qexp qmin qphi kvt_ps ksumblk kvo_ps kvo_sb
            den_ps den_sb rden_s qn att_done sq1_s var1 lnv1_s rstd1_s z1_s z1hi_s z1lo_s
            up gelu down sq2_s var2 lnv2_s rstd2_s z2_s z2hi_s state
            htm_ps htm fstat fstd frstd fin out_sent""".split()
        s = {n: sem(n) for n in names}
        x_in = [sem(f"x_in{i}") for i in range(4)]

        def load_layer(sp, l):
            sp.dma_start(raw_att[:, 0, :], Wq[l]).then_inc(s["raw_loaded"], 16)
            sp.dma_start(raw_att[:, 1, :], Wk[l]).then_inc(s["raw_loaded"], 16)
            sp.dma_start(raw_att[:, 2, :], Wv[l]).then_inc(s["raw_loaded"], 16)
            sp.dma_start(raw_att[:, 3, :], Wo[l]).then_inc(s["raw_loaded"], 16)
            sp.dma_start(raw_bkv[0:1, 0:D], bk[l:l + 1, :] if isinstance(l, int) else bk[bass.ds(l, 1), :]).then_inc(s["raw_loaded"], 16)
            sp.dma_start(raw_bkv[0:1, D:2 * D], bv[l:l + 1, :] if isinstance(l, int) else bv[bass.ds(l, 1), :]).then_inc(s["raw_loaded"], 16)
            sp.dma_start(raw_w1[:, :], W1[l]).then_inc(s["raw_loaded"], 16)
            sp.dma_start(raw_w2[:, :, :], W2[l].rearrange("(j p) n -> p j n", p=P)).then_inc(s["raw_loaded"], 16)
        LOADS = 8 * 16

        ATT_STEPS, FFN_STEPS = 7, 7

        def dve_fold_att_first(dve, l, wait_free):
            a = l * ATT_STEPS
            dve.wait_ge(s["raw_loaded"], l * LOADS + LOADS)
            if wait_free:
                dve.wait_ge(s["attb_ps"], l)
                dve.wait_ge(s["attb_ready"], l * 5)
                dve.wait_ge(s["wqkv_split"], l * 2)
                dve.wait_ge(s["cg2_split"], l * 2)
            nc.vector.tensor_scalar(lv_a[:, :], layer_vecs[:, l, :], 1.0, None, ALU.mult).then_inc(s["att_fold"], 1)
            nc.vector.reduce_sum(wo_sum[:, :], raw_att[:, 3, :], AX.X).then_inc(s["att_fold"], 1)
            dve.wait_ge(s["att_fold"], a + 1)
            nc.vector.tensor_tensor(bo_be2[:, :], lv_a[:, V_BO:V_BO + 1], lv_a[:, V_BE2P:V_BE2P + 1],
                                    ALU.add).then_inc(s["att_fold"], 1)
            dve.wait_ge(s["att_fold"], a + 2)
            nc.vector.tensor_scalar(wo_sum[:, :], wo_sum[:, :], 1.0 / D, None,
                                    ALU.mult).then_inc(s["att_fold"], 1)
            nc.vector.tensor_scalar(be2_bc[:, :], ones[:, :], lv_a[:, V_BE2P:V_BE2P + 1], None,
                                    ALU.mult).then_inc(s["att_fold"], 1)
            nc.vector.tensor_scalar(fold_att[:, :], raw_att[:, 0:3, :], lv_a[:, V_G2P:V_G2P + 1], None,
                                    ALU.mult).then_inc(s["att_fold"], 1)
            nc.vector.tensor_scalar(fold_cg2[:, :], centre[:, :], lv_a[:, V_G2P:V_G2P + 1], None,
                                    ALU.mult).then_inc(s["att_fold"], 1)

        def dve_split_wqkv(dve, l, wait_free):
            dve.wait_ge(s["att_fold"], l * ATT_STEPS + 6)
            if wait_free:
                dve.wait_ge(s["qproj"], l * SEQS)
                dve.wait_ge(s["kvproj"], l * SEQS * 2)
            nc.vector.tensor_copy(wqkv_hi[:, :], fold_att[:, :]).then_inc(s["wqkv_split"], 1)
            dve.wait_ge(s["wqkv_split"], l * 2 + 1)
            nc.vector.tensor_tensor(wqkv_lo[:, :], fold_att[:, :], wqkv_hi[:, :].bitcast(F32),
                                    ALU.subtract).then_inc(s["wqkv_split"], 1)

        def dve_split_cg2(dve, l, wait_free):
            dve.wait_ge(s["att_fold"], l * ATT_STEPS + 7)
            if wait_free:
                dve.wait_ge(s["att_done"], l * SEQS)
            nc.vector.tensor_copy(cg2_hi[:, :], fold_cg2[:, :]).then_inc(s["cg2_split"], 1)
            dve.wait_ge(s["cg2_split"], l * 2 + 1)
            nc.vector.tensor_tensor(cg2_lo[:, :], fold_cg2[:, :], cg2_hi[:, :].bitcast(F32),
                                    ALU.subtract).then_inc(s["cg2_split"], 1)

        def dve_fold_wo(dve, l, wait_free):
            dve.wait_ge(s["att_fold"], l * ATT_STEPS + 4)
            if wait_free:
                dve.wait_ge(s["kvo_ps"], l * SEQS)
            nc.vector.tensor_scalar(wo_c[:, :], raw_att[:, 3, :], wo_sum[:, :], None,
                                    ALU.subtract).then_inc(s["wo_ready"], 1)

        def dve_fold_att_biases(dve, l, wait_free):
            dve.wait_ge(s["attb_ps"], l + 1)
            dve.wait_ge(s["ffnb_ps"], l + 1)
            if wait_free:
                dve.wait_ge(s["cb1_ready"], l)
                dve.wait_ge(s["cb2_ready"], l)
                dve.wait_ge(s["c1_ready"], l)
                dve.wait_ge(s["qphi"], l * SEQS)
                dve.wait_ge(s["kv_biased"], l * SEQS * 2)
            nc.vector.tensor_scalar(bkv1_bc[:, 0:D], BIAS[:, 0:D], 1.0, None, ALU.add).then_inc(s["attb_ready"], 1)
            nc.vector.tensor_copy(bkv1_bc[:, D:2 * D], BIAS[:, D:2 * D]).then_inc(s["attb_ready"], 1)
            nc.vector.tensor_copy(colb[:, :], COLB[:, 1:3 + FC]).then_inc(s["attb_ready"], 1)
            nc.vector.tensor_scalar(bq_f[:, 0:1], COLB[:, 0:1], lv_a[:, V_BQ:V_BQ + 1], None,
                                    ALU.add).then_inc(s["attb_ready"], 1)
            nc.vector.tensor_scalar(bq_f[:, 1:2], COLB[:, 0:1], lv_a[:, V_BQ:V_BQ + 1], 1.0,
                                    ALU.add, ALU.add).then_inc(s["attb_ready"], 1)

        def dve_fold_ffn_first(dve, l, wait_free):
            f = l * FFN_STEPS
            if wait_free:
                dve.wait_ge(s["ffnb_ps"], l)
                dve.wait_ge(s["c1_ready"], l)
                dve.wait_ge(s["w1_split"], l * 2)
                dve.wait_ge(s["ffnw_split"], l * 4)
            nc.vector.tensor_scalar(lv_f[:, :], layer_vecs[:, l, :], 1.0, None, ALU.mult).then_inc(s["ffn_fold"], 1)
            nc.vector.reduce_sum(w2_sum[:, :], raw_w2[:, :, :], AX.X).then_inc(s["ffn_fold"], 1)
            dve.wait_ge(s["ffn_fold"], f + 1)
            nc.vector.tensor_tensor(c2_be1[:, :], lv_f[:, V_C2:V_C2 + 1], lv_f[:, V_BE1:V_BE1 + 1],
                                    ALU.add).then_inc(s["ffn_fold"], 1)
            dve.wait_ge(s["ffn_fold"], f + 2)
            nc.vector.tensor_scalar(w2_sum[:, :], w2_sum[:, :], 1.0 / D, None,
                                    ALU.mult).then_inc(s["ffn_fold"], 1)
            nc.vector.tensor_scalar(fold_w1[:, :], raw_w1[:, :], lv_f[:, V_G1:V_G1 + 1], None,
                                    ALU.mult).then_inc(s["ffn_fold"], 1)
            nc.vector.tensor_scalar(fold_cg1[:, :], centre[:, :], lv_f[:, V_G1:V_G1 + 1], None,
                                    ALU.mult).then_inc(s["ffn_fold"], 1)
            dve.wait_ge(s["ffn_fold"], f + 4)
            nc.vector.tensor_tensor(w2_c[:, :, :], raw_w2[:, :, :],
                                    w2_sum[:, :].unsqueeze(2).to_broadcast([P, FC, D]),
                                    ALU.subtract).then_inc(s["ffn_fold"], 1)

        def dve_split_w1(dve, l, wait_free):
            dve.wait_ge(s["ffn_fold"], l * FFN_STEPS + 5)
            if wait_free:
                dve.wait_ge(s["up"], l * SEQS * FC)
            nc.vector.tensor_copy(w1_hi[:, :], fold_w1[:, :]).then_inc(s["w1_split"], 1)
            dve.wait_ge(s["w1_split"], l * 2 + 1)
            nc.vector.tensor_tensor(w1_lo[:, :], fold_w1[:, :], w1_hi[:, :].bitcast(F32),
                                    ALU.subtract).then_inc(s["w1_split"], 1)

        def dve_split_ffn(dve, l, wait_free):
            dve.wait_ge(s["ffn_fold"], l * FFN_STEPS + 7)
            if wait_free:
                dve.wait_ge(s["down"], l * SEQS)
            nc.vector.tensor_copy(cg1_hi[:, :], fold_cg1[:, :]).then_inc(s["ffnw_split"], 1)
            nc.vector.tensor_copy(w2_hi[:, :, :], w2_c[:, :, :]).then_inc(s["ffnw_split"], 1)
            dve.wait_ge(s["ffnw_split"], l * 4 + 1)
            nc.vector.tensor_tensor(cg1_lo[:, :], fold_cg1[:, :], cg1_hi[:, :].bitcast(F32),
                                    ALU.subtract).then_inc(s["ffnw_split"], 1)
            dve.wait_ge(s["ffnw_split"], l * 4 + 2)
            nc.vector.tensor_tensor(w2_lo[:, :, :], w2_c[:, :, :], w2_hi[:, :, :].bitcast(F32),
                                    ALU.subtract).then_inc(s["ffnw_split"], 1)

        def dve_fold_c1(dve, l, wait_free):
            dve.wait_ge(s["attb_ready"], l * 5 + 5)
            if wait_free:
                dve.wait_ge(s["gelu"], l * SEQS * FC)
            nc.vector.tensor_tensor(c1_f[:, :], colb[:, 1:1 + FC], lv_f[:, V_C1:V_C1 + FC],
                                    ALU.add).then_inc(s["c1_ready"], 1)

        def dve_fold_cb2(dve, l, wait_free):
            if wait_free:
                dve.wait_ge(s["hc2_s"], l * SEQS)
            nc.vector.tensor_copy(cb2[:, :], colb[:, 1 + FC:2 + FC]).then_inc(s["cb2_ready"], 1)

        def pe_fold_biases(pe, l, wait_free):
            pe.wait_ge(s["raw_loaded"], l * LOADS + LOADS)
            pe.wait_ge(s["att_fold"], l * ATT_STEPS + 5)
            if wait_free:
                pe.wait_ge(s["kvo_sb"], l * SEQS - 1)
            nc.tensor.matmul(COLB[:, 0:1], raw_att[:, 0, :], lv_a[:, V_BE2P:V_BE2P + 1], start=True, stop=True)
            nc.tensor.matmul(COLB[:, 1:2], centre[:, :], bo_be2[:, :], start=True, stop=True)
            nc.tensor.matmul(BIAS, be2_bc[:, :], raw_att[:, 1:3, :], start=True, stop=False)
            nc.tensor.matmul(BIAS, ones[0:1, :], raw_bkv[0:1, :], start=False, stop=True).then_inc(s["attb_ps"], 1)
            pe.wait_ge(s["ffn_fold"], l * FFN_STEPS + 3)
            for j in range(FC):
                nc.tensor.matmul(COLB[:, 2 + j:3 + j], raw_w1[:, j * P:(j + 1) * P], lv_f[:, V_BE1:V_BE1 + 1],
                                 start=True, stop=True)
            nc.tensor.matmul(COLB[:, 2 + FC:3 + FC], centre[:, :], c2_be1[:, :],
                             start=True, stop=True).then_inc(s["ffnb_ps"], 1)

        e_in = [sem(f"e_in{i}") for i in range(2)]
        wr_sb = sb("wr_sb", [P, E])
        br_bc = sb("br_bc", [SEQS, E])
        expert_i = sb("expert_i", [SEQS, 1], I32)
        ew_down = sb("ew_down", [P, 2, HID])
        eb_down = sb("eb_down", [HID, 2])
        ew_up = sb("ew_up", [HID, 2, D])
        eb_up = sb("eb_up", [P, 2, D])
        st = sb("st", [P, SEQS * TT, 6])
        mv = sb("mv", [P, SEQS * TT, 2])
        std_x = sb("std_x", [P, SEQS * TT])
        r_x = sb("r_x", [P, SEQS * TT])
        r_f = sb("r_f", [P, SEQS * TT])
        t_x = sb("t_x", [P, SEQS * TT])
        xn_tm = hid[:, 2:4, :]
        zf_tm = hid[:, 0:2, :]
        zf_fm = gate_tm[:, :, :, :].rearrange("p b s d -> p b (s d)")
        zf_sum = sb("zf_sum", [P, SEQS])
        bn_v = sb("bn_v", [P, 2])
        z_bn = sb("z_bn", [P, SEQS])
        lg = sb("lg", [SEQS, E])
        lg_e = sb("lg_e", [SEQS, E])
        r_cols = sb("r_cols", [SEQS, 6])
        gate_d = sb("gate_d", [SEQS, SEQS])
        gate_bc = sb("gate_bc", [P, SEQS])
        e_hid = sb("e_hid", [HID, 2, S])
        e_y = sb("e_y", [P, 2, S])

        with nc.Block() as block:
            @block.sync
            def _(sp):
                for i in range(4):
                    sp.dma_start(x_tm[:, 2 * i:2 * i + 2, :, :], x_dram[:, 2 * i:2 * i + 2]).then_inc(x_in[i], 16)
                for i, v in enumerate((bq, bo, g1, be1, g2, be2, c2)):
                    sp.dma_start(vec_rows[i * L:(i + 1) * L, :], v).then_inc(s["vec_in"], 16)
                sp.dma_start(vec_rows[R_C1:R_C1 + FC * L, :],
                             c1.rearrange("l (j p) -> (l j) p", p=P)).then_inc(s["vec_in"], 16)
                for i, v in enumerate((ln_g, ln_b, bn_g, bn_b, bn_mean, bn_var)):
                    sp.dma_start(vec_rows[R_FFN + i:R_FFN + i + 1, :],
                                 v.rearrange("(a n) -> a n", a=1)).then_inc(s["vec_in"], 16)
                sp.dma_start(wr_sb[:, :], Wr).then_inc(s["row_in"], 16)
                sp.dma_start(br_bc[:, :], br.rearrange("(a n) -> a n", a=1).to_broadcast([SEQS, E])).then_inc(s["row_in"], 16)
                sp.dma_start(gf_bc[:, :], gf.rearrange("(a n) -> a n", a=1).to_broadcast([P, D])).then_inc(s["row_in"], 16)
                sp.dma_start(bef_bc[:, :], bef.rearrange("(a n) -> a n", a=1).to_broadcast([P, D])).then_inc(s["row_in"], 16)
                load_layer(sp, 0)
                sp.wait_ge(s["routed"], 1)
                for b in range(SEQS):
                    e = sp.value_load(expert_i[b:b + 1, 0:1], min_val=0, max_val=E - 1)
                    if b >= 2:
                        sp.wait_ge(s["ey"], b - 1)
                    sp.dma_start(ew_down[:, b % 2, :], W_down[bass.ds(e, 1)].rearrange("a d h -> d (a h)")).then_inc(e_in[b % 2], 16)
                    sp.dma_start(eb_down[:, b % 2:b % 2 + 1], b_down[bass.ds(e, 1)].rearrange("a h -> h a")).then_inc(e_in[b % 2], 16)
                    sp.dma_start(ew_up[:, b % 2, :], W_up[bass.ds(e, 1)].rearrange("a h d -> h (a d)")).then_inc(e_in[b % 2], 16)
                    sp.dma_start(eb_up[:, b % 2, :], b_up[bass.ds(e, 1)].to_broadcast([P, D])).then_inc(e_in[b % 2], 16)

            @block.gpsimd
            def _(pool):
                c = s["const_ready"]
                nc.gpsimd.memset(ident[:, :], 0.0).then_inc(c, 1)
                nc.gpsimd.memset(ones[:, :], 1.0).then_inc(c, 1)
                nc.gpsimd.memset(mean_f32[:, :], 1.0 / D).then_inc(c, 1)
                nc.gpsimd.memset(eps_col[:, :], EPS).then_inc(c, 1)
                nc.gpsimd.memset(neg1_col[:, :], -1.0).then_inc(c, 1)
                nc.gpsimd.memset(den_eps_col[:, :], DEN_EPS).then_inc(c, 1)
                nc.gpsimd.iota(expert_m8[:, :], pattern=[[1, E]], base=-E, channel_multiplier=0,
                               allow_small_or_imprecise_dtypes=True).then_inc(c, 1)
                pool.wait_ge(c, 7)
                nc.gpsimd.affine_select(out=ident[:, :], in_=ident[:, :], pattern=[[-1, P]], compare_op=ALU.not_equal,
                                        fill=1.0, base=0, channel_multiplier=1).then_inc(c, 1)
                nc.gpsimd.affine_select(out=head_mask[:, :], in_=ones[:, :], pattern=[[-DH, D // DH], [0, DH]],
                                        compare_op=ALU.is_ge, fill=0.0, base=0, channel_multiplier=1).then_inc(c, 1)
                pool.wait_ge(c, 9)
                nc.gpsimd.affine_select(out=head_mask[:, :], in_=head_mask[:, :], pattern=[[DH, D // DH], [0, DH]],
                                        compare_op=ALU.is_ge, fill=0.0, base=DH - 1, channel_multiplier=-1).then_inc(c, 1)
                nc.gpsimd.tensor_tensor(centre[:, :], ident[:, :], mean_f32[:, :], ALU.subtract).then_inc(c, 1)
                nc.gpsimd.memset(kv1[:, :, 2 * D:2 * D + 1], 1.0).then_inc(c, 1)
                nc.gpsimd.tensor_copy(mean_mat[:, :], mean_f32[:, :]).then_inc(c, 1)

            @block.scalar
            def _(act):
                act.wait_ge(s["const_ready"], 13)
                act.wait_ge(s["stats"], SEQS * TT)
                nc.scalar.activation(std_x[:, :], mv[:, :, 1], ACT.Sqrt, bias=eps_col[:, :]).then_inc(s["rstd_x"], 1)
                act.wait_ge(s["stats"], SEQS * TT + 2)
                nc.scalar.activation(t_x[:, :], t_x[:, :], ACT.Sqrt, bias=eps_col[:, :]).then_inc(s["rstd_x"], 1)
                act.wait_ge(s["cols_ready"], 1)
                nc.scalar.activation(bn_v[:, 0:1], cols[:, R_FFN + 5:R_FFN + 6], ACT.Sqrt, bias=eps_col[:, :]).then_inc(s["rstd_x"], 1)
                for b in range(SEQS):
                    act.wait_ge(s["zin_ps"], b + 1)
                    nc.scalar.activation(z_hi[:, b, :], kv_ps[b % 2][:, :, :], ACT.Identity).then_inc(s["zin_hi"], 1)
                    act.wait_ge(s["zff_ps"], b + 1)
                    nc.scalar.activation(zf_fm[:, b, :], up_ps[b % 2][:, :], ACT.Identity,
                                         scale=cols[:, R_FFN:R_FFN + 1], bias=cols[:, R_FFN + 1:R_FFN + 2],
                                         accum_out=zf_sum[:, b:b + 1]).then_inc(s["zff"], 1)
                act.wait_ge(s["logit"], 3)
                nc.scalar.activation(lg_e[:, :], lg[:, :], ACT.Exp, bias=r_cols[:, 0:1],
                                     accum_out=r_cols[:, 1:2]).then_inc(s["softmax_e"], 1)
                act.wait_ge(s["gate_bc_r"], 1)
                for b in range(SEQS):
                    act.wait_ge(s["eh_ps"], b + 1)
                    act.wait_ge(e_in[b % 2], 64 * (b // 2 + 1))
                    nc.scalar.activation(e_hid[:, b % 2, :], q_ps[0:HID, :] if b % 2 else att_ps[0:HID, :], ACT.Relu,
                                         bias=eb_down[:, b % 2:b % 2 + 1]).then_inc(s["eh"], 1)
                    act.wait_ge(s["ey"], b + 1)
                    nc.scalar.activation(gate_tm[:, b, :, :], e_y[:, b % 2, :], ACT.Silu,
                                         scale=gate_bc[:, b:b + 1]).then_inc(s["gated"], 1)

            @block.tensor
            def _(pe):
                pe.wait_ge(s["const_ready"], 13)
                pe.wait_ge(s["vec_in"], 14 * 16)
                nc.tensor.transpose(small_ps[:, 0:NVEC], vec_rows[0:NVEC, :], ident[0:NVEC, 0:NVEC]).then_inc(s["tr_ps"], 1)
                for b in range(SEQS):
                    pe.wait_ge(s["xn"], 8 * b + 8)
                    if b >= 2:
                        pe.wait_ge(s["state"], b - 1)
                    for t in range(TT):
                        last = nc.tensor.transpose(kv_ps[b % 2][:, t // 2, (t % 2) * P:(t % 2 + 1) * P],
                                                   xn_tm[:, b % 2, t * D:(t + 1) * D], ident[:, :])
                    last.then_inc(s["zin_ps"], 1)
                    if b >= 2:
                        pe.wait_ge(s["zff"], b - 1)
                    for t in range(TT):
                        last = nc.tensor.transpose(up_ps[b % 2][:, t * P:(t + 1) * P],
                                                   zf_tm[:, b % 2, t * D:(t + 1) * D], ident[:, :])
                    last.then_inc(s["zff_ps"], 1)
                pe.wait_ge(s["bn_chain"], 4)
                pe.wait_ge(s["row_in"], 64)
                nc.tensor.matmul(down_ps[0:SEQS, 0:E], z_bn[:, :], wr_sb[:, :], start=True, stop=True).then_inc(s["logit_ps"], 1)
                pe.wait_ge(s["cols_ready"], 1)
                pe_fold_biases(pe, 0, False)
                pe.wait_ge(s["pmax_r"], 3)
                nc.tensor.matmul(down_ps[:, 0:SEQS], ones[0:SEQS, :], gate_d[:, :], start=True, stop=True).then_inc(s["gate_ps"], 1)
                pe.wait_ge(s["gate_bc_r"], 1)
                for b in range(SEQS):
                    hp = q_ps if b % 2 else att_ps
                    pe.wait_ge(e_in[b % 2], 64 * (b // 2 + 1))
                    nc.tensor.matmul(hp[0:HID, :], ew_down[:, b % 2, :], zf_fm[:, b, :], start=True, stop=True).then_inc(s["eh_ps"], 1)
                    pe.wait_ge(s["eh"], b + 1)
                    if b >= 2:
                        pe.wait_ge(s["ey"], b - 1)
                    for t in range(TT):
                        last = nc.tensor.matmul(up_ps[b % 2][:, t * P:(t + 1) * P], e_hid[:, b % 2, t * P:(t + 1) * P],
                                                ew_up[:, b % 2, :], start=True, stop=True)
                    last.then_inc(s["ey_ps"], 1)

            @block.vector
            def _(dve):
                for b in range(SEQS):
                    if b % 2 == 0:
                        dve.wait_ge(x_in[b // 2], 16)
                    for t in range(TT):
                        nc.vector.bn_stats(st[:, b * TT + t, :], x_tm[:, b, t, :]).then_inc(s["fstat"], 1)
                for i in range(SEQS * TT):
                    dve.wait_ge(s["fstat"], i + 1)
                    nc.vector.bn_aggr(mv[:, i, :], st[:, i, :]).then_inc(s["stats"], 1)
                dve.wait_ge(s["rstd_x"], 1)
                nc.vector.reciprocal(r_x[:, :], std_x[:, :]).then_inc(s["stats"], 1)
                dve.wait_ge(s["stats"], SEQS * TT + 1)
                nc.vector.tensor_tensor(t_x[:, :], r_x[:, :], r_x[:, :], ALU.mult).then_inc(s["fstd"], 1)
                dve.wait_ge(s["fstd"], 1)
                nc.vector.tensor_tensor(t_x[:, :], t_x[:, :], mv[:, :, 1], ALU.mult).then_inc(s["stats"], 1)
                dve.wait_ge(s["rstd_x"], 2)
                nc.vector.reciprocal(t_x[:, :], t_x[:, :]).then_inc(s["fstd"], 1)
                dve.wait_ge(s["fstd"], 2)
                nc.vector.tensor_tensor(r_f[:, :], t_x[:, :], r_x[:, :], ALU.mult).then_inc(s["fstd"], 1)
                dve.wait_ge(s["fstd"], 3)
                dve.wait_ge(s["tr_ps"], 1)
                nc.vector.tensor_copy(cols[:, :], small_ps[:, 0:NVEC]).then_inc(s["cols_ready"], 1)
                dve.wait_ge(s["cols_ready"], 1)
                nc.vector.tensor_copy(layer_vecs[:, 0:L, V_BQ:V_BE1 + 1],
                                      cols[:, 0:4 * L].rearrange("p (v l) -> p l v", l=L)).then_inc(s["lv_ready"], 1)
                nc.vector.tensor_copy(layer_vecs[:, 1:L + 1, V_G2P:V_BE2P + 1],
                                      cols[:, 4 * L:6 * L].rearrange("p (v l) -> p l v", l=L)).then_inc(s["lv_ready"], 1)
                nc.vector.tensor_copy(layer_vecs[:, 0:L, V_C2:V_C2 + 1],
                                      cols[:, 6 * L:7 * L].rearrange("p (v l) -> p l v", l=L)).then_inc(s["lv_ready"], 1)
                nc.vector.tensor_copy(layer_vecs[:, 0:L, V_C1:V_C1 + FC],
                                      cols[:, R_C1:R_C1 + FC * L].rearrange("p (l j) -> p l j", l=L)).then_inc(s["lv_ready"], 1)
                nc.vector.memset(layer_vecs[:, 0, V_G2P:V_G2P + 1], 1.0).then_inc(s["lv_ready"], 1)
                nc.vector.memset(layer_vecs[:, 0, V_BE2P:V_BE2P + 1], 0.0).then_inc(s["lv_ready"], 1)
                dve.wait_ge(s["lv_ready"], 6)
                dve_fold_att_first(dve, 0, False)
                dve_fold_wo(dve, 0, False)
                dve_split_wqkv(dve, 0, False)
                dve_split_cg2(dve, 0, False)
                dve_fold_ffn_first(dve, 0, False)
                dve_split_w1(dve, 0, False)
                dve_split_ffn(dve, 0, False)
                for b in range(SEQS):
                    if b >= 2:
                        dve.wait_ge(s["zff_ps"], b - 1)
                    for t in range(TT):
                        i = b * TT + t
                        nc.vector.tensor_scalar(xn_tm[:, b % 2, t * D:(t + 1) * D], x_tm[:, b, t, :], mv[:, i, 0:1],
                                                r_x[:, i:i + 1], ALU.subtract, ALU.mult).then_inc(s["xn"], 1)
                        nc.vector.tensor_scalar(zf_tm[:, b % 2, t * D:(t + 1) * D], x_tm[:, b, t, :], mv[:, i, 0:1],
                                                r_f[:, i:i + 1], ALU.subtract, ALU.mult).then_inc(s["xn"], 1)
                    if b >= 1:
                        c = b - 1
                        dve.wait_ge(s["zin_hi"], c + 1)
                        nc.vector.tensor_tensor(z_lo[:, c, :], kv_ps[c % 2][:, :, :], z_hi[:, c, :].bitcast(F32),
                                                ALU.subtract).then_inc(s["state"], 1)
                c = SEQS - 1
                dve.wait_ge(s["zin_hi"], c + 1)
                nc.vector.tensor_tensor(z_lo[:, c, :], kv_ps[c % 2][:, :, :], z_hi[:, c, :].bitcast(F32),
                                        ALU.subtract).then_inc(s["state"], 1)
                ch = s["bn_chain"]
                dve.wait_ge(s["rstd_x"], 3)
                nc.vector.reciprocal(bn_v[:, 1:2], bn_v[:, 0:1]).then_inc(ch, 1)
                dve.wait_ge(ch, 1)
                dve.wait_ge(s["zff"], SEQS)
                nc.vector.tensor_scalar(z_bn[:, :], zf_sum[:, :], 1.0 / S, None, ALU.mult).then_inc(ch, 1)
                dve.wait_ge(ch, 2)
                nc.vector.tensor_scalar(z_bn[:, :], z_bn[:, :], cols[:, R_FFN + 4:R_FFN + 5], bn_v[:, 1:2],
                                        ALU.subtract, ALU.mult).then_inc(ch, 1)
                dve.wait_ge(ch, 3)
                nc.vector.tensor_scalar(z_bn[:, :], z_bn[:, :], cols[:, R_FFN + 2:R_FFN + 3],
                                        cols[:, R_FFN + 3:R_FFN + 4], ALU.mult, ALU.add).then_inc(ch, 1)
                lgs = s["logit"]
                dve.wait_ge(s["logit_ps"], 1)
                nc.vector.tensor_tensor(lg[:, :], down_ps[0:SEQS, 0:E], br_bc[:, :], ALU.add).then_inc(lgs, 1)
                dve.wait_ge(lgs, 1)
                nc.vector.reduce_max(r_cols[:, 2:3], lg[:, :], AX.X).then_inc(lgs, 1)
                dve.wait_ge(lgs, 2)
                nc.vector.tensor_scalar(r_cols[:, 0:1], r_cols[:, 2:3], -1.0, None, ALU.mult).then_inc(lgs, 1)
                dve.wait_ge(s["softmax_e"], 1)
                nc.vector.reciprocal(r_cols[:, 3:4], r_cols[:, 1:2]).then_inc(lgs, 1)
                dve.wait_ge(lgs, 4)
                nc.vector.tensor_scalar(lg_e[:, :], lg_e[:, :], r_cols[:, 3:4], None, ALU.mult).then_inc(lgs, 1)
                dve.wait_ge(lgs, 5)
                pm = s["pmax_r"]
                nc.vector.reduce_max(r_cols[:, 4:5], lg_e[:, :], AX.X).then_inc(pm, 1)
                dve.wait_ge(pm, 1)
                nc.vector.tensor_scalar(gate_d[:, :], ident[0:SEQS, 0:SEQS], r_cols[:, 4:5], None, ALU.mult).then_inc(pm, 2)
                nc.vector.tensor_scalar(lg[:, :], lg_e[:, :], r_cols[:, 4:5], None, ALU.is_equal).then_inc(lgs, 1)
                dve.wait_ge(lgs, 6)
                nc.vector.tensor_tensor(lg[:, :], lg[:, :], expert_m8[:, :], ALU.mult).then_inc(lgs, 1)
                dve.wait_ge(lgs, 7)
                nc.vector.tensor_reduce(r_cols[:, 5:6], lg[:, :], AX.X, ALU.min).then_inc(lgs, 1)
                dve.wait_ge(lgs, 8)
                nc.vector.tensor_scalar(expert_i[:, :], r_cols[:, 5:6], float(E), None, ALU.add).then_inc(s["routed"], 1)
                dve_fold_att_biases(dve, 0, False)
                dve.wait_ge(s["attb_ready"], 5)
                nc.vector.tensor_copy(cb1[:, :], colb[:, 0:1]).then_inc(s["cb1_ready"], 1)
                dve_fold_c1(dve, 0, False)
                dve_fold_cb2(dve, 0, False)
                dve.wait_ge(s["gate_ps"], 1)
                nc.vector.tensor_copy(gate_bc[:, :], down_ps[:, 0:SEQS]).then_inc(s["gate_bc_r"], 1)
                for b in range(SEQS):
                    dve.wait_ge(s["ey_ps"], b + 1)
                    dve.wait_ge(e_in[b % 2], 64 * (b // 2 + 1))
                    if b >= 2:
                        dve.wait_ge(s["gated"], b - 1)
                    nc.vector.tensor_tensor(e_y[:, b % 2, :].rearrange("p (t d) -> p t d", d=D),
                                            up_ps[b % 2][:, :].rearrange("p (t d) -> p t d", d=D),
                                            eb_up[:, b % 2, :].unsqueeze(1).to_broadcast([P, TT, D]),
                                            ALU.add).then_inc(s["ey"], 1)

        def three_pass(dst, w_hi, w_lo, a_hi, a_lo, start, stop):
            nc.tensor.matmul(dst, w_hi, a_hi, start=start, stop=False)
            nc.tensor.matmul(dst, w_lo, a_hi, start=False, stop=False)
            return nc.tensor.matmul(dst, w_hi, a_lo, start=False, stop=stop)

        def is_unit(u):
            return not isinstance(u, int) or 0 <= u < UNITS

        def after_first(u):
            return not isinstance(u, int) or u > 0

        def is_layer(l):
            return not isinstance(l, int) or l < L

        def pe_kv(pe, u, b, half):
            if half == 0:
                pe.wait_ge(s["state"], u + 1)
                if after_first(u):
                    pe.wait_ge(s["kv_biased"], u * 2)
            for t in (2 * half, 2 * half + 1):
                a_hi, a_lo = z_hi[:, b, t * P:(t + 1) * P], z_lo[:, b, t * P:(t + 1) * P]
                dst = kv_ps[half][:, t % 2, :]
                nc.tensor.matmul(dst, a_hi, wqkv_hi[:, D:3 * D], start=True, stop=False)
                nc.tensor.matmul(dst, a_hi, wqkv_lo[:, D:3 * D], start=False, stop=False)
                last = nc.tensor.matmul(dst, a_lo, wqkv_hi[:, D:3 * D], start=False, stop=True)
            last.then_inc(s["kvproj"], 1)

        def pe_q(pe, u, b):
            if after_first(u):
                pe.wait_ge(s["qphi"], u)
            three_pass(q_ps[:, :], wqkv_hi[:, 0:D], wqkv_lo[:, 0:D], z_hi[:, b, :], z_lo[:, b, :],
                       True, True).then_inc(s["qproj"], 1)

        def pe_kv_ksum(pe, u, half):
            if half == 0:
                pe.wait_ge(s["kphi"], u + 1)
                if after_first(u):
                    pe.wait_ge(s["kvo_sb"], u)
            for t in (2 * half, 2 * half + 1):
                last = nc.tensor.matmul(KV_KSUM, k_phi[:, t, :], kv1[:, t, D:2 * D + 1], start=(t == 0), stop=(t == TT - 1))
            if half == 1:
                last.then_inc(s["kv_ps"], 1)

        def pe_kv_transpose(pe, u):
            pe.wait_ge(s["kvblk"], u + 1)
            nc.tensor.transpose(KVT, kv_blk[:, :], ident[:, :]).then_inc(s["kvt_ps"], 1)

        def pe_kvo_den(pe, u):
            pe.wait_ge(s["kvt_sb"], u + 1)
            nc.tensor.matmul(KVO, kvT_blk[:, :], wo_c[:, :], start=True, stop=True).then_inc(s["kvo_ps"], 1)
            pe.wait_ge(s["qphi"], u + 1)
            if is_unit(u - 1):
                pe.wait_ge(s["lnv1_s"], u)
            nc.tensor.matmul(up_ps[1][:, :], ksum_blk[:, :], q_phi[:, :], start=True, stop=True).then_inc(s["den_ps"], 1)

        def pe_att(pe, u, b):
            if after_first(u):
                pe.wait_ge(s["z1_s"], u)
            three_pass(att_ps[:, :], cg2_hi[:, :], cg2_lo[:, :], z_hi[:, b, :], z_lo[:, b, :], True, False)
            pe.wait_ge(s["kvo_sb"], u + 1)
            pe.wait_ge(s["qn"], u + 1)
            nc.tensor.matmul(att_ps[:, :], kvo[:, :], q_n[:, :], start=False, stop=True).then_inc(s["att_done"], 1)

        def pe_var2(pe, u):
            if is_unit(u + 1):
                pe.wait_ge(s["gelu"], (u + 2) * FC - 1)
            pe.wait_ge(s["sq2lo_s"], u + 1)
            nc.tensor.matmul(up_ps[0][:, :], mean_mat[:, :], sq2_hi[:, :], start=True, stop=False)
            nc.tensor.matmul(up_ps[0][:, :], mean_mat[:, :], sq2_lo[:, :], start=False, stop=True).then_inc(s["var2"], 1)

        def pe_var1(pe, u):
            if is_unit(u - 1):
                pe.wait_ge(s["gelu"], u * FC)
            pe.wait_ge(s["sq1lo_s"], u + 1)
            nc.tensor.matmul(up_ps[1][:, :], mean_mat[:, :], sq1_hi[:, :], start=True, stop=False)
            nc.tensor.matmul(up_ps[1][:, :], mean_mat[:, :], sq1_lo[:, :], start=False, stop=True).then_inc(s["var1"], 1)

        def pe_up(pe, u, b, chunks):
            if chunks[0] == 0:
                pe.wait_ge(s["z1lo_s"], u + 1)
                if is_unit(u + 1):
                    pe.wait_ge(s["den_sb"], u + 2)
                else:
                    pe.wait_ge(s["lnv1_s"], u + 1)
                if is_unit(u - 2):
                    pe.wait_ge(s["lnv2_s"], u - 1)
            for j in chunks:
                if j >= 2:
                    pe.wait_ge(s["gelu"], u * FC + j - 1)
                three_pass(up_ps[j % 2][:, :], w1_hi[:, j * P:(j + 1) * P], w1_lo[:, j * P:(j + 1) * P],
                           z1_hi[:, b % 2, :], z1_lo[:, b % 2, :], True, True).then_inc(s["up"], 1)

        def pe_down(pe, u, b):
            if after_first(u):
                pe.wait_ge(s["hc2_s"], u)
            three_pass(down_ps[:, :], cg1_hi[:, :], cg1_lo[:, :], z1_hi[:, b % 2, :], z1_lo[:, b % 2, :], True, False)
            for j in range(FC):
                pe.wait_ge(s["hid_lo_s"], u * FC + j + 1)
                last = three_pass(down_ps[:, :], w2_hi[:, j, :], w2_lo[:, j, :], hid_hi[:, j, :], hid_lo[:, j, :],
                                  False, j == FC - 1)
            last.then_inc(s["down"], 1)

        def pe_period(pe, l, b):
            p = l * SEQS + b
            att, ffn, ln1, ln2, proj = is_unit(p), is_unit(p - 2), is_unit(p - 1), is_unit(p - 3), is_unit(p + 1)
            if ffn:
                if b == 2:
                    pe.wait_ge(s["w1_split"], l * 2 + 2)
                pe_up(pe, p - 2, b, (0, 1))
            if att:
                if b == SEQS - 1 and is_layer(l + 1):
                    pe.wait_ge(s["attb_ready"], l * 5 + 10)
                pe_kv_ksum(pe, p, 0)
            if ffn:
                pe_up(pe, p - 2, b, (2, 3))
            if att:
                pe_kv_ksum(pe, p, 1)
            if proj:
                if b == SEQS - 1:
                    pe.wait_ge(s["wqkv_split"], l * 2 + 4)
                pe_kv(pe, p + 1, (b + 1) % SEQS, 0)
            if att:
                pe_kv_transpose(pe, p)
            if ln2:
                pe_var2(pe, p - 3)
            if ln1:
                pe_var1(pe, p - 1)
            if proj:
                pe_kv(pe, p + 1, (b + 1) % SEQS, 1)
                pe_q(pe, p + 1, (b + 1) % SEQS)
            if att:
                if b == 0:
                    pe.wait_ge(s["wo_ready"], l + 1)
                pe_kvo_den(pe, p)
            if ffn:
                if b == 2:
                    pe.wait_ge(s["ffnw_split"], l * 4 + 4)
                pe_down(pe, p - 2, b)
            if att:
                if b == 0:
                    pe.wait_ge(s["cg2_split"], l * 2 + 2)
                pe_att(pe, p, b)
            if b == SEQS - 2 and is_layer(l + 1):
                pe_fold_biases(pe, l + 1, True)

        def act_period(act, l, b):
            p = l * SEQS + b
            att, ffn, ln1, ln2, proj = is_unit(p), is_unit(p - 2), is_unit(p - 1), is_unit(p - 3), is_unit(p + 1)
            u, v = p - 2, p - 3
            if ffn:
                if b == 2:
                    act.wait_ge(s["c1_ready"], l + 1)
                for j in range(FC):
                    act.wait_ge(s["up"], u * FC + j + 1)
                    if after_first(u):
                        act.wait_ge(s["hid_lo_s"], (u - 1) * FC + j + 1)
                    nc.scalar.activation(hid[:, j, :], up_ps[j % 2][:, :], ACT.Gelu,
                                         bias=c1_f[:, j:j + 1]).then_inc(s["gelu"], 1)
            nc.scalar.preload_act_table_set("natural_log_exp_and_others")
            if ln2:
                act.wait_ge(s["var2"], v + 1)
                nc.scalar.activation(lnv2[:, :], up_ps[0][:, :], ACT.Ln, bias=eps_col[:, :]).then_inc(s["lnv2_s"], 1)
            if ln1:
                act.wait_ge(s["var1"], p)
                nc.scalar.activation(lnv1[:, :], up_ps[1][:, :], ACT.Ln, bias=eps_col[:, :]).then_inc(s["lnv1_s"], 1)
            if ln2:
                act.wait_ge(s["lnv2_s"], v + 1)
                if after_first(v):
                    act.wait_ge(s["z2_s"], v)
                nc.scalar.activation(rstd2[:, :], lnv2[:, :], ACT.Exp, scale=-0.5).then_inc(s["rstd2_s"], 1)
            if ln1:
                act.wait_ge(s["lnv1_s"], p)
                if after_first(p - 1):
                    act.wait_ge(s["z1_s"], p - 1)
                nc.scalar.activation(rstd1[:, :], lnv1[:, :], ACT.Exp, scale=-0.5).then_inc(s["rstd1_s"], 1)
            if att:
                act.wait_ge(s["den_ps"], p + 1)
                nc.scalar.activation(den[:, :], up_ps[1][:, :], ACT.Ln, bias=den_eps_col[:, :]).then_inc(s["den_sb"], 1)
                act.wait_ge(s["den_sb"], p + 1)
                if after_first(p):
                    act.wait_ge(s["qn"], p)
                nc.scalar.activation(rden[:, :], den[:, :], ACT.Exp, scale=-1.0).then_inc(s["rden_s"], 1)
            if proj:
                act.wait_ge(s["kmin"], p + 2)
                if after_first(p + 1):
                    act.wait_ge(s["kphi"], p + 1)
                nc.scalar.activation(k_exp[:, :, :], k_min[:, :, :], ACT.Exp, bias=neg1_col[:, :]).then_inc(s["kexp"], 1)
                act.wait_ge(s["qmin"], p + 2)
                if after_first(p + 1):
                    act.wait_ge(s["qphi"], p + 1)
                nc.scalar.activation(q_exp[:, :], q_min[:, :], ACT.Exp).then_inc(s["qexp"], 1)
            nc.scalar.preload_act_table_set("gelu_and_others")
            if ffn:
                act.wait_ge(s["down"], u + 1)
                if b == 2:
                    act.wait_ge(s["cb2_ready"], l + 1)
                if after_first(u):
                    act.wait_ge(s["z2_s"], u)
                nc.scalar.activation(hc2[:, :], down_ps[:, :], ACT.Identity, bias=cb2[:, :]).then_inc(s["hc2_s"], 1)
            if att:
                act.wait_ge(s["att_done"], p + 1)
                if b == 0:
                    act.wait_ge(s["cb1_ready"], l + 1)
                if after_first(p):
                    act.wait_ge(s["sq1lo_s"], p)
                nc.scalar.activation(sq1[:, :], att_ps[:, :], ACT.Square, bias=cb1[:, :]).then_inc(s["sq1_s"], 1)

        def dve_kv_bias(dve, u):
            if after_first(u):
                dve.wait_ge(s["kv_ps"], u)
            for i in range(2):
                dve.wait_ge(s["kvproj"], u * 2 + i + 1)
                nc.vector.tensor_tensor(kv1[:, 2 * i:2 * i + 2, 0:2 * D], kv_ps[i][:, :, :],
                                        bkv1_bc[:, :].unsqueeze(1).to_broadcast([P, 2, 2 * D]),
                                        ALU.add).then_inc(s["kv_biased"], 1)

        def dve_k_min(dve, u):
            if after_first(u):
                dve.wait_ge(s["kexp"], u)
            dve.wait_ge(s["kv_biased"], u * 2 + 2)
            nc.vector.tensor_scalar(k_min[:, :, :], kv1[:, :, 0:D], 1.0, None, ALU.min).then_inc(s["kmin"], 1)

        def dve_q_min(dve, u):
            dve.wait_ge(s["qproj"], u + 1)
            if after_first(u):
                dve.wait_ge(s["qexp"], u)
            nc.vector.tensor_scalar(q_min[:, :], q_ps[:, :], bq_f[:, 0:1], 0.0, ALU.add, ALU.min).then_inc(s["qmin"], 1)

        def dve_k_phi(dve, u, between=None):
            dve.wait_ge(s["kexp"], u + 1)
            nc.vector.tensor_scalar(k_exp[:, :, :], k_exp[:, :, :], -1.0, 1.0, ALU.add, ALU.add).then_inc(s["kexpm1"], 1)
            if between:
                between()
            dve.wait_ge(s["kexpm1"], u + 1)
            nc.vector.tensor_tensor(k_phi[:, :, :], k_exp[:, :, :], kv1[:, :, 0:D], ALU.max).then_inc(s["kphi"], 1)

        def dve_q_phi(dve, u):
            dve.wait_ge(s["qexp"], u + 1)
            nc.vector.tensor_scalar(q_exp[:, :], q_exp[:, :], -1.0, 1.0, ALU.add, ALU.add).then_inc(s["qexpm1"], 1)
            dve.wait_ge(s["qexpm1"], u + 1)
            if after_first(u):
                dve.wait_ge(s["qn"], u)
            nc.vector.scalar_tensor_tensor(q_phi[:, :], q_ps[:, :], bq_f[:, 1:2], q_exp[:, :],
                                           ALU.add, ALU.max).then_inc(s["qphi"], 1)

        def dve_blocks(dve, u):
            dve.wait_ge(s["kv_ps"], u + 1)
            if after_first(u):
                dve.wait_ge(s["den_ps"], u)
            nc.vector.tensor_scalar(ksum_blk[:, :], head_mask[:, :], KV_KSUM[:, D:D + 1], None, ALU.mult).then_inc(s["ksumblk"], 1)
            nc.vector.tensor_tensor(kv_blk[:, :], KV_KSUM[:, 0:D], head_mask[:, :], ALU.mult).then_inc(s["kvblk"], 1)

        def dve_hid_hi(dve, u, chunks):
            for j in chunks:
                dve.wait_ge(s["gelu"], u * FC + j + 1)
                nc.vector.tensor_copy(hid_hi[:, j, :], hid[:, j, :]).then_inc(s["hid_hi_s"], 1)

        def dve_kvt(dve, u):
            dve.wait_ge(s["kvt_ps"], u + 1)
            if after_first(u):
                dve.wait_ge(s["kvo_ps"], u)
            nc.vector.tensor_copy(kvT_blk[:, :], KVT).then_inc(s["kvt_sb"], 1)

        def dve_kvo(dve, u):
            dve.wait_ge(s["kvo_ps"], u + 1)
            if after_first(u):
                dve.wait_ge(s["att_done"], u)
            nc.vector.tensor_copy(kvo[:, :], KVO).then_inc(s["kvo_sb"], 1)

        def dve_period(dve, l, b):
            p = l * SEQS + b
            att, ffn, ln1, ln2, proj = is_unit(p), is_unit(p - 2), is_unit(p - 1), is_unit(p - 3), is_unit(p + 1)
            u, v = p - 2, p - 3
            fold = is_layer(l + 1)
            folded = not isinstance(l, int) or 0 < l < L
            if ln2:
                dve.wait_ge(s["sq2_s"], v + 1)
                if after_first(v):
                    dve.wait_ge(s["var2"], v)
                nc.vector.tensor_copy(sq2_hi[:, :], sq2[:, :]).then_inc(s["sq2hi_s"], 1)
            if ln1:
                dve.wait_ge(s["sq1_s"], p)
                if after_first(p - 1):
                    dve.wait_ge(s["var1"], p - 1)
                nc.vector.tensor_copy(sq1_hi[:, :], sq1[:, :]).then_inc(s["sq1hi_s"], 1)
                dve.wait_ge(s["sq1hi_s"], p)
                nc.vector.tensor_tensor(sq1_lo[:, :], sq1[:, :], sq1_hi[:, :].bitcast(F32),
                                        ALU.subtract).then_inc(s["sq1lo_s"], 1)
            if b == 0 and folded:
                dve_split_cg2(dve, l, True)
            if b == 2 and folded:
                dve_split_ffn(dve, l, True)
            if ffn:
                if after_first(u):
                    dve.wait_ge(s["down"], u)
                dve_hid_hi(dve, u, (0, 1))
            if att:
                dve_blocks(dve, p)
            if ffn:
                dve_hid_hi(dve, u, (2,))
            if att:
                dve_kvt(dve, p)
            if ffn:
                dve_hid_hi(dve, u, (3,))
            if proj:
                dve_kv_bias(dve, p + 1)
            if ln2:
                dve.wait_ge(s["rstd2_s"], v + 1)
                if after_first(v):
                    dve.wait_ge(s["state"], v + SEQS)
                nc.vector.tensor_tensor(z2[:, :], hc2[:, :], rstd2[:, :], ALU.mult).then_inc(s["z2_s"], 1)
            if proj:
                dve_k_min(dve, p + 1)
            if ln1:
                dve.wait_ge(s["rstd1_s"], p)
                if after_first(p - 1):
                    dve.wait_ge(s["z1lo_s"], p - 1)
                nc.vector.scalar_tensor_tensor(z1[:, :], att_ps[:, :], cb1[:, :], rstd1[:, :],
                                               ALU.add, ALU.mult).then_inc(s["z1_s"], 1)
            if ln2:
                dve.wait_ge(s["z2_s"], v + 1)
                nc.vector.tensor_copy(z_hi[:, (b - 3) % SEQS, :], z2[:, :]).then_inc(s["z2hi_s"], 1)
            if proj:
                dve_q_min(dve, p + 1)
            if ln1:
                dve.wait_ge(s["z1_s"], p)
                if is_unit(p - 3):
                    dve.wait_ge(s["down"], p - 2)
                nc.vector.tensor_copy(z1_hi[:, (b - 1) % 2, :], z1[:, :]).then_inc(s["z1hi_s"], 1)
            if att and b == 0 and folded:
                nc.vector.tensor_copy(cb1[:, :], colb[:, 0:1]).then_inc(s["cb1_ready"], 1)
            if b == 2 and folded:
                dve_fold_cb2(dve, l, True)
            if att:
                dve.wait_ge(s["rden_s"], p + 1)
                if after_first(p):
                    dve.wait_ge(s["att_done"], p)
                nc.vector.tensor_tensor(q_n[:, :], q_phi[:, :], rden[:, :], ALU.mult).then_inc(s["qn"], 1)
            if proj:
                dve_k_phi(dve, p + 1, (lambda: dve_kvo(dve, p)) if att else None)
                dve_q_phi(dve, p + 1)
            elif att:
                dve_kvo(dve, p)
            if b == 1 and folded:
                dve_fold_c1(dve, l, True)
                dve_split_w1(dve, l, True)
            if b == SEQS - 3 and fold:
                dve_fold_att_first(dve, l + 1, True)
                dve_fold_ffn_first(dve, l + 1, True)
            if b == SEQS - 2 and fold:
                dve_split_wqkv(dve, l + 1, True)
            if b == SEQS - 1 and fold and att:
                dve_fold_wo(dve, l + 1, True)
            if b == SEQS - 2 and fold:
                dve_fold_att_biases(dve, l + 1, True)

        def pool_period(pool, l, b):
            p = l * SEQS + b
            ffn, ln1, ln2 = is_unit(p - 2), is_unit(p - 1), is_unit(p - 3)
            u, v = p - 2, p - 3
            if ln2:
                pool.wait_ge(s["sq2hi_s"], v + 1)
                if after_first(v):
                    pool.wait_ge(s["var2"], v)
                nc.gpsimd.tensor_tensor(sq2_lo[:, :], sq2[:, :], sq2_hi[:, :].bitcast(F32),
                                        ALU.subtract).then_inc(s["sq2lo_s"], 1)
            if ffn:
                if after_first(u):
                    pool.wait_ge(s["down"], u)
                for j in range(FC):
                    pool.wait_ge(s["hid_hi_s"], u * FC + j + 1)
                    nc.gpsimd.tensor_tensor(hid_lo[:, j, :], hid[:, j, :], hid_hi[:, j, :].bitcast(F32),
                                            ALU.subtract).then_inc(s["hid_lo_s"], 1)
            if ln1:
                pool.wait_ge(s["z1hi_s"], p)
                nc.gpsimd.tensor_tensor(z1_lo[:, (b - 1) % 2, :], z1[:, :], z1_hi[:, (b - 1) % 2, :].bitcast(F32),
                                        ALU.subtract).then_inc(s["z1lo_s"], 1)
            if ln2:
                pool.wait_ge(s["z2hi_s"], v + 1)
                nc.gpsimd.tensor_tensor(z_lo[:, (b - 3) % SEQS, :], z2[:, :], z_hi[:, (b - 3) % SEQS, :].bitcast(F32),
                                        ALU.subtract).then_inc(s["state"], 1)
            if ffn:
                pool.wait_ge(s["hc2_s"], u + 1)
                if after_first(u):
                    pool.wait_ge(s["sq2lo_s"], u)
                nc.gpsimd.tensor_tensor(sq2[:, :], hc2[:, :], hc2[:, :], ALU.mult).then_inc(s["sq2_s"], 1)

        with nc.Block() as block:
            def all_periods(eng, period):
                period(eng, -1, SEQS - 1)
                for b in range(SEQS):
                    period(eng, 0, b)
                with eng.Fori(1, L - 1) as l:
                    for b in range(SEQS):
                        period(eng, l, b)
                for b in range(SEQS + 3):
                    period(eng, L - 1 + b // SEQS, b % SEQS)

            @block.sync
            def _(sp):
                with sp.Fori(1, L) as l:
                    splits, steps = l * 2, l * FFN_STEPS
                    sp.wait_ge(s["wqkv_split"], splits)
                    sp.wait_ge(s["wo_ready"], l)
                    sp.sem_inc(s["sp_waited"], 1)
                    sp.wait_ge(s["ffn_fold"], steps)
                    sp.wait_ge(s["attb_ps"], l)
                    sp.sem_inc(s["sp_waited"], 1)
                    sp.wait_ge(s["ffnb_ps"], l)
                    sp.sem_inc(s["sp_waited"], 1)
                    load_layer(sp, l)

            @block.gpsimd
            def _(pool):
                all_periods(pool, pool_period)

            @block.tensor
            def _(pe):
                all_periods(pe, pe_period)

            @block.scalar
            def _(act):
                all_periods(act, act_period)

            @block.vector
            def _(dve):
                all_periods(dve, dve_period)

        h_tm = hid[:, :, :].rearrange("p b (t d) -> p b t d", d=D)
        y_tm = sb("y_tm", [P, 2, TT, D])
        f_st = sb("f_st", [P, SEQS * TT, 6])
        f_mv = sb("f_mv", [P, SEQS * TT, 2])
        f_std = sb("f_std", [P, SEQS * TT])
        f_r = sb("f_r", [P, SEQS * TT])
        g_hi, g_lo = cg2_hi, cg2_lo
        o_sent = [sem(f"o_sent{i}") for i in range(2)]
        with nc.Block() as block:
            @block.gpsimd
            def _(pool):
                f = s["fin"]
                nc.gpsimd.tensor_scalar(fold_cg2[:, :], ident[:, :], layer_vecs[:, L, V_G2P:V_G2P + 1], None,
                                        ALU.mult).then_inc(f, 1)
                nc.gpsimd.tensor_scalar(be2_bc[:, :], ones[:, :], layer_vecs[:, L, V_BE2P:V_BE2P + 1], None,
                                        ALU.mult).then_inc(f, 1)
                pool.wait_ge(f, 2)
                nc.gpsimd.tensor_copy(g_hi[:, :], fold_cg2[:, :]).then_inc(f, 1)
                pool.wait_ge(f, 3)
                nc.gpsimd.tensor_tensor(g_lo[:, :], fold_cg2[:, :], g_hi[:, :].bitcast(F32), ALU.subtract).then_inc(f, 1)

            @block.tensor
            def _(pe):
                pe.wait_ge(s["fin"], 4)
                nc.tensor.matmul(small_ps[:, 0:P], be2_bc[:, :], ident[:, :], start=True, stop=True).then_inc(s["bias_in"], 1)
                banks = [up_ps[0], up_ps[1]]
                for b in range(SEQS):
                    if b >= 2:
                        pe.wait_ge(s["htm"], b - 1)
                    for t in range(TT):
                        a_hi, a_lo = z_hi[:, b, t * P:(t + 1) * P], z_lo[:, b, t * P:(t + 1) * P]
                        dst = banks[b % 2][:, t * P:(t + 1) * P]
                        nc.tensor.matmul(dst, a_hi, g_hi[:, :], start=True, stop=False)
                        nc.tensor.matmul(dst, a_hi, g_lo[:, :], start=False, stop=False)
                        last = nc.tensor.matmul(dst, a_lo, g_hi[:, :], start=False, stop=True)
                    last.then_inc(s["htm_ps"], 1)

            @block.scalar
            def _(act):
                for b in range(SEQS):
                    act.wait_ge(s["fstd"], 3 + TT * (b + 1))
                    nc.scalar.activation(f_std[:, b * TT:(b + 1) * TT], f_mv[:, b * TT:(b + 1) * TT, 1], ACT.Sqrt,
                                         bias=eps_col[:, :]).then_inc(s["frstd"], 1)

            @block.vector
            def _(dve):
                dve.wait_ge(s["bias_in"], 1)
                nc.vector.tensor_copy(bkv1_bc[:, 0:P], small_ps[:, 0:P]).then_inc(s["zsum"], 1)
                dve.wait_ge(s["zsum"], 1)
                sc = s["eh"]
                sent = 0
                for b in range(SEQS + 1):
                    if b < SEQS:
                        dve.wait_ge(s["htm_ps"], b + 1)
                        nc.vector.tensor_tensor(h_tm[:, b % 4], up_ps[b % 2][:, :].rearrange("p (t d) -> p t d", d=D),
                                                bkv1_bc[:, 0:P].unsqueeze(1).to_broadcast([P, TT, D]),
                                                ALU.add).then_inc(s["htm"], 1)
                        dve.wait_ge(s["htm"], b + 1)
                        for t in range(TT):
                            nc.vector.bn_stats(f_st[:, b * TT + t, :], h_tm[:, b % 4, t, :]).then_inc(s["fstat"], 1)
                        for t in range(TT):
                            dve.wait_ge(s["fstat"], SEQS * TT + b * TT + t + 1)
                            nc.vector.bn_aggr(f_mv[:, b * TT + t, :], f_st[:, b * TT + t, :]).then_inc(s["fstd"], 1)
                    if b >= 1:
                        c = b - 1
                        dve.wait_ge(s["frstd"], c + 1)
                        dve.wait_ge(s["fstd"], 3 + TT * (c + 1))
                        nc.vector.reciprocal(f_r[:, c * TT:(c + 1) * TT], f_std[:, c * TT:(c + 1) * TT]).then_inc(s["bias_in"], 1)
                        dve.wait_ge(s["bias_in"], c + 2)
                        if c >= 2:
                            dve.wait_ge(o_sent[c % 2], 16 * (c // 2))
                        y = y_tm[:, c % 2]
                        for t in range(TT):
                            i = c * TT + t
                            nc.vector.tensor_scalar(y[:, t, :], h_tm[:, c % 4, t, :], f_mv[:, i, 0:1], f_r[:, i:i + 1],
                                                    ALU.subtract, ALU.mult).then_inc(s["z1hi_s"], 1)
                        dve.wait_ge(s["z1hi_s"], UNITS + TT * (c + 1))
                        nc.vector.tensor_tensor(y, y, gf_bc[:, :].unsqueeze(1).to_broadcast([P, TT, D]), ALU.mult).then_inc(s["z2hi_s"], 1)
                        dve.wait_ge(s["z2hi_s"], UNITS + 3 * c + 1)
                        nc.vector.tensor_tensor(y, y, bef_bc[:, :].unsqueeze(1).to_broadcast([P, TT, D]), ALU.add).then_inc(s["z2hi_s"], 1)
                        dve.wait_ge(s["z2hi_s"], UNITS + 3 * c + 2)
                        nc.vector.tensor_tensor(y, y, gate_tm[:, c], ALU.mult).then_inc(s["z2hi_s"], 1)
                        dve.wait_ge(s["z2hi_s"], UNITS + 3 * c + 3)
                        nc.vector.tensor_tensor(y, y, x_tm[:, c], ALU.add).then_inc(s["out_sent"], 1)

            @block.sync
            def _(sp):
                for b in range(SEQS):
                    sp.wait_ge(s["out_sent"], b + 1)
                    sp.dma_start(out_dram[:, b], y_tm[:, b % 2]).then_inc(o_sent[b % 2], 16)
                sp.wait_ge(o_sent[0], 16 * SEQS // 2)
                sp.wait_ge(o_sent[1], 16 * SEQS // 2)


NAMES = ("x", "Wq", "bq", "Wk", "bk", "Wv", "bv", "Wo", "bo", "g1", "be1", "g2", "be2", "W1", "c1", "W2", "c2",
         "gf", "bef")
FFN_NAMES = ("ln_g", "ln_b", "bn_g", "bn_b", "bn_mean", "bn_var", "Wr", "br", "W_down", "b_down", "W_up", "b_up")


def kernel(**inputs):
    import numpy as np
    import concourse.bacc as bacc
    from concourse.bass_utils import run_bass_kernel_spmd

    nc = bacc.Bacc("TRN2", target_bir_lowering=False, num_devices=1)
    arrays, args = {}, []
    for name in [f"L0_attn_{n}" for n in NAMES] + [f"L0_ffn_{n}" for n in FFN_NAMES]:
        a = np.ascontiguousarray(inputs[name])
        arrays[f"in_{name}"] = a
        args.append(nc.dram_tensor(f"in_{name}", a.shape, mybir.dt.from_np(a.dtype), kind="ExternalInput").ap())
    shape = inputs["L0_attn_x"].shape
    out = nc.dram_tensor("out_y", shape, mybir.dt.float32, kind="ExternalOutput").ap()
    build(nc, *args, out)
    r = run_bass_kernel_spmd(nc, [arrays], core_ids=[0])
    return r.results[0]["out_y"]
```

```python
import concourse.bass as bass
from concourse import mybir
from contextlib import ExitStack

P = 128
EPS = 1e-5
DEN_EPS = 1e-6


def build(nc, x, Wq, bq, Wk, bk, Wv, bv, Wo, bo, g1, be1, g2, be2, W1, c1, W2, c2, gf, bef,
          ln_g, ln_b, bn_g, bn_b, bn_mean, bn_var, Wr, br, W_down, b_down, W_up, b_up, out):
    F32 = mybir.dt.float32
    F32R = mybir.dt.float32r
    I32 = mybir.dt.int32
    ALU = mybir.AluOpType
    ACT = mybir.ActivationFunctionType
    AX = mybir.AxisListType

    SEQS, S, D = x.shape
    L = Wq.shape[0]
    F = W1.shape[2]
    FC = F // P
    DH = D // 16
    UNITS = L * SEQS
    TT = S // P
    E, _, HID = W_down.shape
    assert D == P and S == 512 and E == SEQS

    x_dram = x.rearrange("b (p s) d -> p b s d", s=TT)
    out_dram = out.rearrange("b (p s) d -> p b s d", s=TT)

    with ExitStack() as ctx:
        def sb(name, shape, dt=F32):
            return ctx.enter_context(nc.sbuf_tensor(name, shape, dt))

        def ps(name, shape):
            return ctx.enter_context(nc.psum_tensor(name, shape, F32))

        def sem(name):
            return ctx.enter_context(nc.semaphore(name))

        ident = sb("ident", [P, P])
        centre = sb("centre", [P, P])
        head_mask = sb("head_mask", [P, P])
        mean_f32 = sb("mean_f32", [P, P])
        mean_mat = sb("mean_mat", [P, P], F32R)
        ones = sb("ones", [P, P])
        eps_col = sb("eps_col", [P, 1])
        den_eps_col = sb("den_eps_col", [P, 1])
        neg1_col = sb("neg1_col", [P, 1])
        expert_m8 = sb("expert_m8", [SEQS, E])

        x_tm = sb("x_tm", [P, SEQS, TT, D])
        gate_tm = sb("gate_tm", [P, SEQS, TT, D])
        vec_rows = sb("vec_rows", [P, D])
        R_C1 = 7 * L
        NVEC = R_C1 + FC * L
        ffn_rows = sb("ffn_rows", [8, D])
        ffn_cols = sb("ffn_cols", [P, 8])
        C_LN_G, C_LN_B, C_BN_G, C_BN_B, C_BN_MEAN, C_BN_VAR, C_GF, C_BEF = range(8)
        cols = sb("cols", [P, NVEC])
        NLV = 7 + FC
        layer_vecs = sb("layer_vecs", [P, L + 1, NLV])
        V_BQ, V_BO, V_G1, V_BE1, V_G2P, V_BE2P, V_C2, V_C1 = range(8)
        z_hi = sb("z_hi", [P, SEQS, S], F32R)
        z_lo = sb("z_lo", [P, SEQS, S], F32R)

        raw_att = sb("raw_att", [P, 4, D])
        raw_w1 = sb("raw_w1", [P, F])
        raw_w2 = sb("raw_w2", [P, FC, D])
        raw_bkv = sb("raw_bkv", [1, 2 * D])
        lv_a = sb("lv_a", [P, NLV])
        lv_f = sb("lv_f", [P, NLV])
        fold_att = sb("fold_att", [P, 3 * D])
        fold_cg2 = sb("fold_cg2", [P, D])
        fold_w1 = sb("fold_w1", [P, F])
        fold_cg1 = sb("fold_cg1", [P, D])
        wqkv_hi = sb("wqkv_hi", [P, 3 * D], F32R)
        wqkv_lo = sb("wqkv_lo", [P, 3 * D], F32R)
        cg2_hi = sb("cg2_hi", [P, D], F32R)
        cg2_lo = sb("cg2_lo", [P, D], F32R)
        wo_sum = sb("wo_sum", [P, 1])
        wo_c = sb("wo_c", [P, D])
        w1_hi = sb("w1_hi", [P, F], F32R)
        w1_lo = sb("w1_lo", [P, F], F32R)
        cg1_hi = sb("cg1_hi", [P, D], F32R)
        cg1_lo = sb("cg1_lo", [P, D], F32R)
        w2_sum = sb("w2_sum", [P, FC])
        w2_c = sb("w2_c", [P, FC, D])
        w2_hi = sb("w2_hi", [P, FC, D], F32R)
        w2_lo = sb("w2_lo", [P, FC, D], F32R)
        be2_bc = sb("be2_bc", [P, P])
        bkv1_bc = sb("bkv1_bc", [P, 2 * D])
        bo_be2 = sb("bo_be2", [P, 1])
        c2_be1 = sb("c2_be1", [P, 1])
        bq_f = sb("bq_f", [P, 2])
        cb1 = sb("cb1", [P, 1])
        c1_f = sb("c1_f", [P, FC])
        colb = sb("colb", [P, FC + 2])
        cb2 = sb("cb2", [P, 1])

        kv1 = sb("kv1", [P, TT, 2 * D + 1])
        k_min = sb("k_min", [P, TT, D])
        k_exp = sb("k_exp", [P, TT, D])
        k_phi = sb("k_phi", [P, TT, D])
        q_exp = sb("q_exp", [P, S])
        q_min = sb("q_min", [P, S])
        q_phi = sb("q_phi", [P, S])
        q_phi_hi = sb("q_phi_hi", [P, S], F32R)
        q_phi_lo = sb("q_phi_lo", [P, S], F32R)
        ksum_blk = sb("ksum_blk", [P, P])
        ksum_hi = sb("ksum_hi", [P, P], F32R)
        ksum_lo = sb("ksum_lo", [P, P], F32R)
        kv_blk = sb("kv_blk", [P, P])
        kvT_blk = sb("kvT_blk", [P, P])
        kvo = sb("kvo", [P, P])
        den = sb("den", [P, S])
        rden = sb("rden", [P, S])
        q_n = sb("q_n", [P, S])
        sq1 = sb("sq1", [P, S])
        sq1_hi = sb("sq1_hi", [P, S], F32R)
        sq1_lo = sb("sq1_lo", [P, S], F32R)
        hc2 = sb("hc2", [P, S])
        sq2 = sb("sq2", [P, S])
        sq2_hi = sb("sq2_hi", [P, S], F32R)
        sq2_lo = sb("sq2_lo", [P, S], F32R)
        lnv1 = sb("lnv1", [P, S])
        lnv2 = sb("lnv2", [P, S])
        rstd1 = sb("rstd1", [P, S])
        rstd2 = sb("rstd2", [P, S])
        z1 = sb("z1", [P, S])
        z1_hi = sb("z1_hi", [P, 2, S], F32R)
        z1_lo = sb("z1_lo", [P, 2, S], F32R)
        z2 = sb("z2", [P, S])
        hid = sb("hid", [P, FC, S])
        hid_hi = sb("hid_hi", [P, FC, S], F32R)
        hid_lo = sb("hid_lo", [P, FC, S], F32R)

        kv_ps = [ps(f"kv_ps{i}", [P, TT // 2, 2 * D]) for i in range(2)]
        q_ps = ps("q_ps", [P, S])
        small_ps = ps("small_ps", [P, 512])
        KV_KSUM, KVT, KVO = small_ps[:, 0:P + 1], small_ps[:, 2 * P:3 * P], small_ps[:, 3 * P:4 * P]
        BIAS, COLB = small_ps[:, 0:2 * P], small_ps[:, 2 * P:2 * P + 8]
        att_ps = ps("att_ps", [P, S])
        up_ps = [ps(f"up_ps{i}", [P, S]) for i in range(2)]
        down_ps = ps("down_ps", [P, S])

        names = """const_ready vec_in ffn_vec_in row_in cols_ps cols_ready lv_ready ffn_cols_ps ffn_cols_ready
            bn_stats stats ln_x_s r_x_ready r_x_sq v_xn_ready r_xn_ready r_f_ready
            xn xn_ps xn_hi zf zf_ps zf_fm_s bn_ln bn_rstd bn_chain logit_ps logit softmax_e gate_diag
            gate_ps gate_bc_ready routed expert_in e_down e_hid_s e_up gated
            raw_loaded sp_waited att_fold ffn_fold wqkv_split cg2_split wo_ready w1_split ffnw_split
            attb_ps ffnb_ps attb_ready cb1_ready c1_ready cb2_ready
            kvproj qproj kv_biased kmin kexp kexpm1 kphi qmin qexp qexpm1 qphi
            kv_ps ksumblk ksum_hi_s ksum_lo_s qphi_hi_s qphi_lo_s kvblk kvt_ps kvt_sb kvo_ps kvo_sb den_ps den_sb rden_s qn att_done
            sq1_s sq1hi_s sq1lo_s var1 lnv1_s rstd1_s z1_s z1hi_s z1lo_s
            up gelu hid_hi_s hid_lo_s down hc2_s sq2_s sq2hi_s sq2lo_s var2 lnv2_s rstd2_s z2_s z2hi_s state x_state
            fin_fold cbf_ps cbf_ready fin_h fin_sq_s fin_var fin_ln_s fin_rstd_s fin_z fin_y fin_out_ps
            fin_gated y_ready out_sent""".split()
        s = {n: sem(n) for n in names}

        def load_layer(sp, l):
            sp.dma_start(raw_att[:, 0, :], Wq[l]).then_inc(s["raw_loaded"], 16)
            sp.dma_start(raw_att[:, 1, :], Wk[l]).then_inc(s["raw_loaded"], 16)
            sp.dma_start(raw_att[:, 2, :], Wv[l]).then_inc(s["raw_loaded"], 16)
            sp.dma_start(raw_att[:, 3, :], Wo[l]).then_inc(s["raw_loaded"], 16)
            row = slice(l, l + 1) if isinstance(l, int) else bass.ds(l, 1)
            sp.dma_start(raw_bkv[0:1, 0:D], bk[row, :]).then_inc(s["raw_loaded"], 16)
            sp.dma_start(raw_bkv[0:1, D:2 * D], bv[row, :]).then_inc(s["raw_loaded"], 16)
            sp.dma_start(raw_w1[:, :], W1[l]).then_inc(s["raw_loaded"], 16)
            sp.dma_start(raw_w2[:, :, :], W2[l].rearrange("(j p) n -> p j n", p=P)).then_inc(s["raw_loaded"], 16)
        LOADS = 8 * 16

        ATT_STEPS, FFN_STEPS = 7, 7

        def dve_fold_att_vectors(dve, l, wait_free):
            a = l * ATT_STEPS
            dve.wait_ge(s["raw_loaded"], l * LOADS + LOADS)
            if wait_free:
                dve.wait_ge(s["attb_ps"], l)
                dve.wait_ge(s["attb_ready"], l * 5)
            nc.vector.tensor_scalar(lv_a[:, :], layer_vecs[:, l, :], 1.0, None, ALU.mult).then_inc(s["att_fold"], 1)
            nc.vector.reduce_sum(wo_sum[:, :], raw_att[:, 3, :], AX.X).then_inc(s["att_fold"], 1)
            dve.wait_ge(s["att_fold"], a + 1)
            nc.vector.tensor_tensor(bo_be2[:, :], lv_a[:, V_BO:V_BO + 1], lv_a[:, V_BE2P:V_BE2P + 1],
                                    ALU.add).then_inc(s["att_fold"], 1)
            dve.wait_ge(s["att_fold"], a + 2)
            nc.vector.tensor_scalar(wo_sum[:, :], wo_sum[:, :], 1.0 / D, None,
                                    ALU.mult).then_inc(s["att_fold"], 1)
            nc.vector.tensor_scalar(be2_bc[:, :], ones[:, :], lv_a[:, V_BE2P:V_BE2P + 1], None,
                                    ALU.mult).then_inc(s["att_fold"], 1)

        def dve_fold_wqkv(dve, l, wait_free):
            if wait_free:
                dve.wait_ge(s["wqkv_split"], l * 2)
            nc.vector.tensor_scalar(fold_att[:, :], raw_att[:, 0:3, :], lv_a[:, V_G2P:V_G2P + 1], None,
                                    ALU.mult).then_inc(s["att_fold"], 1)

        def dve_fold_cg2(dve, l, wait_free):
            if wait_free:
                dve.wait_ge(s["cg2_split"], l * 2)
            nc.vector.tensor_scalar(fold_cg2[:, :], centre[:, :], lv_a[:, V_G2P:V_G2P + 1], None,
                                    ALU.mult).then_inc(s["att_fold"], 1)

        def dve_split_wqkv(dve, l, wait_free):
            dve.wait_ge(s["att_fold"], l * ATT_STEPS + 6)
            if wait_free:
                dve.wait_ge(s["qproj"], l * SEQS)
                dve.wait_ge(s["kvproj"], l * SEQS * 2)
            nc.vector.tensor_copy(wqkv_hi[:, :], fold_att[:, :]).then_inc(s["wqkv_split"], 1)
            dve.wait_ge(s["wqkv_split"], l * 2 + 1)
            nc.vector.tensor_tensor(wqkv_lo[:, :], fold_att[:, :], wqkv_hi[:, :].bitcast(F32),
                                    ALU.subtract).then_inc(s["wqkv_split"], 1)

        def dve_split_cg2(dve, l, wait_free):
            dve.wait_ge(s["att_fold"], l * ATT_STEPS + 7)
            if wait_free:
                dve.wait_ge(s["att_done"], l * SEQS)
            nc.vector.tensor_copy(cg2_hi[:, :], fold_cg2[:, :]).then_inc(s["cg2_split"], 1)
            dve.wait_ge(s["cg2_split"], l * 2 + 1)
            nc.vector.tensor_tensor(cg2_lo[:, :], fold_cg2[:, :], cg2_hi[:, :].bitcast(F32),
                                    ALU.subtract).then_inc(s["cg2_split"], 1)

        def dve_fold_wo(dve, l, wait_free):
            dve.wait_ge(s["att_fold"], l * ATT_STEPS + 4)
            if wait_free:
                dve.wait_ge(s["kvo_ps"], l * SEQS)
            nc.vector.tensor_scalar(wo_c[:, :], raw_att[:, 3, :], wo_sum[:, :], None,
                                    ALU.subtract).then_inc(s["wo_ready"], 1)

        def dve_fold_att_biases(dve, l, wait_free):
            dve.wait_ge(s["attb_ps"], l + 1)
            dve.wait_ge(s["ffnb_ps"], l + 1)
            if wait_free:
                dve.wait_ge(s["cb1_ready"], l)
                dve.wait_ge(s["cb2_ready"], l)
                dve.wait_ge(s["c1_ready"], l)
                dve.wait_ge(s["qphi"], l * SEQS)
                dve.wait_ge(s["kv_biased"], l * SEQS * 2)
            nc.vector.tensor_scalar(bkv1_bc[:, 0:D], BIAS[:, 0:D], 1.0, None, ALU.add).then_inc(s["attb_ready"], 1)
            nc.vector.tensor_copy(bkv1_bc[:, D:2 * D], BIAS[:, D:2 * D]).then_inc(s["attb_ready"], 1)
            nc.vector.tensor_copy(colb[:, :], COLB[:, 1:3 + FC]).then_inc(s["attb_ready"], 1)
            nc.vector.tensor_scalar(bq_f[:, 0:1], COLB[:, 0:1], lv_a[:, V_BQ:V_BQ + 1], None,
                                    ALU.add).then_inc(s["attb_ready"], 1)
            nc.vector.tensor_scalar(bq_f[:, 1:2], COLB[:, 0:1], lv_a[:, V_BQ:V_BQ + 1], 1.0,
                                    ALU.add, ALU.add).then_inc(s["attb_ready"], 1)

        def dve_fold_ffn_vectors(dve, l, wait_free):
            f = l * FFN_STEPS
            if wait_free:
                dve.wait_ge(s["ffnb_ps"], l)
                dve.wait_ge(s["c1_ready"], l)
            nc.vector.tensor_scalar(lv_f[:, :], layer_vecs[:, l, :], 1.0, None, ALU.mult).then_inc(s["ffn_fold"], 1)
            nc.vector.reduce_sum(w2_sum[:, :], raw_w2[:, :, :], AX.X).then_inc(s["ffn_fold"], 1)
            dve.wait_ge(s["ffn_fold"], f + 1)
            nc.vector.tensor_tensor(c2_be1[:, :], lv_f[:, V_C2:V_C2 + 1], lv_f[:, V_BE1:V_BE1 + 1],
                                    ALU.add).then_inc(s["ffn_fold"], 1)
            dve.wait_ge(s["ffn_fold"], f + 2)
            nc.vector.tensor_scalar(w2_sum[:, :], w2_sum[:, :], 1.0 / D, None,
                                    ALU.mult).then_inc(s["ffn_fold"], 1)

        def dve_fold_w1(dve, l, wait_free):
            dve.wait_ge(s["raw_loaded"], l * LOADS + LOADS)
            if wait_free:
                dve.wait_ge(s["w1_split"], l * 2)
            nc.vector.tensor_scalar(fold_w1[:, :], raw_w1[:, :], lv_f[:, V_G1:V_G1 + 1], None,
                                    ALU.mult).then_inc(s["ffn_fold"], 1)
            nc.vector.tensor_scalar(fold_cg1[:, :], centre[:, :], lv_f[:, V_G1:V_G1 + 1], None,
                                    ALU.mult).then_inc(s["ffn_fold"], 1)

        def dve_fold_w2(dve, l, wait_free):
            dve.wait_ge(s["ffn_fold"], l * FFN_STEPS + 4)
            if wait_free:
                dve.wait_ge(s["ffnw_split"], l * 4)
            nc.vector.tensor_tensor(w2_c[:, :, :], raw_w2[:, :, :],
                                    w2_sum[:, :].unsqueeze(2).to_broadcast([P, FC, D]),
                                    ALU.subtract).then_inc(s["ffn_fold"], 1)

        def dve_w1_hi(dve, l, wait_free):
            dve.wait_ge(s["ffn_fold"], l * FFN_STEPS + 5)
            if wait_free:
                dve.wait_ge(s["up"], l * SEQS * FC)
            nc.vector.tensor_copy(w1_hi[:, :], fold_w1[:, :]).then_inc(s["w1_split"], 1)

        def pool_w1_lo(pool, l):
            pool.wait_ge(s["w1_split"], l * 2 + 1)
            nc.gpsimd.tensor_tensor(w1_lo[:, :], fold_w1[:, :], w1_hi[:, :].bitcast(F32),
                                    ALU.subtract).then_inc(s["w1_split"], 1)

        def dve_split_ffn(dve, l, wait_free):
            dve.wait_ge(s["ffn_fold"], l * FFN_STEPS + 7)
            if wait_free:
                dve.wait_ge(s["down"], l * SEQS)
            nc.vector.tensor_copy(cg1_hi[:, :], fold_cg1[:, :]).then_inc(s["ffnw_split"], 1)
            nc.vector.tensor_copy(w2_hi[:, :, :], w2_c[:, :, :]).then_inc(s["ffnw_split"], 1)
            dve.wait_ge(s["ffnw_split"], l * 4 + 1)
            nc.vector.tensor_tensor(cg1_lo[:, :], fold_cg1[:, :], cg1_hi[:, :].bitcast(F32),
                                    ALU.subtract).then_inc(s["ffnw_split"], 1)

        def pool_w2_lo(pool, l):
            pool.wait_ge(s["ffnw_split"], l * 4 + 3)
            nc.gpsimd.tensor_tensor(w2_lo[:, :, :], w2_c[:, :, :], w2_hi[:, :, :].bitcast(F32),
                                    ALU.subtract).then_inc(s["ffnw_split"], 1)

        def dve_fold_c1(dve, l, wait_free):
            dve.wait_ge(s["attb_ready"], l * 5 + 5)
            if wait_free:
                dve.wait_ge(s["gelu"], l * SEQS * FC)
            nc.vector.tensor_tensor(c1_f[:, :], colb[:, 1:1 + FC], lv_f[:, V_C1:V_C1 + FC],
                                    ALU.add).then_inc(s["c1_ready"], 1)

        def dve_fold_cb2(dve, l, wait_free):
            if wait_free:
                dve.wait_ge(s["hc2_s"], l * SEQS)
            nc.vector.tensor_copy(cb2[:, :], colb[:, 1 + FC:2 + FC]).then_inc(s["cb2_ready"], 1)

        def pe_fold_biases(pe, l, wait_free):
            pe.wait_ge(s["raw_loaded"], l * LOADS + LOADS)
            pe.wait_ge(s["att_fold"], l * ATT_STEPS + 5)
            if wait_free:
                pe.wait_ge(s["kvo_sb"], l * SEQS - 1)
            nc.tensor.matmul(COLB[:, 0:1], raw_att[:, 0, :], lv_a[:, V_BE2P:V_BE2P + 1], start=True, stop=True)
            nc.tensor.matmul(COLB[:, 1:2], centre[:, :], bo_be2[:, :], start=True, stop=True)
            nc.tensor.matmul(BIAS, be2_bc[:, :], raw_att[:, 1:3, :], start=True, stop=False)
            nc.tensor.matmul(BIAS, ones[0:1, :], raw_bkv[0:1, :], start=False, stop=True).then_inc(s["attb_ps"], 1)
            pe.wait_ge(s["ffn_fold"], l * FFN_STEPS + 3)
            for j in range(FC):
                nc.tensor.matmul(COLB[:, 2 + j:3 + j], raw_w1[:, j * P:(j + 1) * P], lv_f[:, V_BE1:V_BE1 + 1],
                                 start=True, stop=True)
            nc.tensor.matmul(COLB[:, 2 + FC:3 + FC], centre[:, :], c2_be1[:, :],
                             start=True, stop=True).then_inc(s["ffnb_ps"], 1)

        x_in = [sem(f"x_in{i}") for i in range(SEQS // 2)]
        wr_sb = sb("wr_sb", [P, E])
        br_bc = sb("br_bc", [SEQS, E])
        expert_i = sb("expert_i", [SEQS, 1], I32)
        ew_down = sb("ew_down", [P, SEQS, HID])
        eb_down = sb("eb_down", [HID, SEQS])
        ew_up = sb("ew_up", [HID + 1, SEQS, D])
        e_hid = sb("e_hid", [HID + 1, 2, S])
        st = sb("st", [P, SEQS * TT, 6])
        mv = sb("mv", [P, SEQS * TT, 2])
        ln_x = sb("ln_x", [P, SEQS * TT])
        r_x = sb("r_x", [P, SEQS * TT])
        v_xn = sb("v_xn", [P, SEQS * TT])
        r_xn = sb("r_xn", [P, SEQS * TT])
        r_f = sb("r_f", [P, SEQS * TT])
        fin_zb = sb("fin_zb", [P, 2, S])
        xn_tm = fin_zb[:, :, :]
        zf_tm = hid[:, 0:2, :]
        zf_fm = gate_tm[:, :, :, :].rearrange("p b s d -> p b (s d)")
        zf_sum = sb("zf_sum", [P, SEQS])
        bn_v = sb("bn_v", [P, 2])
        z_bn = sb("z_bn", [P, SEQS])
        lg = sb("lg", [SEQS, E])
        lg_e = sb("lg_e", [SEQS, E])
        r_cols = sb("r_cols", [SEQS, 6])
        gate_d = sb("gate_d", [SEQS, SEQS])
        gate_bc = sb("gate_bc", [P, SEQS])
        CONSTS = 14

        cbf = sb("cbf", [P, 1])
        fin_sq = hid[:, 0:2, :]
        fin_ln = sb("fin_ln", [P, S])
        fin_rstd = hid[:, 2:4, :]

        STATS_GROUPS = [(i, i + 2) for i in range(0, SEQS, 2)]

        def dve_stats(dve, g):
            b0, b1 = STATS_GROUPS[g]
            for b in range(b0, b1):
                if b % 2 == 0:
                    dve.wait_ge(x_in[b // 2], 16)
                for t in range(TT):
                    nc.vector.bn_stats(st[:, b * TT + t, :], x_tm[:, b, t, :]).then_inc(s["bn_stats"], 1)
            for i in range(b0 * TT, b1 * TT):
                dve.wait_ge(s["bn_stats"], i + 1)
                nc.vector.bn_aggr(mv[:, i, :], st[:, i, :]).then_inc(s["stats"], 1)

        def dve_stats_of_xn(dve, g):
            i0, i1 = STATS_GROUPS[g][0] * TT, STATS_GROUPS[g][1] * TT
            dve.wait_ge(s["r_x_ready"], g + 1)
            nc.vector.tensor_tensor(v_xn[:, i0:i1], r_x[:, i0:i1], r_x[:, i0:i1], ALU.mult).then_inc(s["r_x_sq"], 1)
            dve.wait_ge(s["r_x_sq"], g + 1)
            nc.vector.tensor_tensor(v_xn[:, i0:i1], v_xn[:, i0:i1], mv[:, i0:i1, 1], ALU.mult).then_inc(s["v_xn_ready"], 1)

        def dve_r_f(dve, g):
            i0, i1 = STATS_GROUPS[g][0] * TT, STATS_GROUPS[g][1] * TT
            dve.wait_ge(s["r_xn_ready"], g + 1)
            nc.vector.tensor_tensor(r_f[:, i0:i1], r_xn[:, i0:i1], r_x[:, i0:i1], ALU.mult).then_inc(s["r_f_ready"], 1)

        def act_rstd_x(act, g):
            i0, i1 = STATS_GROUPS[g][0] * TT, STATS_GROUPS[g][1] * TT
            act.wait_ge(s["stats"], i1)
            nc.scalar.activation(ln_x[:, i0:i1], mv[:, i0:i1, 1], ACT.Ln, bias=eps_col[:, :]).then_inc(s["ln_x_s"], 1)
            act.wait_ge(s["ln_x_s"], 2 * g + 1)
            nc.scalar.activation(r_x[:, i0:i1], ln_x[:, i0:i1], ACT.Exp, scale=-0.5).then_inc(s["r_x_ready"], 1)
            act.wait_ge(s["v_xn_ready"], g + 1)
            nc.scalar.activation(ln_x[:, i0:i1], v_xn[:, i0:i1], ACT.Ln, bias=eps_col[:, :]).then_inc(s["ln_x_s"], 1)
            act.wait_ge(s["ln_x_s"], 2 * g + 2)
            nc.scalar.activation(r_xn[:, i0:i1], ln_x[:, i0:i1], ACT.Exp, scale=-0.5).then_inc(s["r_xn_ready"], 1)

        LATE_XN = range(4, SEQS)
        def dve_xn(dve, b):
            if b >= 2:
                dve.wait_ge(s["xn_ps"], b - 1)
            for t in range(TT):
                i = b * TT + t
                nc.vector.tensor_scalar(xn_tm[:, b % 2, t * D:(t + 1) * D], x_tm[:, b, t, :], mv[:, i, 0:1],
                                        r_x[:, i:i + 1], ALU.subtract, ALU.mult).then_inc(s["xn"], 1)

        def xn_bank(b):
            return att_ps if b in LATE_XN else up_ps[0]

        def pe_xn_transpose(pe, b):
            pe.wait_ge(s["xn"], TT * (b + 1))
            if b in LATE_XN:
                pe.wait_ge(s["z1_s"], b - 3)
            elif b >= 1:
                pe.wait_ge(s["x_state"], b)
            for t in range(TT):
                last = nc.tensor.transpose(xn_bank(b)[:, t * P:(t + 1) * P], xn_tm[:, b % 2, t * D:(t + 1) * D], ident[:, :])
            last.then_inc(s["xn_ps"], 1)

        def act_xn_hi(act, b):
            act.wait_ge(s["xn_ps"], b + 1)
            nc.scalar.activation(z_hi[:, b, :], xn_bank(b)[:, :], ACT.Identity).then_inc(s["xn_hi"], 1)

        def dve_xn_lo(dve, b):
            dve.wait_ge(s["xn_hi"], b + 1)
            nc.vector.tensor_tensor(z_lo[:, b, :], xn_bank(b)[:, :], z_hi[:, b, :].bitcast(F32),
                                    ALU.subtract).then_inc(s["x_state"], 1)

        def dve_zf(dve, b):
            dve.wait_ge(s["r_f_ready"], b // 2 + 1)
            if b >= 2:
                dve.wait_ge(s["zf_ps"], b - 1)
            for t in range(TT):
                i = b * TT + t
                nc.vector.tensor_scalar(zf_tm[:, b % 2, t * D:(t + 1) * D], x_tm[:, b, t, :], mv[:, i, 0:1],
                                        r_f[:, i:i + 1], ALU.subtract, ALU.mult).then_inc(s["zf"], 1)

        def zf_bank(b):
            return up_ps[0] if b in (5, 7) else down_ps

        def pe_zf_transpose(pe, b):
            pe.wait_ge(s["zf"], TT * (b + 1))
            if b >= 1:
                pe.wait_ge(s["zf_fm_s"], b if b < 5 else b - 1)
            for t in range(TT):
                last = nc.tensor.transpose(zf_bank(b)[:, t * P:(t + 1) * P], zf_tm[:, b % 2, t * D:(t + 1) * D], ident[:, :])
            last.then_inc(s["zf_ps"], 1)

        def act_zf_fm(act, b):
            act.wait_ge(s["zf_ps"], b + 1)
            if b == 0:
                act.wait_ge(s["ffn_cols_ready"], 1)
            nc.scalar.activation(zf_fm[:, b, :], zf_bank(b)[:, :], ACT.Identity,
                                 scale=ffn_cols[:, C_LN_G:C_LN_G + 1], bias=ffn_cols[:, C_LN_B:C_LN_B + 1],
                                 accum_out=zf_sum[:, b:b + 1]).then_inc(s["zf_fm_s"], 1)

        def pe_cols(pe):
            pe.wait_ge(s["const_ready"], CONSTS)
            pe.wait_ge(s["vec_in"], 8 * 16)
            nc.tensor.transpose(small_ps[:, 0:NVEC], vec_rows[0:NVEC, :], ident[0:NVEC, 0:NVEC]).then_inc(s["cols_ps"], 1)

        def pe_ffn_cols(pe):
            pe.wait_ge(s["ffn_vec_in"], 8 * 16)
            nc.tensor.transpose(att_ps[:, 0:8], ffn_rows[:, :], ident[0:8, 0:8]).then_inc(s["ffn_cols_ps"], 1)

        def dve_cols(dve):
            dve.wait_ge(s["cols_ps"], 1)
            nc.vector.tensor_copy(cols[:, :], small_ps[:, 0:NVEC]).then_inc(s["cols_ready"], 1)
            dve.wait_ge(s["cols_ready"], 1)
            nc.vector.tensor_copy(layer_vecs[:, 0:L, V_BQ:V_BE1 + 1],
                                  cols[:, 0:4 * L].rearrange("p (v l) -> p l v", l=L)).then_inc(s["lv_ready"], 1)
            nc.vector.tensor_copy(layer_vecs[:, 1:L + 1, V_G2P:V_BE2P + 1],
                                  cols[:, 4 * L:6 * L].rearrange("p (v l) -> p l v", l=L)).then_inc(s["lv_ready"], 1)
            nc.vector.tensor_copy(layer_vecs[:, 0:L, V_C2:V_C2 + 1],
                                  cols[:, 6 * L:7 * L].rearrange("p (v l) -> p l v", l=L)).then_inc(s["lv_ready"], 1)
            nc.vector.tensor_copy(layer_vecs[:, 0:L, V_C1:V_C1 + FC],
                                  cols[:, R_C1:R_C1 + FC * L].rearrange("p (l j) -> p l j", l=L)).then_inc(s["lv_ready"], 1)
            nc.vector.memset(layer_vecs[:, 0, V_G2P:V_G2P + 1], 1.0).then_inc(s["lv_ready"], 1)
            nc.vector.memset(layer_vecs[:, 0, V_BE2P:V_BE2P + 1], 0.0).then_inc(s["lv_ready"], 1)
            dve.wait_ge(s["lv_ready"], 6)

        def act_bn_rstd(act):
            act.wait_ge(s["ffn_cols_ready"], 1)
            nc.scalar.activation(bn_v[:, 0:1], ffn_cols[:, C_BN_VAR:C_BN_VAR + 1], ACT.Ln, bias=eps_col[:, :]).then_inc(s["bn_ln"], 1)
            act.wait_ge(s["bn_ln"], 1)
            nc.scalar.activation(bn_v[:, 1:2], bn_v[:, 0:1], ACT.Exp, scale=-0.5).then_inc(s["bn_rstd"], 1)

        def dve_batch_norm(dve):
            ch = s["bn_chain"]
            dve.wait_ge(s["zf_fm_s"], SEQS)
            dve.wait_ge(s["bn_rstd"], 1)
            nc.vector.tensor_scalar(z_bn[:, :], zf_sum[:, :], 1.0 / S, None, ALU.mult).then_inc(ch, 1)
            dve.wait_ge(ch, 1)
            nc.vector.tensor_scalar(z_bn[:, :], z_bn[:, :], ffn_cols[:, C_BN_MEAN:C_BN_MEAN + 1], bn_v[:, 1:2],
                                    ALU.subtract, ALU.mult).then_inc(ch, 1)
            dve.wait_ge(ch, 2)
            nc.vector.tensor_scalar(z_bn[:, :], z_bn[:, :], ffn_cols[:, C_BN_G:C_BN_G + 1],
                                    ffn_cols[:, C_BN_B:C_BN_B + 1], ALU.mult, ALU.add).then_inc(ch, 1)

        def pe_logits(pe):
            pe.wait_ge(s["bn_chain"], 3)
            pe.wait_ge(s["row_in"], 32)
            nc.tensor.matmul(down_ps[0:SEQS, 0:E], z_bn[:, :], wr_sb[:, :], start=True, stop=True).then_inc(s["logit_ps"], 1)

        def act_softmax(act):
            act.wait_ge(s["logit"], 3)
            nc.scalar.activation(lg_e[:, :], lg[:, :], ACT.Exp, bias=r_cols[:, 0:1],
                                 accum_out=r_cols[:, 1:2]).then_inc(s["softmax_e"], 1)

        def pe_gate_bc(pe):
            pe.wait_ge(s["gate_diag"], 1)
            nc.tensor.matmul(down_ps[:, 0:SEQS], ones[0:SEQS, :], gate_d[:, :], start=True, stop=True).then_inc(s["gate_ps"], 1)

        def dve_route(dve):
            lgs = s["logit"]
            dve.wait_ge(s["logit_ps"], 1)
            nc.vector.tensor_tensor(lg[:, :], down_ps[0:SEQS, 0:E], br_bc[:, :], ALU.add).then_inc(lgs, 1)
            dve.wait_ge(lgs, 1)
            nc.vector.reduce_max(r_cols[:, 2:3], lg[:, :], AX.X).then_inc(lgs, 1)
            dve.wait_ge(lgs, 2)
            nc.vector.tensor_scalar(r_cols[:, 0:1], r_cols[:, 2:3], -1.0, None, ALU.mult).then_inc(lgs, 1)
            dve.wait_ge(s["softmax_e"], 1)
            nc.vector.reciprocal(r_cols[:, 3:4], r_cols[:, 1:2]).then_inc(lgs, 1)
            dve.wait_ge(lgs, 4)
            nc.vector.tensor_scalar(lg_e[:, :], lg_e[:, :], r_cols[:, 3:4], None, ALU.mult).then_inc(lgs, 1)
            dve.wait_ge(lgs, 5)
            nc.vector.reduce_max(r_cols[:, 4:5], lg_e[:, :], AX.X).then_inc(lgs, 1)
            dve.wait_ge(lgs, 6)
            nc.vector.tensor_scalar(gate_d[:, :], ident[0:SEQS, 0:SEQS], r_cols[:, 4:5], None, ALU.mult).then_inc(s["gate_diag"], 1)
            nc.vector.tensor_scalar(lg[:, :], lg_e[:, :], r_cols[:, 4:5], None, ALU.is_equal).then_inc(lgs, 1)
            dve.wait_ge(lgs, 7)
            nc.vector.tensor_tensor(lg[:, :], lg[:, :], expert_m8[:, :], ALU.mult).then_inc(lgs, 1)
            dve.wait_ge(lgs, 8)
            nc.vector.tensor_reduce(r_cols[:, 5:6], lg[:, :], AX.X, ALU.min).then_inc(lgs, 1)
            dve.wait_ge(lgs, 9)
            nc.vector.tensor_scalar(expert_i[:, :], r_cols[:, 5:6], float(E), None, ALU.add).then_inc(s["routed"], 1)
            dve.wait_ge(s["gate_ps"], 1)
            nc.vector.tensor_copy(gate_bc[:, :], down_ps[:, 0:SEQS]).then_inc(s["gate_bc_ready"], 1)

        def pe_expert_down(pe, b):
            if b == 0:
                pe.wait_ge(s["expert_in"], SEQS * 64)
            if b >= 2:
                pe.wait_ge(s["e_hid_s"], b - 1)
            if b == 1:
                pe.wait_ge(s["cbf_ready"], 1)
            bank = small_ps if b % 2 else q_ps
            nc.tensor.matmul(bank[0:HID, :], ew_down[:, b, :], zf_fm[:, b, :], start=True, stop=True).then_inc(s["e_down"], 1)

        def dve_expert_relu(dve, b):
            dve.wait_ge(s["e_down"], b + 1)
            if b >= 2:
                dve.wait_ge(s["e_up"], b - 1)
            bank = small_ps if b % 2 else q_ps
            nc.vector.tensor_scalar(e_hid[0:HID, b % 2, :], bank[0:HID, :], eb_down[:, b:b + 1], 0.0,
                                    ALU.add, ALU.max).then_inc(s["e_hid_s"], 1)

        def pe_expert_up(pe, b):
            pe.wait_ge(s["e_hid_s"], b + 1)
            if b >= 2:
                pe.wait_ge(s["gated"], b - 1)
            for t in range(TT):
                last = nc.tensor.matmul(kv_ps[b % 2][:, t // 2, (t % 2) * D:(t % 2 + 1) * D],
                                        e_hid[:, b % 2, t * P:(t + 1) * P], ew_up[:, b, :], start=True, stop=True)
            last.then_inc(s["e_up"], 1)

        def act_expert_silu(act, b):
            act.wait_ge(s["e_up"], b + 1)
            if b == 0:
                act.wait_ge(s["gate_bc_ready"], 1)
            nc.scalar.activation(gate_tm[:, b, :, :], kv_ps[b % 2][:, :, :], ACT.Silu,
                                 scale=gate_bc[:, b:b + 1]).then_inc(s["gated"], 1)

        def dve_final_fold(dve):
            dve.wait_ge(s["cg2_split"], L * 2)
            nc.vector.tensor_scalar(fold_cg2[:, :], centre[:, :], layer_vecs[:, L, V_G2P:V_G2P + 1], None,
                                    ALU.mult).then_inc(s["fin_fold"], 1)
            dve.wait_ge(s["att_done"], UNITS)
            dve.wait_ge(s["fin_fold"], 1)
            nc.vector.tensor_copy(cg2_hi[:, :], fold_cg2[:, :]).then_inc(s["fin_fold"], 1)
            dve.wait_ge(s["fin_fold"], 2)
            nc.vector.tensor_tensor(cg2_lo[:, :], fold_cg2[:, :], cg2_hi[:, :].bitcast(F32),
                                    ALU.subtract).then_inc(s["fin_fold"], 1)

        def pe_final_bias(pe):
            pe.wait_ge(s["kvo_sb"], UNITS)
            nc.tensor.matmul(COLB[:, 0:1], centre[:, :], layer_vecs[:, L, V_BE2P:V_BE2P + 1],
                             start=True, stop=True).then_inc(s["cbf_ps"], 1)

        def dve_final_bias(dve):
            dve.wait_ge(s["cbf_ps"], 1)
            nc.vector.tensor_copy(cbf[:, :], COLB[:, 0:1]).then_inc(s["cbf_ready"], 1)

        fin_h_ps = [kv_ps[i][:, :, :].rearrange("p a b -> p (a b)") for i in range(2)] + [down_ps[:, :]]
        fin_var_ps = (q_ps, small_ps)
        fin_out_ps = (att_ps, up_ps[1])

        def pe_final_centre(pe, w):
            pe.wait_ge(s["state"], UNITS - SEQS + w + 1)
            if w == 0:
                pe.wait_ge(s["fin_fold"], 3)
                pe.wait_ge(s["gated"], SEQS)
            if w == 2:
                pe.wait_ge(s["hc2_s"], UNITS)
            if w >= 3:
                pe.wait_ge(s["fin_z"], w - 2)
            three_pass(fin_h_ps[w % 3], cg2_hi[:, :], cg2_lo[:, :], z_hi[:, w, :], z_lo[:, w, :],
                       True, True).then_inc(s["fin_h"], 1)

        def act_final_square(act, w):
            act.wait_ge(s["fin_h"], w + 1)
            if w >= 2:
                act.wait_ge(s["fin_var"], w - 1)
            nc.scalar.activation(fin_sq[:, w % 2, :], fin_h_ps[w % 3], ACT.Square,
                                 bias=cbf[:, :]).then_inc(s["fin_sq_s"], 1)

        def pe_final_var(pe, w):
            pe.wait_ge(s["fin_sq_s"], w + 1)
            if w >= 2:
                pe.wait_ge(s["fin_ln_s"], w - 1)
            nc.tensor.matmul(fin_var_ps[w % 2][:, :], mean_f32[:, :], fin_sq[:, w % 2, :],
                             start=True, stop=True).then_inc(s["fin_var"], 1)

        def act_final_rstd(act, w):
            act.wait_ge(s["fin_var"], w + 1)
            if w >= 1:
                act.wait_ge(s["fin_rstd_s"], w)
            nc.scalar.activation(fin_ln[:, :], fin_var_ps[w % 2][:, :], ACT.Ln, bias=eps_col[:, :]).then_inc(s["fin_ln_s"], 1)
            act.wait_ge(s["fin_ln_s"], w + 1)
            if w >= 2:
                act.wait_ge(s["fin_z"], w - 1)
            nc.scalar.activation(fin_rstd[:, w % 2, :], fin_ln[:, :], ACT.Exp, scale=-0.5).then_inc(s["fin_rstd_s"], 1)

        def dve_final_z(dve, w):
            dve.wait_ge(s["fin_rstd_s"], w + 1)
            if w >= 2:
                dve.wait_ge(s["fin_out_ps"], w - 1)
            nc.vector.scalar_tensor_tensor(fin_zb[:, w % 2, :], fin_h_ps[w % 3], cbf[:, :], fin_rstd[:, w % 2, :],
                                           ALU.add, ALU.mult).then_inc(s["fin_z"], 1)
            dve.wait_ge(s["fin_z"], w + 1)
            nc.vector.tensor_scalar(fin_zb[:, w % 2, :], fin_zb[:, w % 2, :], ffn_cols[:, C_GF:C_GF + 1],
                                    ffn_cols[:, C_BEF:C_BEF + 1], ALU.mult, ALU.add).then_inc(s["fin_y"], 1)

        def pe_final_transpose(pe, w):
            pe.wait_ge(s["fin_y"], w + 1)
            if w >= 2:
                pe.wait_ge(s["fin_gated"], w - 1)
            for t in range(TT):
                last = nc.tensor.transpose(fin_out_ps[w % 2][:, t * P:(t + 1) * P],
                                           fin_zb[:, w % 2, t * P:(t + 1) * P], ident[:, :])
            last.then_inc(s["fin_out_ps"], 1)

        def dve_final_gate(dve, w):
            dve.wait_ge(s["fin_out_ps"], w + 1)
            nc.vector.tensor_tensor(gate_tm[:, w], fin_out_ps[w % 2][:, :].rearrange("p (t d) -> p t d", d=D), gate_tm[:, w],
                                    ALU.mult).then_inc(s["fin_gated"], 1)

        def pool_final_residual(pool, w):
            pool.wait_ge(s["fin_gated"], w + 1)
            nc.gpsimd.tensor_tensor(gate_tm[:, w], gate_tm[:, w], x_tm[:, w], ALU.add).then_inc(s["y_ready"], 1)

        def three_pass(dst, w_hi, w_lo, a_hi, a_lo, start, stop):
            nc.tensor.matmul(dst, w_hi, a_hi, start=start, stop=False)
            nc.tensor.matmul(dst, w_lo, a_hi, start=False, stop=False)
            return nc.tensor.matmul(dst, w_hi, a_lo, start=False, stop=stop)

        def is_unit(u):
            return not isinstance(u, int) or 0 <= u < UNITS

        def after_first(u):
            return not isinstance(u, int) or u > 0

        def p_is_not(p, n):
            return not isinstance(p, int) or p != n

        def dve_has_hid_lo(u):
            return isinstance(u, int) and u >= UNITS - 2

        def is_layer(l):
            return not isinstance(l, int) or l < L

        def pe_kv(pe, u, b, half):
            if half == 0:
                if isinstance(u, int) and u < SEQS:
                    pe.wait_ge(s["x_state"], u + 1)
                else:
                    pe.wait_ge(s["state"], u - SEQS + 1)
                if after_first(u):
                    pe.wait_ge(s["kv_biased"], u * 2)
            for t in (2 * half, 2 * half + 1):
                a_hi, a_lo = z_hi[:, b, t * P:(t + 1) * P], z_lo[:, b, t * P:(t + 1) * P]
                dst = kv_ps[half][:, t % 2, :]
                nc.tensor.matmul(dst, a_hi, wqkv_hi[:, D:3 * D], start=True, stop=False)
                nc.tensor.matmul(dst, a_hi, wqkv_lo[:, D:3 * D], start=False, stop=False)
                last = nc.tensor.matmul(dst, a_lo, wqkv_hi[:, D:3 * D], start=False, stop=True)
            last.then_inc(s["kvproj"], 1)

        def pe_q(pe, u, b):
            if after_first(u):
                pe.wait_ge(s["qphi"], u)
            three_pass(q_ps[:, :], wqkv_hi[:, 0:D], wqkv_lo[:, 0:D], z_hi[:, b, :], z_lo[:, b, :],
                       True, True).then_inc(s["qproj"], 1)

        def pe_kv_ksum(pe, u, half):
            if half == 0:
                pe.wait_ge(s["kphi"], u + 1)
                if after_first(u):
                    pe.wait_ge(s["kvo_sb"], u)
            for t in (2 * half, 2 * half + 1):
                last = nc.tensor.matmul(KV_KSUM, k_phi[:, t, :], kv1[:, t, D:2 * D + 1], start=(t == 0), stop=(t == TT - 1))
            if half == 1:
                last.then_inc(s["kv_ps"], 1)

        def pe_kv_transpose(pe, u):
            pe.wait_ge(s["kvblk"], u + 1)
            nc.tensor.transpose(KVT, kv_blk[:, :], ident[:, :]).then_inc(s["kvt_ps"], 1)

        def pe_kvo_den(pe, u):
            pe.wait_ge(s["kvt_sb"], u + 1)
            nc.tensor.matmul(KVO, kvT_blk[:, :], wo_c[:, :], start=True, stop=True).then_inc(s["kvo_ps"], 1)
            pe.wait_ge(s["ksum_lo_s"], u + 1)
            pe.wait_ge(s["qphi_lo_s"], u + 1)
            if is_unit(u - 1):
                pe.wait_ge(s["lnv1_s"], u)
            three_pass(up_ps[1][:, :], ksum_hi[:, :], ksum_lo[:, :], q_phi_hi[:, :], q_phi_lo[:, :],
                       True, True).then_inc(s["den_ps"], 1)

        def pe_att(pe, u, b):
            if isinstance(u, int) and u == 0:
                pe.wait_ge(s["ffn_cols_ready"], 1)
            if isinstance(u, int) and u + 3 in LATE_XN:
                pe.wait_ge(s["x_state"], u + 4)
            if after_first(u):
                pe.wait_ge(s["z1_s"], u)
            three_pass(att_ps[:, :], cg2_hi[:, :], cg2_lo[:, :], z_hi[:, b, :], z_lo[:, b, :], True, False)
            pe.wait_ge(s["kvo_sb"], u + 1)
            pe.wait_ge(s["qn"], u + 1)
            nc.tensor.matmul(att_ps[:, :], kvo[:, :], q_n[:, :], start=False, stop=True).then_inc(s["att_done"], 1)

        def pe_var2(pe, u):
            if is_unit(u + 1):
                pe.wait_ge(s["gelu"], (u + 2) * FC - 1)
            pe.wait_ge(s["sq2lo_s"], u + 1)
            nc.tensor.matmul(up_ps[0][:, :], mean_mat[:, :], sq2_hi[:, :], start=True, stop=False)
            nc.tensor.matmul(up_ps[0][:, :], mean_mat[:, :], sq2_lo[:, :], start=False, stop=True).then_inc(s["var2"], 1)

        def pe_var1(pe, u):
            if is_unit(u - 1):
                pe.wait_ge(s["gelu"], u * FC)
            pe.wait_ge(s["sq1lo_s"], u + 1)
            nc.tensor.matmul(up_ps[1][:, :], mean_mat[:, :], sq1_hi[:, :], start=True, stop=False)
            nc.tensor.matmul(up_ps[1][:, :], mean_mat[:, :], sq1_lo[:, :], start=False, stop=True).then_inc(s["var1"], 1)

        def pe_up(pe, u, b, chunks):
            if chunks[0] == 0:
                pe.wait_ge(s["z1lo_s"], u + 1)
                if is_unit(u + 1):
                    pe.wait_ge(s["den_sb"], u + 2)
                else:
                    pe.wait_ge(s["lnv1_s"], u + 1)
                if is_unit(u - 2):
                    pe.wait_ge(s["lnv2_s"], u - 1)
            for j in chunks:
                if j >= 2:
                    pe.wait_ge(s["gelu"], u * FC + j - 1)
                three_pass(up_ps[j % 2][:, :], w1_hi[:, j * P:(j + 1) * P], w1_lo[:, j * P:(j + 1) * P],
                           z1_hi[:, b % 2, :], z1_lo[:, b % 2, :], True, True).then_inc(s["up"], 1)

        def pe_down(pe, u, b):
            if after_first(u):
                pe.wait_ge(s["hc2_s"], u)
            three_pass(down_ps[:, :], cg1_hi[:, :], cg1_lo[:, :], z1_hi[:, b % 2, :], z1_lo[:, b % 2, :], True, False)
            for j in range(FC):
                pe.wait_ge(s["hid_lo_s"], u * FC + j + 1)
                last = three_pass(down_ps[:, :], w2_hi[:, j, :], w2_lo[:, j, :], hid_hi[:, j, :], hid_lo[:, j, :],
                                  False, j == FC - 1)
            last.then_inc(s["down"], 1)

        def pe_period(pe, l, b, between=None):
            p = l * SEQS + b
            att, ffn, ln1, ln2, proj = is_unit(p), is_unit(p - 2), is_unit(p - 1), is_unit(p - 3), is_unit(p + 1)
            if ffn:
                if b == 2:
                    pe.wait_ge(s["w1_split"], l * 2 + 2)
                pe_up(pe, p - 2, b, (0, 1))
            if att:
                if b == SEQS - 1 and is_layer(l + 1):
                    pe.wait_ge(s["attb_ready"], l * 5 + 10)
                pe_kv_ksum(pe, p, 0)
            if ffn:
                pe_up(pe, p - 2, b, (2, 3))
            if att:
                pe_kv_ksum(pe, p, 1)
            if proj:
                if b == SEQS - 1:
                    pe.wait_ge(s["wqkv_split"], l * 2 + 4)
                pe_kv(pe, p + 1, (b + 1) % SEQS, 0)
            if att:
                pe_kv_transpose(pe, p)
            if ln2:
                pe_var2(pe, p - 3)
            if ln1:
                pe_var1(pe, p - 1)
            if proj:
                pe_kv(pe, p + 1, (b + 1) % SEQS, 1)
                pe_q(pe, p + 1, (b + 1) % SEQS)
            if att:
                if b == 0:
                    pe.wait_ge(s["wo_ready"], l + 1)
                pe_kvo_den(pe, p)
            if between:
                between()
            if ffn:
                if b == 2:
                    pe.wait_ge(s["ffnw_split"], l * 4 + 4)
                pe_down(pe, p - 2, b)
            if att:
                if b == 0:
                    pe.wait_ge(s["cg2_split"], l * 2 + 2)
                pe_att(pe, p, b)
            if b == SEQS - 2 and is_layer(l + 1):
                pe_fold_biases(pe, l + 1, True)

        def act_gelu(act, u, chunks):
            for j in chunks:
                act.wait_ge(s["up"], u * FC + j + 1)
                if after_first(u):
                    act.wait_ge(s["hid_lo_s"], (u - 1) * FC + j + 1)
                nc.scalar.activation(hid[:, j, :], up_ps[j % 2][:, :], ACT.Gelu,
                                     bias=c1_f[:, j:j + 1]).then_inc(s["gelu"], 1)

        def act_ln_var2(act, v):
            act.wait_ge(s["var2"], v + 1)
            nc.scalar.activation(lnv2[:, :], up_ps[0][:, :], ACT.Ln, bias=eps_col[:, :]).then_inc(s["lnv2_s"], 1)

        def act_rstd2(act, v):
            act.wait_ge(s["lnv2_s"], v + 1)
            if after_first(v):
                act.wait_ge(s["z2_s"], v)
            nc.scalar.activation(rstd2[:, :], lnv2[:, :], ACT.Exp, scale=-0.5).then_inc(s["rstd2_s"], 1)

        def act_hc2(act, u):
            act.wait_ge(s["down"], u + 1)
            if after_first(u):
                act.wait_ge(s["z2_s"], u)
            nc.scalar.activation(hc2[:, :], down_ps[:, :], ACT.Identity, bias=cb2[:, :]).then_inc(s["hc2_s"], 1)

        def act_period(act, l, b, between=None):
            p = l * SEQS + b
            att, ffn, ln1, ln2, proj = is_unit(p), is_unit(p - 2), is_unit(p - 1), is_unit(p - 3), is_unit(p + 1)
            u, v = p - 2, p - 3
            if ffn:
                if b == 2:
                    act.wait_ge(s["c1_ready"], l + 1)
                act_gelu(act, u, range(FC))
                nc.scalar.preload_act_table_set("natural_log_exp_and_others")
            if ln2:
                act_ln_var2(act, v)
            if ln1:
                act.wait_ge(s["var1"], p)
                nc.scalar.activation(lnv1[:, :], up_ps[1][:, :], ACT.Ln, bias=eps_col[:, :]).then_inc(s["lnv1_s"], 1)
            if ln2:
                act_rstd2(act, v)
            if ln1:
                act.wait_ge(s["lnv1_s"], p)
                if after_first(p - 1):
                    act.wait_ge(s["z1_s"], p - 1)
                nc.scalar.activation(rstd1[:, :], lnv1[:, :], ACT.Exp, scale=-0.5).then_inc(s["rstd1_s"], 1)
            if att:
                act.wait_ge(s["den_ps"], p + 1)
                nc.scalar.activation(den[:, :], up_ps[1][:, :], ACT.Ln, bias=den_eps_col[:, :]).then_inc(s["den_sb"], 1)
                act.wait_ge(s["den_sb"], p + 1)
                if after_first(p):
                    act.wait_ge(s["qn"], p)
                nc.scalar.activation(rden[:, :], den[:, :], ACT.Exp, scale=-1.0).then_inc(s["rden_s"], 1)
            if proj:
                act.wait_ge(s["kmin"], p + 2)
                if after_first(p + 1):
                    act.wait_ge(s["kphi"], p + 1)
                nc.scalar.activation(k_exp[:, :, :], k_min[:, :, :], ACT.Exp, bias=neg1_col[:, :]).then_inc(s["kexp"], 1)
                act.wait_ge(s["qmin"], p + 2)
                if after_first(p + 1):
                    act.wait_ge(s["qphi"], p + 1)
                nc.scalar.activation(q_exp[:, :], q_min[:, :], ACT.Exp).then_inc(s["qexp"], 1)
            if att and is_unit(p - 1) and p_is_not(p, 1):
                nc.scalar.preload_act_table_set("gelu_and_others")
            if between:
                between()
            if ffn:
                if b == 2:
                    act.wait_ge(s["cb2_ready"], l + 1)
                act_hc2(act, u)
            if att:
                act.wait_ge(s["att_done"], p + 1)
                if b == 0:
                    act.wait_ge(s["cb1_ready"], l + 1)
                if after_first(p):
                    act.wait_ge(s["sq1lo_s"], p)
                nc.scalar.activation(sq1[:, :], att_ps[:, :], ACT.Square, bias=cb1[:, :]).then_inc(s["sq1_s"], 1)

        def dve_kv_bias(dve, u):
            if after_first(u):
                dve.wait_ge(s["kv_ps"], u)
            for i in range(2):
                dve.wait_ge(s["kvproj"], u * 2 + i + 1)
                nc.vector.tensor_tensor(kv1[:, 2 * i:2 * i + 2, 0:2 * D], kv_ps[i][:, :, :],
                                        bkv1_bc[:, :].unsqueeze(1).to_broadcast([P, 2, 2 * D]),
                                        ALU.add).then_inc(s["kv_biased"], 1)

        def dve_k_min(dve, u):
            if after_first(u):
                dve.wait_ge(s["kexp"], u)
            dve.wait_ge(s["kv_biased"], u * 2 + 2)
            nc.vector.tensor_scalar(k_min[:, :, :], kv1[:, :, 0:D], 1.0, None, ALU.min).then_inc(s["kmin"], 1)

        def dve_q_min(dve, u):
            dve.wait_ge(s["qproj"], u + 1)
            if after_first(u):
                dve.wait_ge(s["qexp"], u)
            nc.vector.tensor_scalar(q_min[:, :], q_ps[:, :], bq_f[:, 0:1], 0.0, ALU.add, ALU.min).then_inc(s["qmin"], 1)

        def dve_k_phi(dve, u, between=None):
            dve.wait_ge(s["kexp"], u + 1)
            nc.vector.tensor_scalar(k_exp[:, :, :], k_exp[:, :, :], -1.0, 1.0, ALU.add, ALU.add).then_inc(s["kexpm1"], 1)
            if between:
                between()
            dve.wait_ge(s["kexpm1"], u + 1)
            nc.vector.tensor_tensor(k_phi[:, :, :], k_exp[:, :, :], kv1[:, :, 0:D], ALU.max).then_inc(s["kphi"], 1)

        def dve_q_phi(dve, u):
            dve.wait_ge(s["qexp"], u + 1)
            nc.vector.tensor_scalar(q_exp[:, :], q_exp[:, :], -1.0, 1.0, ALU.add, ALU.add).then_inc(s["qexpm1"], 1)
            dve.wait_ge(s["qexpm1"], u + 1)
            if after_first(u):
                dve.wait_ge(s["qn"], u)
            nc.vector.scalar_tensor_tensor(q_phi[:, :], q_ps[:, :], bq_f[:, 1:2], q_exp[:, :],
                                           ALU.add, ALU.max).then_inc(s["qphi"], 1)

        def dve_q_phi_hi(dve, u):
            dve.wait_ge(s["qphi"], u + 1)
            if after_first(u):
                dve.wait_ge(s["den_ps"], u)
            nc.vector.tensor_copy(q_phi_hi[:, :], q_phi[:, :]).then_inc(s["qphi_hi_s"], 1)

        def dve_blocks(dve, u):
            dve.wait_ge(s["kv_ps"], u + 1)
            if after_first(u):
                dve.wait_ge(s["den_ps"], u)
            nc.vector.tensor_scalar(ksum_blk[:, :], head_mask[:, :], KV_KSUM[:, D:D + 1], None, ALU.mult).then_inc(s["ksumblk"], 1)
            nc.vector.tensor_tensor(kv_blk[:, :], KV_KSUM[:, 0:D], head_mask[:, :], ALU.mult).then_inc(s["kvblk"], 1)
            dve.wait_ge(s["ksumblk"], u + 1)
            nc.vector.tensor_copy(ksum_hi[:, :], ksum_blk[:, :]).then_inc(s["ksum_hi_s"], 1)

        def dve_hid_hi(dve, u, chunks):
            if after_first(u):
                dve.wait_ge(s["down"], u)
            for j in chunks:
                dve.wait_ge(s["gelu"], u * FC + j + 1)
                nc.vector.tensor_copy(hid_hi[:, j, :], hid[:, j, :]).then_inc(s["hid_hi_s"], 1)
                if dve_has_hid_lo(u):
                    dve.wait_ge(s["hid_hi_s"], u * FC + j + 1)
                    nc.vector.tensor_tensor(hid_lo[:, j, :], hid[:, j, :], hid_hi[:, j, :].bitcast(F32),
                                            ALU.subtract).then_inc(s["hid_lo_s"], 1)

        def dve_kvt(dve, u):
            dve.wait_ge(s["kvt_ps"], u + 1)
            if after_first(u):
                dve.wait_ge(s["kvo_ps"], u)
            nc.vector.tensor_copy(kvT_blk[:, :], KVT).then_inc(s["kvt_sb"], 1)
            dve.wait_ge(s["ksum_hi_s"], u + 1)
            nc.vector.tensor_tensor(ksum_lo[:, :], ksum_blk[:, :], ksum_hi[:, :].bitcast(F32),
                                    ALU.subtract).then_inc(s["ksum_lo_s"], 1)

        def dve_kvo(dve, u):
            dve.wait_ge(s["kvo_ps"], u + 1)
            if after_first(u):
                dve.wait_ge(s["att_done"], u)
            nc.vector.tensor_copy(kvo[:, :], KVO).then_inc(s["kvo_sb"], 1)

        def dve_sq2_hi(dve, v):
            dve.wait_ge(s["sq2_s"], v + 1)
            if after_first(v):
                dve.wait_ge(s["var2"], v)
            nc.vector.tensor_copy(sq2_hi[:, :], sq2[:, :]).then_inc(s["sq2hi_s"], 1)

        def dve_z2(dve, v):
            dve.wait_ge(s["rstd2_s"], v + 1)
            if after_first(v):
                dve.wait_ge(s["state"], v)
            nc.vector.tensor_tensor(z2[:, :], hc2[:, :], rstd2[:, :], ALU.mult).then_inc(s["z2_s"], 1)

        def dve_z2_hi(dve, v, b):
            dve.wait_ge(s["z2_s"], v + 1)
            nc.vector.tensor_copy(z_hi[:, b, :], z2[:, :]).then_inc(s["z2hi_s"], 1)

        def dve_period(dve, l, b, early=None, between=None):
            p = l * SEQS + b
            att, ffn, ln1, ln2, proj = is_unit(p), is_unit(p - 2), is_unit(p - 1), is_unit(p - 3), is_unit(p + 1)
            u, v = p - 2, p - 3
            fold = is_layer(l + 1)
            folded = not isinstance(l, int) or 0 < l < L
            if att:
                dve_q_phi_hi(dve, p)
            if ln2:
                dve_sq2_hi(dve, v)
            if ln1:
                dve.wait_ge(s["sq1_s"], p)
                if after_first(p - 1):
                    dve.wait_ge(s["var1"], p - 1)
                nc.vector.tensor_copy(sq1_hi[:, :], sq1[:, :]).then_inc(s["sq1hi_s"], 1)
                dve.wait_ge(s["sq1hi_s"], p)
                nc.vector.tensor_tensor(sq1_lo[:, :], sq1[:, :], sq1_hi[:, :].bitcast(F32),
                                        ALU.subtract).then_inc(s["sq1lo_s"], 1)
            if early:
                early()
            if b == 2 and folded:
                dve_split_ffn(dve, l, True)
            if ffn:
                dve_hid_hi(dve, u, (0, 1))
            if att:
                dve_blocks(dve, p)
            if ffn:
                dve_hid_hi(dve, u, (2,))
            if att:
                dve_kvt(dve, p)
            if ffn:
                dve_hid_hi(dve, u, (3,))
            if b == 1 and folded:
                dve_w1_hi(dve, l, True)
            if proj:
                dve_kv_bias(dve, p + 1)
            if ln2:
                dve_z2(dve, v)
            if proj:
                dve_k_min(dve, p + 1)
            if ln1:
                dve.wait_ge(s["rstd1_s"], p)
                if after_first(p - 1):
                    dve.wait_ge(s["z1lo_s"], p - 1)
                nc.vector.scalar_tensor_tensor(z1[:, :], att_ps[:, :], cb1[:, :], rstd1[:, :],
                                               ALU.add, ALU.mult).then_inc(s["z1_s"], 1)
            if ln2:
                dve_z2_hi(dve, v, (b - 3) % SEQS)
            if proj:
                dve_q_min(dve, p + 1)
            if ln1:
                dve.wait_ge(s["z1_s"], p)
                if is_unit(p - 3):
                    dve.wait_ge(s["down"], p - 2)
                nc.vector.tensor_copy(z1_hi[:, (b - 1) % 2, :], z1[:, :]).then_inc(s["z1hi_s"], 1)
            if b == 0 and folded:
                dve_split_cg2(dve, l, True)
            if att and b == 0 and folded:
                nc.vector.tensor_copy(cb1[:, :], colb[:, 0:1]).then_inc(s["cb1_ready"], 1)
            if b == 2 and folded:
                dve_fold_cb2(dve, l, True)
            if between:
                between()
            if att:
                dve.wait_ge(s["rden_s"], p + 1)
                if after_first(p):
                    dve.wait_ge(s["att_done"], p)
                nc.vector.tensor_tensor(q_n[:, :], q_phi[:, :], rden[:, :], ALU.mult).then_inc(s["qn"], 1)
            if proj:
                dve_k_phi(dve, p + 1, (lambda: dve_kvo(dve, p)) if att else None)
                dve_q_phi(dve, p + 1)
            elif att:
                dve_kvo(dve, p)
            if b == 1 and folded:
                dve_fold_c1(dve, l, True)
            if b == 3 and fold:
                dve_fold_att_vectors(dve, l + 1, True)
            if b == 4 and fold:
                dve_fold_ffn_vectors(dve, l + 1, True)
            if b == 5 and fold:
                dve_fold_wqkv(dve, l + 1, True)
                dve_fold_w1(dve, l + 1, True)
            if b == SEQS - 2 and fold:
                dve_split_wqkv(dve, l + 1, True)
            if b == SEQS - 1 and fold and att:
                dve_fold_wo(dve, l + 1, True)
                dve_fold_cg2(dve, l + 1, True)
                dve_fold_w2(dve, l + 1, True)
            if b == SEQS - 2 and fold:
                dve_fold_att_biases(dve, l + 1, True)

        def pool_sq2_lo(pool, v):
            pool.wait_ge(s["sq2hi_s"], v + 1)
            if after_first(v):
                pool.wait_ge(s["var2"], v)
            nc.gpsimd.tensor_tensor(sq2_lo[:, :], sq2[:, :], sq2_hi[:, :].bitcast(F32),
                                    ALU.subtract).then_inc(s["sq2lo_s"], 1)

        def pool_hid_lo(pool, u):
            if after_first(u):
                pool.wait_ge(s["down"], u)
            for j in range(FC):
                pool.wait_ge(s["hid_hi_s"], u * FC + j + 1)
                nc.gpsimd.tensor_tensor(hid_lo[:, j, :], hid[:, j, :], hid_hi[:, j, :].bitcast(F32),
                                        ALU.subtract).then_inc(s["hid_lo_s"], 1)

        def pool_z2_lo(pool, v, b):
            pool.wait_ge(s["z2hi_s"], v + 1)
            nc.gpsimd.tensor_tensor(z_lo[:, b, :], z2[:, :], z_hi[:, b, :].bitcast(F32),
                                    ALU.subtract).then_inc(s["state"], 1)

        def pool_sq2(pool, u):
            pool.wait_ge(s["hc2_s"], u + 1)
            if after_first(u):
                pool.wait_ge(s["sq2lo_s"], u)
            nc.gpsimd.tensor_tensor(sq2[:, :], hc2[:, :], hc2[:, :], ALU.mult).then_inc(s["sq2_s"], 1)

        def pool_period(pool, l, b):
            p = l * SEQS + b
            ffn, ln1, ln2 = is_unit(p - 2), is_unit(p - 1), is_unit(p - 3)
            u, v = p - 2, p - 3
            if is_unit(p):
                pool.wait_ge(s["qphi_hi_s"], p + 1)
                if after_first(p):
                    pool.wait_ge(s["den_ps"], p)
                nc.gpsimd.tensor_tensor(q_phi_lo[:, :], q_phi[:, :], q_phi_hi[:, :].bitcast(F32),
                                        ALU.subtract).then_inc(s["qphi_lo_s"], 1)
            if ln2:
                pool_sq2_lo(pool, v)
            folded = not isinstance(l, int) or 0 < l < L
            if b == 2 and folded:
                pool_w2_lo(pool, l)
            if ffn and not dve_has_hid_lo(u):
                pool_hid_lo(pool, u)
            if b == 1 and folded:
                pool_w1_lo(pool, l)
            if ln1:
                pool.wait_ge(s["z1hi_s"], p)
                nc.gpsimd.tensor_tensor(z1_lo[:, (b - 1) % 2, :], z1[:, :], z1_hi[:, (b - 1) % 2, :].bitcast(F32),
                                        ALU.subtract).then_inc(s["z1lo_s"], 1)
            if ln2:
                pool_z2_lo(pool, v, (b - 3) % SEQS)
            if ffn:
                pool_sq2(pool, u)

        with nc.Block() as block:
            @block.sync
            def _(sp):
                def load_x(i):
                    sp.dma_start(x_tm[:, 2 * i:2 * i + 2, :, :], x_dram[:, 2 * i:2 * i + 2]).then_inc(x_in[i], 16)
                load_x(0)
                for i, v in enumerate((bq, bo, g1, be1, g2, be2, c2)):
                    sp.dma_start(vec_rows[i * L:(i + 1) * L, :], v).then_inc(s["vec_in"], 16)
                sp.dma_start(vec_rows[R_C1:R_C1 + FC * L, :],
                             c1.rearrange("l (j p) -> (l j) p", p=P)).then_inc(s["vec_in"], 16)
                load_layer(sp, 0)
                for i in range(1, 4):
                    load_x(i)
                for i, v in enumerate((ln_g, ln_b, bn_g, bn_b, bn_mean, bn_var, gf, bef)):
                    sp.dma_start(ffn_rows[i:i + 1, :], v.rearrange("(a n) -> a n", a=1)).then_inc(s["ffn_vec_in"], 16)
                sp.dma_start(wr_sb[:, :], Wr).then_inc(s["row_in"], 16)
                sp.dma_start(br_bc[:, :], br.rearrange("(a n) -> a n", a=1).to_broadcast([SEQS, E])).then_inc(s["row_in"], 16)

                sp.wait_ge(s["wqkv_split"], 2)
                sp.wait_ge(s["wo_ready"], 1)
                sp.wait_ge(s["ffn_fold"], FFN_STEPS)
                sp.wait_ge(s["attb_ps"], 1)
                sp.wait_ge(s["ffnb_ps"], 1)
                load_layer(sp, 1)

                sp.wait_ge(s["routed"], 1)
                for b in range(SEQS):
                    e = sp.value_load(expert_i[b:b + 1, 0:1], min_val=0, max_val=E - 1)
                    sp.dma_start(ew_down[:, b, :], W_down[bass.ds(e, 1)].rearrange("a d h -> d (a h)")).then_inc(s["expert_in"], 16)
                    sp.dma_start(eb_down[:, b:b + 1], b_down[bass.ds(e, 1)].rearrange("a h -> h a")).then_inc(s["expert_in"], 16)
                    sp.dma_start(ew_up[0:HID, b, :], W_up[bass.ds(e, 1)].rearrange("a h d -> h (a d)")).then_inc(s["expert_in"], 16)
                    sp.dma_start(ew_up[HID:HID + 1, b, :], b_up[bass.ds(e, 1)]).then_inc(s["expert_in"], 16)

                with sp.Fori(2, L) as l:
                    splits, steps = l * 2, l * FFN_STEPS
                    sp.wait_ge(s["wqkv_split"], splits)
                    sp.wait_ge(s["wo_ready"], l)
                    sp.sem_inc(s["sp_waited"], 1)
                    sp.wait_ge(s["ffn_fold"], steps)
                    sp.wait_ge(s["attb_ps"], l)
                    sp.sem_inc(s["sp_waited"], 1)
                    sp.wait_ge(s["ffnb_ps"], l)
                    sp.sem_inc(s["sp_waited"], 1)
                    load_layer(sp, l)

                for w in range(SEQS):
                    sp.wait_ge(s["y_ready"], w + 1)
                    sp.dma_start(out_dram[:, w], gate_tm[:, w]).then_inc(s["out_sent"], 16)
                sp.wait_ge(s["out_sent"], 16 * SEQS)

            @block.gpsimd
            def _(pool):
                c = s["const_ready"]
                nc.gpsimd.memset(ident[:, :], 0.0).then_inc(c, 1)
                nc.gpsimd.memset(ones[:, :], 1.0).then_inc(c, 1)
                nc.gpsimd.memset(mean_f32[:, :], 1.0 / D).then_inc(c, 1)
                nc.gpsimd.memset(eps_col[:, :], EPS).then_inc(c, 1)
                nc.gpsimd.memset(neg1_col[:, :], -1.0).then_inc(c, 1)
                nc.gpsimd.memset(den_eps_col[:, :], DEN_EPS).then_inc(c, 1)
                nc.gpsimd.iota(expert_m8[:, :], pattern=[[1, E]], base=-E, channel_multiplier=0,
                               allow_small_or_imprecise_dtypes=True).then_inc(c, 1)
                pool.wait_ge(c, 7)
                nc.gpsimd.affine_select(out=ident[:, :], in_=ident[:, :], pattern=[[-1, P]], compare_op=ALU.not_equal,
                                        fill=1.0, base=0, channel_multiplier=1).then_inc(c, 1)
                nc.gpsimd.affine_select(out=head_mask[:, :], in_=ones[:, :], pattern=[[-DH, D // DH], [0, DH]],
                                        compare_op=ALU.is_ge, fill=0.0, base=0, channel_multiplier=1).then_inc(c, 1)
                pool.wait_ge(c, 9)
                nc.gpsimd.affine_select(out=head_mask[:, :], in_=head_mask[:, :], pattern=[[DH, D // DH], [0, DH]],
                                        compare_op=ALU.is_ge, fill=0.0, base=DH - 1, channel_multiplier=-1).then_inc(c, 1)
                nc.gpsimd.tensor_tensor(centre[:, :], ident[:, :], mean_f32[:, :], ALU.subtract).then_inc(c, 1)
                nc.gpsimd.memset(kv1[:, :, 2 * D:2 * D + 1], 1.0).then_inc(c, 1)
                nc.gpsimd.tensor_copy(mean_mat[:, :], mean_f32[:, :]).then_inc(c, 1)
                pool.wait_ge(c, 13)
                nc.gpsimd.memset(e_hid[HID:HID + 1, :, :], 1.0).then_inc(c, 1)

                pool_period(pool, 0, 0)
                pool_period(pool, 0, 1)
                pool_w1_lo(pool, 0)
                pool_w2_lo(pool, 0)
                for b in range(2, SEQS):
                    pool_period(pool, 0, b)
                with pool.Fori(1, L - 1) as l:
                    for b in range(SEQS):
                        pool_period(pool, l, b)
                for b in range(SEQS + 1):
                    pool_period(pool, L - 1 + b // SEQS, b % SEQS)
                pool_sq2_lo(pool, UNITS - 2)
                pool_z2_lo(pool, UNITS - 2, SEQS - 2)
                pool_sq2(pool, UNITS - 1)
                pool_sq2_lo(pool, UNITS - 1)
                pool_z2_lo(pool, UNITS - 1, SEQS - 1)
                for w in range(SEQS):
                    pool_final_residual(pool, w)

            @block.tensor
            def _(pe):
                pe_cols(pe)
                pe_xn_transpose(pe, 0)
                pe_fold_biases(pe, 0, False)
                pe_ffn_cols(pe)
                pe_period(pe, -1, SEQS - 1)
                pe_xn_transpose(pe, 1)
                pe_zf_transpose(pe, 0)
                pe_period(pe, 0, 0, lambda: pe_zf_transpose(pe, 1))
                pe_xn_transpose(pe, 2)
                pe_zf_transpose(pe, 2)
                pe_xn_transpose(pe, 3)
                pe_zf_transpose(pe, 3)

                def late_transposes():
                    pe_xn_transpose(pe, 4)
                    pe_zf_transpose(pe, 4)
                pe_period(pe, 0, 1, late_transposes)
                for b in range(5, SEQS):
                    pe_zf_transpose(pe, b)
                pe_logits(pe)
                pe_gate_bc(pe)
                for b in range(2, 5):
                    pe_period(pe, 0, b, lambda: pe_xn_transpose(pe, b + 3))
                for b in range(5, SEQS):
                    pe_period(pe, 0, b)
                with pe.Fori(1, L - 1) as l:
                    for b in range(SEQS):
                        pe_period(pe, l, b)
                for b in range(SEQS):
                    pe_period(pe, L - 1, b)
                last = UNITS - 1

                def first_expert():
                    pe_final_bias(pe)
                    pe_expert_down(pe, 0)
                pe_period(pe, L, 0, first_expert)
                pe_expert_down(pe, 1)
                pe_expert_up(pe, 0)
                pe_up(pe, last, 1, range(FC))
                pe_expert_down(pe, 2)
                pe_var2(pe, last - 1)
                pe_expert_up(pe, 1)
                pe_expert_down(pe, 3)
                pe_down(pe, last, 1)
                for b in range(2, SEQS):
                    pe_expert_up(pe, b)
                    if b + 2 < SEQS:
                        pe_expert_down(pe, b + 2)
                pe_var2(pe, last)
                for k in range(SEQS + 3):
                    if k < SEQS:
                        pe_final_centre(pe, k)
                    if 0 <= k - 1 < SEQS:
                        pe_final_var(pe, k - 1)
                    if k >= 3:
                        pe_final_transpose(pe, k - 3)

            @block.scalar
            def _(act):
                nc.scalar.preload_act_table_set("natural_log_exp_and_others")
                act.wait_ge(s["const_ready"], CONSTS)
                act_rstd_x(act, 0)
                act_xn_hi(act, 0)
                act_rstd_x(act, 1)
                act_period(act, -1, SEQS - 1)
                act_xn_hi(act, 1)
                act_zf_fm(act, 0)
                act_bn_rstd(act)
                act_period(act, 0, 0, lambda: act_zf_fm(act, 1))
                act_rstd_x(act, 2)
                act_xn_hi(act, 2)
                act_zf_fm(act, 2)
                act_xn_hi(act, 3)
                act_zf_fm(act, 3)

                def late_copies():
                    act_xn_hi(act, 4)
                    act_zf_fm(act, 4)
                    act_rstd_x(act, 3)
                act_period(act, 0, 1, late_copies)
                for b in range(5, SEQS):
                    act_zf_fm(act, b)
                act_softmax(act)
                nc.scalar.preload_act_table_set("gelu_and_others")
                for b in range(2, 5):
                    act_period(act, 0, b, lambda: act_xn_hi(act, b + 3))
                for b in range(5, SEQS):
                    act_period(act, 0, b)
                with act.Fori(1, L - 1) as l:
                    for b in range(SEQS):
                        act_period(act, l, b)
                for b in range(SEQS):
                    act_period(act, L - 1, b)
                act_period(act, L, 0)
                last = UNITS - 1
                nc.scalar.preload_act_table_set("gelu_and_others")
                act_gelu(act, last, range(FC))
                nc.scalar.preload_act_table_set("natural_log_exp_and_others")
                act_ln_var2(act, last - 1)
                act_rstd2(act, last - 1)
                act_expert_silu(act, 0)
                act_expert_silu(act, 1)
                act_hc2(act, last)
                for b in range(2, SEQS):
                    act_expert_silu(act, b)
                nc.scalar.preload_act_table_set("natural_log_exp_and_others")
                act_ln_var2(act, last)
                act_rstd2(act, last)
                for k in range(SEQS + 1):
                    if k < SEQS:
                        act_final_square(act, k)
                    if k >= 1:
                        act_final_rstd(act, k - 1)

            @block.vector
            def _(dve):
                dve_stats(dve, 0)
                dve_stats_of_xn(dve, 0)
                dve_xn(dve, 0)
                dve_r_f(dve, 0)
                dve_cols(dve)
                dve_xn(dve, 1)
                dve_zf(dve, 0)
                dve.wait_ge(s["const_ready"], CONSTS)
                dve_fold_att_vectors(dve, 0, False)
                dve_fold_ffn_vectors(dve, 0, False)
                dve_fold_wqkv(dve, 0, False)
                dve_split_wqkv(dve, 0, False)
                dve_xn_lo(dve, 0)
                dve_stats(dve, 1)
                dve_stats_of_xn(dve, 1)
                dve_fold_att_biases(dve, 0, False)
                dve_r_f(dve, 1)
                dve.wait_ge(s["ffn_cols_ps"], 1)
                nc.vector.tensor_copy(ffn_cols[:, :], att_ps[:, 0:8]).then_inc(s["ffn_cols_ready"], 1)
                dve.wait_ge(s["attb_ready"], 5)
                dve_period(dve, -1, SEQS - 1)
                dve_xn_lo(dve, 1)
                dve_fold_wo(dve, 0, False)
                dve_fold_cg2(dve, 0, False)
                dve_split_cg2(dve, 0, False)
                nc.vector.tensor_copy(cb1[:, :], colb[:, 0:1]).then_inc(s["cb1_ready"], 1)

                def stats_and_zf():
                    dve_zf(dve, 1)
                    dve_stats(dve, 2)
                dve_period(dve, 0, 0, None, stats_and_zf)
                dve_xn(dve, 2)
                dve_zf(dve, 2)
                dve_stats_of_xn(dve, 2)
                dve_xn_lo(dve, 2)
                dve_xn(dve, 3)
                dve_zf(dve, 3)
                dve_r_f(dve, 2)
                dve_xn_lo(dve, 3)

                def within_period_1():
                    dve_zf(dve, 4)
                    dve_stats(dve, 3)
                    dve_xn_lo(dve, 4)
                    dve_stats_of_xn(dve, 3)
                dve_period(dve, 0, 1, lambda: dve_xn(dve, 4), within_period_1)
                dve_zf(dve, 5)
                dve_r_f(dve, 3)
                dve_zf(dve, 6)
                dve_zf(dve, 7)
                dve_fold_w1(dve, 0, False)
                dve_fold_w2(dve, 0, False)
                dve_w1_hi(dve, 0, False)
                dve_split_ffn(dve, 0, False)
                dve_fold_c1(dve, 0, False)
                dve_fold_cb2(dve, 0, False)
                dve_batch_norm(dve)
                dve_route(dve)
                for b in range(2, 5):
                    dve_period(dve, 0, b, lambda: dve_xn(dve, b + 3))
                    dve_xn_lo(dve, b + 3)
                for b in range(5, SEQS):
                    dve_period(dve, 0, b)
                with dve.Fori(1, L - 1) as l:
                    for b in range(SEQS):
                        dve_period(dve, l, b)
                for b in range(SEQS):
                    dve_period(dve, L - 1, b)
                dve_period(dve, L, 0, lambda: dve_final_fold(dve))
                last = UNITS - 1
                dve_final_bias(dve)
                dve_expert_relu(dve, 0)
                dve_expert_relu(dve, 1)
                dve_sq2_hi(dve, last - 1)
                dve_hid_hi(dve, last, range(FC))
                dve_expert_relu(dve, 2)
                dve_expert_relu(dve, 3)
                dve_z2(dve, last - 1)
                dve_z2_hi(dve, last - 1, SEQS - 2)
                for b in range(4, SEQS - 1):
                    dve_expert_relu(dve, b)
                dve_sq2_hi(dve, last)
                dve_expert_relu(dve, SEQS - 1)
                dve_z2(dve, last)
                dve_z2_hi(dve, last, SEQS - 1)
                for k in range(2, SEQS + 3):
                    if 0 <= k - 2 < SEQS:
                        dve_final_z(dve, k - 2)
                    if k >= 3:
                        dve_final_gate(dve, k - 3)


NAMES = ("x", "Wq", "bq", "Wk", "bk", "Wv", "bv", "Wo", "bo", "g1", "be1", "g2", "be2", "W1", "c1", "W2", "c2",
         "gf", "bef")
FFN_NAMES = ("ln_g", "ln_b", "bn_g", "bn_b", "bn_mean", "bn_var", "Wr", "br", "W_down", "b_down", "W_up", "b_up")


def kernel(**inputs):
    import numpy as np
    import concourse.bacc as bacc
    from concourse.bass_utils import run_bass_kernel_spmd

    nc = bacc.Bacc("TRN2", target_bir_lowering=False, num_devices=1)
    arrays, args = {}, []
    for name in [f"L0_attn_{n}" for n in NAMES] + [f"L0_ffn_{n}" for n in FFN_NAMES]:
        a = np.ascontiguousarray(inputs[name])
        arrays[f"in_{name}"] = a
        args.append(nc.dram_tensor(f"in_{name}", a.shape, mybir.dt.from_np(a.dtype), kind="ExternalInput").ap())
    shape = inputs["L0_attn_x"].shape
    out = nc.dram_tensor("out_y", shape, mybir.dt.float32, kind="ExternalOutput").ap()
    build(nc, *args, out)
    r = run_bass_kernel_spmd(nc, [arrays], core_ids=[0])
    return r.results[0]["out_y"]
```
